# Optimizing a Trainium2 kernel written in Bass

```python
import numpy as np
import jax
import jax.numpy as jnp

def _softmax(x, axis=-1):
    return jax.nn.softmax(x, axis=axis)

def _gelu(x):
    return jax.nn.gelu(x, approximate=True)

def _silu(x):
    return jax.nn.silu(x)

def _sigmoid(x):
    return jax.nn.sigmoid(x)

def _layernorm(x, axis=-1, eps=1e-05):
    m = jnp.mean(x, axis=axis, keepdims=True)
    v = jnp.var(x, axis=axis, keepdims=True)
    return (x - m) / jnp.sqrt(v + eps)

def _scatter_add(tgt, idx, src, axis=0):
    return tgt.at[idx].add(src)

def _segment_sum(src, seg, n):
    return jax.ops.segment_sum(src, seg, n)
kernel_name = 'mk_early_fusion_d1_tok_img1024_r4_8d2848'

def setup_inputs(seed: int=0):
    np.random.seed(seed)
    _w = jnp.asarray

    def _rec_inputs():
        import jax
        import jax.numpy as jnp
        _rk = jax.random.key(seed)
        x = -0.00016672 + 0.999947 * jax.random.normal(jax.random.fold_in(_rk, 1), (16, 3, 96, 96), jnp.float32)
        txt = -0.000497171 + 0.57724 * jax.random.normal(jax.random.fold_in(_rk, 2), (16, 128, 256), jnp.float32)
        return (x, txt)
    x, txt = _rec_inputs()

    def _L0_tok_setup():
        import jax, jax.numpy as jnp
        import numpy as np
        IMG = 96
        PATCH = 16
        CH = 3
        EMBED = 256
        PATCH_DIM = CH * PATCH * PATCH

        def _patchify(x):
            B, C, H, Wd = x.shape
            hp, wp = (H // PATCH, Wd // PATCH)
            p = x.reshape(B, C, hp, PATCH, wp, PATCH)
            p = p.transpose(0, 2, 4, 1, 3, 5)
            return p.reshape(B, hp * wp, C * PATCH * PATCH)
        key = jax.random.key(seed)
        kx, kw, kb, kc = jax.random.split(key, 4)
        x = jax.random.normal(kx, (64, CH, IMG, IMG), dtype=jnp.float32)
        bound = 1.0 / np.sqrt(PATCH_DIM)
        W = jax.random.uniform(kw, (PATCH_DIM, EMBED), minval=-bound, maxval=bound, dtype=jnp.float32)
        b = jax.random.uniform(kb, (EMBED,), minval=-bound, maxval=bound, dtype=jnp.float32)
        cls_token = jnp.zeros((1, 1, EMBED), dtype=jnp.float32)
        return {'x': x, 'W': W, 'b': b, 'cls_token': cls_token}
    _L0_tok_all = _L0_tok_setup()
    _L0_tok_in = {k: v for k, v in _L0_tok_all.items() if k in ('W', 'b', 'cls_token')}
    del _L0_tok_all

    def _L0_attn_setup():
        import jax, jax.numpy as jnp
        import numpy as np
        D_MODEL = 256
        NUM_HEADS = 16
        HEAD_DIM = D_MODEL // NUM_HEADS
        ROPE_THETA = 10000.0

        def apply_rope(x):
            S, d_k = (x.shape[-2], x.shape[-1])
            inv_freq = ROPE_THETA ** (jnp.arange(0, d_k, 2, dtype=jnp.float32) / d_k)
            ang = jnp.arange(S, dtype=jnp.float32)[:, None] / inv_freq[None, :]
            cos, sin = (jnp.cos(ang), jnp.sin(ang))
            xp = x.reshape(x.shape[:-1] + (d_k // 2, 2))
            x0, x1 = (xp[..., 0], xp[..., 1])
            out = jnp.stack([x0 * cos - x1 * sin, x0 * sin + x1 * cos], axis=-1)
            return out.reshape(x.shape)
        key = jax.random.key(seed)
        k1, k2, k3 = jax.random.split(key, 3)
        B, S = (2, 512)
        std = 2.0 / (D_MODEL + 3 * D_MODEL)
        std_o = 2.0 / (D_MODEL + D_MODEL)
        return {'x': jax.random.normal(k1, (B, S, D_MODEL), dtype=jnp.float32), 'W_qkv': jax.random.normal(k2, (3 * D_MODEL, D_MODEL), dtype=jnp.float32) * std, 'W_o': jax.random.normal(k3, (D_MODEL, D_MODEL), dtype=jnp.float32) * std_o}
    _L0_attn_all = _L0_attn_setup()
    _L0_attn_in = {k: v for k, v in _L0_attn_all.items() if k in ('W_qkv', 'W_o')}
    del _L0_attn_all

    def _L0_ffn_setup():
        import jax, jax.numpy as jnp
        import numpy as np
        D_MODEL = 256
        D_FF = 1024
        N_EXPERTS = 8
        TOP_K = 2
        LN_EPS = 1e-06

        def _moe(x, router_w, w1, b1, w2, b2, gamma, beta):
            B, S, D = x.shape
            x_flat = x.reshape(-1, D)
            N = x_flat.shape[0]
            logits = x_flat @ router_w
            gate_vals, gate_idx = jax.lax.top_k(logits, TOP_K)
            gate_w = jax.nn.softmax(gate_vals, axis=-1)
            gates = jnp.zeros_like(logits).at[jnp.arange(N)[:, None], gate_idx].set(gate_w)
            h = jax.nn.gelu(jnp.einsum('nd,edf->enf', x_flat, w1) + b1[:, None, :], approximate=False)
            out = jnp.einsum('enf,efd->end', h, w2) + b2[:, None, :]
            res = x_flat[None, :, :] + out
            mu = jnp.mean(res, axis=-1, keepdims=True)
            var = jnp.mean(jnp.square(res - mu), axis=-1, keepdims=True)
            normed = (res - mu) * jax.lax.rsqrt(var + LN_EPS)
            expert_out = normed * gamma[:, None, :] + beta[:, None, :]
            y = jnp.einsum('end,ne->nd', expert_out, gates)
            return y.reshape(B, S, D)
        key = jax.random.key(seed)
        ks = jax.random.split(key, 8)
        x = jax.random.normal(ks[0], (2, 512, D_MODEL), dtype=jnp.float32)
        router_w = jax.random.normal(ks[1], (D_MODEL, N_EXPERTS), dtype=jnp.float32) * 0.02
        w1 = jax.random.normal(ks[2], (N_EXPERTS, D_MODEL, D_FF), dtype=jnp.float32) * 0.02
        b1 = jnp.zeros((N_EXPERTS, D_FF), dtype=jnp.float32)
        w2 = jax.random.normal(ks[3], (N_EXPERTS, D_FF, D_MODEL), dtype=jnp.float32) * 0.02
        b2 = jnp.zeros((N_EXPERTS, D_MODEL), dtype=jnp.float32)
        gamma = jnp.ones((N_EXPERTS, D_MODEL), dtype=jnp.float32)
        beta = jnp.zeros((N_EXPERTS, D_MODEL), dtype=jnp.float32)
        return {'x': x, 'router_w': router_w, 'w1': w1, 'b1': b1, 'w2': w2, 'b2': b2, 'gamma': gamma, 'beta': beta}
    _L0_ffn_all = _L0_ffn_setup()
    _L0_ffn_in = {k: v for k, v in _L0_ffn_all.items() if k in ('router_w', 'w1', 'b1', 'w2', 'b2', 'gamma', 'beta')}
    del _L0_ffn_all
    return {'x': x, 'txt': txt, 'L0_tok_W': _L0_tok_in['W'], 'L0_tok_b': _L0_tok_in['b'], 'L0_tok_cls_token': _L0_tok_in['cls_token'], 'L0_attn_W_qkv': _L0_attn_in['W_qkv'], 'L0_attn_W_o': _L0_attn_in['W_o'], 'L0_ffn_router_w': _L0_ffn_in['router_w'], 'L0_ffn_w1': _L0_ffn_in['w1'], 'L0_ffn_b1': _L0_ffn_in['b1'], 'L0_ffn_w2': _L0_ffn_in['w2'], 'L0_ffn_b2': _L0_ffn_in['b2'], 'L0_ffn_gamma': _L0_ffn_in['gamma'], 'L0_ffn_beta': _L0_ffn_in['beta']}

def reference(x, txt, L0_tok_W, L0_tok_b, L0_tok_cls_token, L0_attn_W_qkv, L0_attn_W_o, L0_ffn_router_w, L0_ffn_w1, L0_ffn_b1, L0_ffn_w2, L0_ffn_b2, L0_ffn_gamma, L0_ffn_beta):
    import jax
    import jax.numpy as jnp

    def _L0_tok_ref(x, W, b, cls_token):
        import jax, jax.numpy as jnp
        import numpy as np
        IMG = 96
        PATCH = 16
        CH = 3
        EMBED = 256
        PATCH_DIM = CH * PATCH * PATCH

        def _patchify(x):
            B, C, H, Wd = x.shape
            hp, wp = (H // PATCH, Wd // PATCH)
            p = x.reshape(B, C, hp, PATCH, wp, PATCH)
            p = p.transpose(0, 2, 4, 1, 3, 5)
            return p.reshape(B, hp * wp, C * PATCH * PATCH)
        B = x.shape[0]
        patches = _patchify(x)
        proj = jnp.einsum('bnd,de->bne', patches, W) + b
        cls = jnp.broadcast_to(cls_token, (B, 1, cls_token.shape[-1]))
        return jnp.concatenate((cls, proj), axis=1)

    def _L0_attn_ref(x, W_qkv, W_o):
        import jax, jax.numpy as jnp
        import numpy as np
        D_MODEL = 256
        NUM_HEADS = 16
        HEAD_DIM = D_MODEL // NUM_HEADS
        ROPE_THETA = 10000.0

        def apply_rope(x):
            S, d_k = (x.shape[-2], x.shape[-1])
            inv_freq = ROPE_THETA ** (jnp.arange(0, d_k, 2, dtype=jnp.float32) / d_k)
            ang = jnp.arange(S, dtype=jnp.float32)[:, None] / inv_freq[None, :]
            cos, sin = (jnp.cos(ang), jnp.sin(ang))
            xp = x.reshape(x.shape[:-1] + (d_k // 2, 2))
            x0, x1 = (xp[..., 0], xp[..., 1])
            out = jnp.stack([x0 * cos - x1 * sin, x0 * sin + x1 * cos], axis=-1)
            return out.reshape(x.shape)
        B, S, d_model = x.shape
        H, d_k = (NUM_HEADS, HEAD_DIM)
        qkv = jnp.einsum('bsi,oi->bso', x, W_qkv)
        Q, K, V = jnp.split(qkv, 3, axis=-1)

        def to_heads(t):
            return t.reshape(B, S, H, d_k).transpose(0, 2, 1, 3)
        Q, K, V = (to_heads(Q), to_heads(K), to_heads(V))
        Q, K = (apply_rope(Q), apply_rope(K))
        scores = jnp.einsum('bhqd,bhkd->bhqk', Q, K) / jnp.sqrt(jnp.float32(d_k))
        causal = jnp.tril(jnp.ones((S, S), dtype=bool))
        scores = jnp.where(causal, scores, -jnp.inf)
        attn = jax.nn.softmax(scores, axis=-1)
        out = jnp.einsum('bhqk,bhkd->bhqd', attn, V)
        out = out.transpose(0, 2, 1, 3).reshape(B, S, d_model)
        return jnp.einsum('bsi,oi->bso', out, W_o)

    def _L0_ffn_ref(x, router_w, w1, b1, w2, b2, gamma, beta):
        import jax, jax.numpy as jnp
        import numpy as np
        D_MODEL = 256
        D_FF = 1024
        N_EXPERTS = 8
        TOP_K = 2
        LN_EPS = 1e-06

        def _moe(x, router_w, w1, b1, w2, b2, gamma, beta):
            B, S, D = x.shape
            x_flat = x.reshape(-1, D)
            N = x_flat.shape[0]
            logits = x_flat @ router_w
            gate_vals, gate_idx = jax.lax.top_k(logits, TOP_K)
            gate_w = jax.nn.softmax(gate_vals, axis=-1)
            gates = jnp.zeros_like(logits).at[jnp.arange(N)[:, None], gate_idx].set(gate_w)
            h = jax.nn.gelu(jnp.einsum('nd,edf->enf', x_flat, w1) + b1[:, None, :], approximate=False)
            out = jnp.einsum('enf,efd->end', h, w2) + b2[:, None, :]
            res = x_flat[None, :, :] + out
            mu = jnp.mean(res, axis=-1, keepdims=True)
            var = jnp.mean(jnp.square(res - mu), axis=-1, keepdims=True)
            normed = (res - mu) * jax.lax.rsqrt(var + LN_EPS)
            expert_out = normed * gamma[:, None, :] + beta[:, None, :]
            y = jnp.einsum('end,ne->nd', expert_out, gates)
            return y.reshape(B, S, D)
        return _moe(x, router_w, w1, b1, w2, b2, gamma, beta)
    h = _L0_tok_ref(x, L0_tok_W, L0_tok_b, L0_tok_cls_token)
    h = jnp.concatenate([h, txt], axis=1)
    h = h + _L0_attn_ref(_layernorm(h, axis=-1), L0_attn_W_qkv, L0_attn_W_o)
    h = h + _L0_ffn_ref(_layernorm(h, axis=-1), L0_ffn_router_w, L0_ffn_w1, L0_ffn_b1, L0_ffn_w2, L0_ffn_b2, L0_ffn_gamma, L0_ffn_beta)
    return h

_drawn_inputs = setup_inputs


def setup_inputs(seed=0):
    import zlib

    import numpy as np

    out = dict(_drawn_inputs(seed))
    spreads = {'L0_tok_cls_token': (0.0, 0.1),
     'L0_ffn_b1': (0.0, 0.47),
     'L0_ffn_b2': (0.0, 0.1),
     'L0_ffn_gamma': (1.0, 0.2),
     'L0_ffn_beta': (0.0, 0.1)}
    factors = {'L0_tok_b': 2.835, 'L0_attn_W_qkv': 8.0, 'L0_attn_W_o': 8.0}
    for name, (base, spread) in spreads.items():
        noise = np.random.default_rng([zlib.crc32(name.encode()), seed]).standard_normal(out[name].shape)
        drawn = base * np.exp(spread * noise) if base else spread * noise
        out[name] = jnp.asarray(drawn.astype(out[name].dtype))
    for name, factor in factors.items():
        out[name] = (out[name] * factor).astype(out[name].dtype)
    return out
```

```python
from contextlib import ExitStack

import numpy as np
import concourse.bass as bass
from concourse import mybir

F32 = mybir.dt.float32
F16 = mybir.dt.float16
BF16 = mybir.dt.bfloat16
I32 = mybir.dt.int32
U32 = mybir.dt.uint32
ALU = mybir.AluOpType
ACT = mybir.ActivationFunctionType
AX = mybir.AxisListType

P = 128
NB, CH, IMG, PATCH = 16, 3, 96, 16
GRID = IMG // PATCH
NPATCH = GRID * GRID
KP = CH * PATCH * PATCH // P
D = 256
KD = D // P
TXT = 128
S = 1 + NPATCH + TXT
SR = S + 1
TAIL = S - P
HEAD = 1 + NPATCH
NH, DK = 16, 16
PAIRS = NH // 2
E, FF = 8, 1024
KF = FF // P
N = NB * S
REG = N + P
XROW = D + 2
TILES = (2 * N + E * (P - 1)) // P
WSCALE = 64.0
NEG = -1.0e30
LN1_EPS = 1e-5
MOE_EPS = 1e-6
MSCALE = 16.0
TAIL_UNITS = [(0, 3, 3), (6, 1, 1)]
ST_UNITS = [(0, 3), (3, 3), (6, 2)]
SLOT = 64


def wait_apart(eng, sem, value, stood):
    if not isinstance(value, int):
        value = eng.to_reg(value)
    eng.wait_ge(stood, 1)
    eng.wait_ge(sem, value)


class Chain:

    def __init__(self, eng, sem, base, stood=None):
        self.eng, self.sem, self.base, self.stood, self.n = eng, sem, base, stood, 0

    def __call__(self, ins, alone=False):
        self.n += 1
        ins.then_inc(self.sem, 1)
        if alone:
            wait_apart(self.eng, self.sem, self.base + self.n, self.stood)
        else:
            self.eng.wait_ge(self.sem, self.base + self.n)


def stage_patches(nc, patch_t, tok_w, tok_b, pe_rows):
    tiles = [(t * P, min(P, NB * NPATCH - t * P)) for t in range(-(-NB * NPATCH // P))]
    with ExitStack() as ctx:
        sb = lambda n, s, d: ctx.enter_context(nc.sbuf_tensor(n, s, d))
        sem = lambda n: ctx.enter_context(nc.semaphore(n))
        pt = sb("pt", [P, KP, NB * NPATCH], F32)
        pw = sb("pw", [P, KP, D], F32)
        pb = sb("pb", [P, D], F32)
        emb = sb("emb", [P, len(tiles), D], F32)
        acc = [ctx.enter_context(nc.psum_tensor(f"pacc{i}", [P, 512], F32)) for i in range(len(tiles))]
        w_in = sem("w_in")
        x_in = [sem(f"x_in{k}") for k in range(KP)]
        b_in = sem("b_in")
        emb_mm = sem("emb_mm")
        emb_ok = sem("emb_ok")
        pe_out = sem("pe_out")
        block = ctx.enter_context(nc.Block())

        @block.sync
        def _(sp):
            for k in range(KP):
                sp.dma_start(pt[:, k, :], patch_t[k * P:(k + 1) * P, :]).then_inc(x_in[k], 16)
            for t, (r0, n) in enumerate(tiles):
                sp.wait_ge(emb_ok, t + 1)
                sp.dma_start(pe_rows[r0:r0 + n, :], emb[0:n, t, :]).then_inc(pe_out, 16)
            sp.wait_ge(pe_out, 16 * len(tiles))

        @block.scalar
        def _(act):
            act.dma_start(pw[:, :, :], tok_w.rearrange("(k p) d -> p k d", p=P)).then_inc(w_in, 16)
            act.dma_start(pb[:, :], tok_b.rearrange("(a d) -> a d", a=1).to_broadcast([P, D])).then_inc(b_in, 16)

        @block.tensor
        def _(pe):
            pe.wait_ge(w_in, 16)
            for k in range(KP):
                pe.wait_ge(x_in[k], 16)
                for t, (r0, n) in enumerate(tiles):
                    mm = nc.tensor.matmul(acc[t][0:n, 0:D], pt[:, k, r0:r0 + n], pw[:, k, :],
                                          start=(k == 0), stop=(k == KP - 1))
                    if k == KP - 1:
                        mm.then_inc(emb_mm, 1)

        @block.vector
        def _(dve):
            dve.wait_ge(b_in, 16)
            for t, (r0, n) in enumerate(tiles):
                dve.wait_ge(emb_mm, t + 1)
                nc.vector.tensor_tensor(emb[0:n, t, :], acc[t][0:n, 0:D], pb[0:n, :], ALU.add).then_inc(emb_ok, 1)


def stage_attention(nc, a, wts):
    W1H, W1L, W2H, W2L = wts
    with ExitStack() as ctx:
        sb = lambda n, s, d: ctx.enter_context(nc.sbuf_tensor(n, s, d))
        ps = lambda n, s, d=F32: ctx.enter_context(nc.psum_tensor(n, s, d))
        sem = lambda n: ctx.enter_context(nc.semaphore(n))

        ident = sb("ident", [P, P], F32)
        ident_h = sb("ident_h", [P, P], F16)
        ident_b = sb("ident_b", [P, P], BF16)
        mask_m = sb("mask_m", [P, 4, P], BF16)
        mask_t = sb("mask_t", [P, 3, S], BF16)
        cosT = sb("cosT", [P, 2, DK], F32)
        sinT = sb("sinT", [P, 2, DK], F32)
        upper = sb("upper", [P, P], BF16)
        ones_b = sb("ones_b", [P, P], BF16)
        route_c = sb("route_c", [P, 24], F32)
        wq_h = sb("wq_h", [P, KD, 3 * D], F16)
        wq_l = sb("wq_l", [P, KD, 3 * D], F16)
        wo_h = sb("wo_h", [P, KD, D], F16)
        wo_l = sb("wo_l", [P, KD, D], F16)
        rw = sb("rw", [P, KD, E], F32)
        H = sb("H", [P, 2, 2, D], F32)
        st1 = sb("st1", [P, 2, 6], F32)
        mv1 = sb("mv1", [P, 2, 2], F32)
        rs1 = sb("rs1", [P, 2, 1], F32)
        ve1 = sb("ve1", [P, 2, 1], F32)
        ve2 = sb("ve2", [P, 2, 1], F32)
        mhalf = sb("mhalf", [P, 2, 1], F32)
        xn = sb("xn", [P, 2, D], F32)
        xh = sb("xh", [P, KD, 2 * P], F16)
        xl = sb("xl", [P, KD, 2 * P], F16)
        rt1 = sb("rt1", [P, 2, 2 * D], F32)
        rt2 = sb("rt2", [P, 2, 2 * D], F32)
        blk = sb("blk", [P, 2, 2, NH, SLOT], F16)
        V = sb("V", [P, 2, 2, NH, DK + 1], F32)
        QA = sb("QA", [P, PAIRS, SR], F16)
        KA = sb("KA", [P, PAIRS, SR], F16)
        mx_m = sb("mx_m", [P, 2, PAIRS], F32)
        mx_t = sb("mx_t", [P, 2, 4], F32)
        mT_m = sb("mT_m", [2 * PAIRS, P], F16)
        mT_t = sb("mT_t", [8, P], F16)
        PT = sb("PT", [P, 2, PAIRS, S], F32)
        PTt = sb("PTt", [P, 2, PAIRS, TAIL], F32)
        rec = sb("rec", [P, 2, NH], F32)
        On = sb("On", [P, 2, D], F32)
        oh = sb("oh", [P, KD, 2 * P], F16)
        ol = sb("ol", [P, KD, 2 * P], F16)
        H2 = sb("H2", [P, 2, D], F32)
        st2 = sb("st2", [P, 2, 6], F32)
        mv2 = sb("mv2", [P, 2, 2], F32)
        rs2 = sb("rs2", [P, 2, 1], F32)
        XR = sb("XR", [P, 2, 2, XROW], F32)
        x2T = PTt[:, :, :, :].rearrange("p a j t -> p (a j t)")[:, 0:KD * 2 * P].rearrange("p (k t) -> p k t", k=KD)
        lg = sb("lg", [P, 2, E], F32)
        m8 = sb("m8", [P, 2, 8], F32)
        i8 = sb("i8", [P, 2, 8], U32)
        idf = sb("idf", [P, 2, 2], F32)
        df = sb("df", [P, 2, 1], F32)
        ed = sb("ed", [P, 2, 1], F32)
        e1 = sb("e1", [P, 2, 1], F32)
        onehot = sb("onehot", [P, 2, 2, E], F32)
        cnt = sb("cnt", [P, 2, E], BF16)
        run = sb("run", [P, 2, E], F32)
        runb = sb("runb", [P, 2, E], BF16)
        rkb = sb("rkb", [P, 2, E], F32)
        prod = sb("prod", [P, 2, 2, E], F32)
        slotf = sb("slotf", [P, 2, 2], F32)
        slotu = sb("slotu", [P, 2, 2], U32)
        dest = sb("dest", [P, 2, 2], F32)
        stg = sb("stg", [P, 2, FF], F32)

        A = [ps(f"A{i}", [P, 512]) for i in range(6, 8)]
        A6, A7 = A
        AQ = ps("AQ", [P, 2, 512])
        AS = [ps("AS0", [P, 512]), ps("AS1", [P, 512])]
        AT = [ps("AT0", [P, 512]), ps("AT1", [P, 512])]

        names = ("ve1_ok ve2_ok rs1_ok rs2_ok const_in h_in0 h_in1 wst memsets wsplit_h wsplit_l qwo_in fch bch pch "
                 "xn_ok xT_ps xh_ok xl_ok qk_ps v_ps v_ok rt_ok rope_ok hi_ok lo_ok qa_ps qa_ev s_ps s_max "
                 "mt_ps mt_ok mrow st_ps exp_ok sel_ok pv_ps on_ok ot_ps oh_ok ol_ok pj_ps h2_ok x2_ok x2b_ok x2t_ps x2t_ok "
                 "lg_ps lg_ok df_ok ed_ok cnt_ok rk_ps rk_ok slot_ok row_ok scat0 scat1 h2_out whi wlo a7_free cmem actm wcv").split()
        s = {n: sem(n) for n in names}
        block = ctx.enter_context(nc.Block())
        h_in = [s["h_in0"], s["h_in1"]]

        def w1_src(b):
            return a["w1"].rearrange("e (k p) f -> p (e k) f", p=P)[:, bass.ds(b, 1), :]

        def w2_src(b):
            return a["w2"].rearrange("e (k p) f -> p (e k) f", p=P)[:, bass.ds(b * 4, 4), :]

        CONSTS = [(ident, "ident"), (ident_h, "ident_h"), (ident_b, "ident_b"), (mask_m, "mask_m"), (mask_t, "mask_t"),
                  (cosT, "cosT"), (sinT, "sinT"), (upper, "upper"), (ones_b, "ones_b"), (route_c, "route_c")]

        def loop(eng, step, first, last):
            first()
            with eng.Fori(0, (NB - 2) // 2) as g:
                step(g * 2 + 1, 1)
                step(g * 2 + 2, 0)
            step(NB - 1, 1)
            last()

        @block.sync
        def _(sp):
            sp.dma_start(stg[:, :, :].rearrange("p a f -> p (a f)")[:, 0:3 * D * KD].rearrange("p (k f) -> p k f", k=KD),
                         a["wqkv_t"].rearrange("(k p) f -> p k f", p=P)).then_inc(s["qwo_in"], 16)
            sp.dma_start(stg[:, :, :].rearrange("p a f -> p (a f)")[:, 3 * D * KD:4 * D * KD].rearrange("p (k f) -> p k f", k=KD),
                         a["wo_t"].rearrange("(k p) f -> p k f", p=P)).then_inc(s["qwo_in"], 16)
            for t, n in CONSTS:
                dst = t[:].bitcast(mybir.dt.uint16) if t.dtype == BF16 else t[:]
                sp.dma_start(dst, a[n]).then_inc(s["const_in"], 16)
            sp.dma_start(rw[:, :, :], a["router"].rearrange("(k p) e -> p k e", p=P)).then_inc(s["const_in"], 16)

            def load_h(b, par):
                sp.dma_start(H[0:1, par, 0, :], a["cls"].rearrange("a b d -> (a b) d")).then_inc(h_in[par], 16)
                sp.dma_start(H[1:HEAD, par, 0, :], a["pe_rows"][bass.ds(b * NPATCH, NPATCH), :]).then_inc(h_in[par], 16)
                txt = a["txt"].rearrange("b t d -> (b t) d")
                sp.dma_start(H[HEAD:P, par, 0, :], txt[bass.ds(b * TXT, P - HEAD), :]).then_inc(h_in[par], 16)
                sp.dma_start(H[0:TAIL, par, 1, :], txt[bass.ds(b * TXT + P - HEAD, TAIL), :]).then_inc(h_in[par], 16)

            def load_w(b):
                sp.dma_start(stg[:, 0:1, :], w1_src(b)).then_inc(s["wst"], 16)
                sp.dma_start(stg[:, 1, :].rearrange("p (a f) -> p a f", a=4), w2_src(b)).then_inc(s["wst"], 16)

            def mrow(b):
                sp.wait_ge(s["mt_ok"], 2 * b + 2)
                sp.dma_start(QA[48:49, :, 0:P], mT_m[0:PAIRS, :]).then_inc(s["mrow"], 16)
                sp.dma_start(QA[112:113, :, 0:P], mT_m[PAIRS:2 * PAIRS, :]).then_inc(s["mrow"], 16)
                for par in range(2):
                    row = QA[48 + 64 * par:49 + 64 * par, :, P:S]
                    for a0, n, gap in TAIL_UNITS:
                        c = 4 * par + (0 if a0 == 0 else 3)
                        sp.dma_start(row[:, a0:a0 + n, :], mT_t[c:c + n, 0:TAIL]).then_inc(s["mrow"], 16)
                        sp.dma_start(row[:, a0 + gap:a0 + gap + n, :], mT_t[c:c + n, 64:64 + TAIL]).then_inc(s["mrow"], 16)

            def store_h2(b):
                sp.wait_ge(s["h2_ok"], b + 1)
                sp.dma_start(a["h2_rows"][bass.ds(b * S, P), :], H2[:, 0, :]).then_inc(s["h2_out"], 16)
                sp.dma_start(a["h2_rows"][bass.ds(b * S + P, TAIL), :], H2[0:TAIL, 1, :]).then_inc(s["h2_out"], 16)

            sp.wait_ge(s["cmem"], 1)
            load_h(0, 0)
            load_h(1, 1)
            sp.wait_ge(s["wcv"], 4)
            load_w(0)

            def next_w(b):
                sp.wait_ge(s["wlo"], b + 1)
                load_w(b + 1)

            def first():
                mrow(0)
                next_w(0)

            def step(b, par):
                store_h2(b - 1)
                more = not (isinstance(b, int) and b == NB - 1)
                if more:
                    load_h(b + 1, 1 - par)
                mrow(b)
                if more:
                    next_w(b)

            loop(sp, step, first, lambda: store_h2(NB - 1))
            sp.wait_ge(s["h2_out"], 32 * NB)

        @block.gpsimd
        def _(pool):
            nc.gpsimd.memset(H[:, :, 1, :], 0.0)
            nc.gpsimd.memset(On[:, 1, :], 0.0)
            nc.gpsimd.memset(V[:, :, :, :, DK:DK + 1], 1.0)
            nc.gpsimd.memset(run[:, :, :], 0.0)
            nc.gpsimd.memset(mhalf[:, :, :], -0.5)
            nc.gpsimd.memset(blk[:, :, 0, :, 48:SLOT], 0.0)
            nc.gpsimd.memset(blk[:, :, 1, :, 48:SLOT], 0.0).then_inc(s["pch"], 1)
            pool.wait_ge(s["pch"], 1)
            nc.gpsimd.memset(blk[:, :, 1, :, 48:49], MSCALE).then_inc(s["cmem"], 1)
            pool.wait_ge(s["const_in"], 16 * (len(CONSTS) + 1))
            nc.gpsimd.tensor_copy(dest[:, :, :], route_c[:, 18:22].rearrange("p (a b) -> p a b", a=2)).then_inc(s["cmem"], 1)
            def rsqrt(ve, rs, done, wanted, b):
                pool.wait_ge(s[wanted], b + 1)
                nc.gpsimd.tensor_tensor(rs[:, :, :], ve[:, :, :], mhalf[:, :, :], ALU.pow).then_inc(s[done], 1)

            def rsqrt1(b):
                rsqrt(ve1, rs1, "rs1_ok", "ve1_ok", b)

            def rsqrt2(b):
                rsqrt(ve2, rs2, "rs2_ok", "ve2_ok", b)

            def rope(b):
                pool.wait_ge(s["rt_ok"], 3 * b + 3)
                nc.gpsimd.tensor_tensor(rt1[:, :, :], rt1[:, :, :], rt2[:, :, :], ALU.add).then_inc(s["rope_ok"], 1)

            def lows(b):
                pool.wait_ge(s["hi_ok"], 4 * b + 4)
                r = rt1[:, :, :].rearrange("p a (q h d) -> p a q h d", q=2, h=NH)
                for q, slot in ((0, 2), (1, 1)):
                    nc.gpsimd.tensor_tensor(blk[:, :, q, :, slot * DK:(slot + 1) * DK], r[:, :, q],
                                            blk[:, :, q, :, 0:DK], ALU.subtract).then_inc(s["lo_ok"], 1)

            def select(b):
                for r, (a0, n) in enumerate(ST_UNITS):
                    for par in range(2):
                        wait_apart(pool, s["exp_ok"], 8 * b + 2 * r + par + 1, s["pch"])
                        v = PT[:, par, a0:a0 + n, 0:P]
                        nc.gpsimd.affine_select(out=v, in_=v, compare_op=ALU.is_ge, fill=0.0, base=0,
                                                pattern=[[0, n], [1, P]], channel_multiplier=-1).then_inc(s["sel_ok"], 1)
                wait_apart(pool, s["exp_ok"], 8 * b + 8, s["pch"])
                v = PTt[0:TAIL, :, :, :].rearrange("p a j t -> p (a j) t")
                nc.gpsimd.affine_select(out=v, in_=v, compare_op=ALU.is_ge, fill=0.0, base=0,
                                        pattern=[[0, 2 * PAIRS], [1, TAIL]], channel_multiplier=-1).then_inc(s["sel_ok"], 1)

            def scatter(b, par):
                wait_apart(pool, s["row_ok"], b + 1, s["pch"])
                pool.wait_ge(s["x2b_ok"], b + 1)
                pool.wait_ge(s["slot_ok"], b + 1)
                for half, n in ((0, P), (1, TAIL)):
                    for c in range(2):
                        nc.gpsimd.indirect_dma_start(
                            out=a["slots"], out_offset=bass.IndirectOffsetOnAxis(ap=slotu[0:n, half, c:c + 1], axis=0),
                            in_=XR[0:n, half, c, :], in_offset=None).then_inc(s["scat0"], 16)

            def first():
                rsqrt1(0)
                rope(0)
                lows(0)
                rsqrt1(1)

            def step(b, par):
                select(b - 1)
                rope(b)
                lows(b)
                if isinstance(b, int) and b == NB - 1:
                    rsqrt2(b - 1)
                else:
                    rsqrt2(b - 1)
                    rsqrt1(b + 1)
                scatter(b - 1, par)

            loop(pool, step, first, lambda: (select(NB - 1), rsqrt2(NB - 1), scatter(NB - 1, 0)))
            pool.wait_ge(s["scat0"], 64 * NB)

        @block.scalar
        def _(act):
            act.wait_ge(s["qwo_in"], 32)
            wq = stg[:, :, :].rearrange("p a f -> p (a f)")[:, 0:3 * D * KD].rearrange("p (k f) -> p k f", k=KD)
            wo = stg[:, :, :].rearrange("p a f -> p (a f)")[:, 3 * D * KD:4 * D * KD].rearrange("p (k f) -> p k f", k=KD)
            nc.scalar.activation(wq_h[:, :, :], wq, ACT.Copy, scale=WSCALE).then_inc(s["wcv"], 1)
            nc.scalar.activation(wo_h[:, :, :], wo, ACT.Copy, scale=WSCALE).then_inc(s["wcv"], 1)

            def x_high(b):
                act.wait_ge(s["xT_ps"], b + 1)
                nc.scalar.activation(xh[:, :, :], A6[:, :].rearrange("p (k t) -> p k t", k=KD), ACT.Copy).then_inc(s["xh_ok"], 1)

            def v_copy(b, par):
                act.wait_ge(s["v_ps"], b + 1)
                for half in range(2):
                    nc.scalar.activation(V[:, par, half, :, 0:DK],
                                         A6[:, half * D:(half + 1) * D].rearrange("p (h d) -> p h d", h=NH),
                                         ACT.Copy, scale=1.0 / WSCALE).then_inc(s["v_ok"], 1)

            def highs(b):
                act.wait_ge(s["rope_ok"], b + 1)
                r = rt1[:, :, :].rearrange("p a (q h d) -> p a q h d", q=2, h=NH)
                for q, slot in ((0, 0), (1, 0), (0, 1), (1, 2)):
                    nc.scalar.activation(blk[:, :, q, :, slot * DK:(slot + 1) * DK], r[:, :, q], ACT.Copy).then_inc(s["hi_ok"], 1)

            def qa_evac(b):
                for u in (0, 2):
                    act.wait_ge(s["qa_ps"], 4 * b + u + 1)
                    dst = (QA, KA)[u // 2][:, 0:4, 0:S]
                    src = AQ[:, u % 2, :].bitcast(F16)[:, 0:4 * SR].rearrange("p (j t) -> p j t", j=4)[:, :, 0:S]
                    nc.scalar.activation(dst, src, ACT.Copy).then_inc(s["qa_ev"], 1)

            def exps(b):
                if not (isinstance(b, int) and b == 0):
                    act.wait_ge(s["pv_ps"], b)
                u = 0
                for a0, n in ST_UNITS:
                    for par in range(2):
                        u += 1
                        act.wait_ge(s["st_ps"], 8 * b + u)
                        nc.scalar.activation(PT[:, par, a0:a0 + n, :],
                                             AT[par][:, 0:n * S].rearrange("p (j t) -> p j t", j=n),
                                             ACT.Exp, scale=DK ** -0.5).then_inc(s["exp_ok"], 1)
                for par in range(2):
                    u += 1
                    act.wait_ge(s["st_ps"], 8 * b + u)
                    nc.scalar.activation(PTt[0:TAIL, par, :, :],
                                         AT[par][0:TAIL, 0:PAIRS * TAIL].rearrange("p (j t) -> p j t", j=PAIRS),
                                         ACT.Exp, scale=DK ** -0.5).then_inc(s["exp_ok"], 1)

            def w_high(b, par):
                act.wait_ge(s["wst"], 32 * b + 32)
                nc.scalar.activation(W1H[:, bass.ds(b, 1), :], stg[:, 0:1, :], ACT.Copy, scale=WSCALE)
                nc.scalar.activation(W2H[:, bass.ds(b * 4, 4), :], stg[:, 1, :].rearrange("p (a f) -> p a f", a=4),
                                     ACT.Copy, scale=WSCALE).then_inc(s["whi"], 1)

            def o_high(b):
                act.wait_ge(s["ot_ps"], b + 1)
                nc.scalar.activation(oh[:, :, :], A7[:, :].rearrange("p (k t) -> p k t", k=KD), ACT.Copy).then_inc(s["oh_ok"], 1)

            def x2_t(b):
                act.wait_ge(s["x2t_ps"], b + 1)
                nc.scalar.activation(x2T[:, :, :], A7[:, :].rearrange("p (k t) -> p k t", k=KD), ACT.Copy).then_inc(s["x2t_ok"], 1)

            def x2_copy(b):
                act.wait_ge(s["x2_ok"], b + 1)
                nc.scalar.activation(XR[:, :, 1, 0:D], XR[:, :, 0, 0:D], ACT.Copy).then_inc(s["x2b_ok"], 1)

            def gate_exp(b):
                act.wait_ge(s["df_ok"], b + 1)
                nc.scalar.activation(ed[:, :, :], df[:, :, :], ACT.Exp).then_inc(s["ed_ok"], 1)

            def first():
                x_high(0)
                act.wait_ge(s["cmem"], 2)
                v_copy(0, 0)
                highs(0)
                qa_evac(0)
                w_high(0, 0)

            def step(b, par):
                x_high(b)
                exps(b - 1)
                v_copy(b, par)
                highs(b)
                qa_evac(b)
                o_high(b - 1)
                x2_copy(b - 1)
                x2_t(b - 1)
                gate_exp(b - 1)
                w_high(b, par)

            def last():
                b = NB - 1
                exps(b)
                o_high(b)
                x2_copy(b)
                x2_t(b)
                gate_exp(b)

            loop(act, step, first, last)

        @block.vector
        def _(dve):
            act_w = stg[:, :, :].rearrange("p a f -> p (a f)")[:, 0:3 * D * KD].rearrange("p (k f) -> p k f", k=KD)
            act_o = stg[:, :, :].rearrange("p a f -> p (a f)")[:, 3 * D * KD:4 * D * KD].rearrange("p (k f) -> p k f", k=KD)
            dve.wait_ge(s["wcv"], 2)
            nc.vector.scalar_tensor_tensor(out=wq_l[:, :, :], in0=act_w, scalar=WSCALE, in1=wq_h[:, :, :],
                                           op0=ALU.mult, op1=ALU.subtract).then_inc(s["wcv"], 1)
            nc.vector.scalar_tensor_tensor(out=wo_l[:, :, :], in0=act_o, scalar=WSCALE, in1=wo_h[:, :, :],
                                           op0=ALU.mult, op1=ALU.subtract).then_inc(s["wcv"], 1)
            dve.wait_ge(s["const_in"], 16 * (len(CONSTS) + 1))
            dve.wait_ge(s["cmem"], 2)

            def stats(link, src, st, mv, ve):
                for half in range(2):
                    ins = nc.vector.bn_stats(st[:, half, :], src[:, half, :])
                link(ins, alone=True)
                for half in range(2):
                    ins = nc.vector.bn_aggr(mv[:, half, :], st[:, half, :])
                link(ins)
                return nc.vector.tensor_scalar(ve[:, :, :], mv[:, :, 1:2], LN1_EPS, None, ALU.add)

            def normed(src, mv, rs, dst):
                for half in range(2):
                    ins = nc.vector.tensor_scalar(dst[:, half], src[:, half, :], mv[:, half, 0:1], rs[:, half, :],
                                                  ALU.subtract, ALU.mult)
                return ins

            def norm1(b, par):
                link = Chain(dve, s["fch"], b * 2, s["cmem"])
                dve.wait_ge(h_in[par], 64 * (b // 2 + 1) if isinstance(b, int) else (b + (2 - par)) * 32)
                stats(link, H[:, par], st1, mv1, ve1).then_inc(s["ve1_ok"], 1)

            def norm1_apply(b, par):
                dve.wait_ge(s["rs1_ok"], b + 1)
                normed(H[:, par], mv1, rs1, xn).then_inc(s["xn_ok"], 1)

            def x_low(b):
                dve.wait_ge(s["xh_ok"], b + 1)
                nc.vector.tensor_tensor(xl[:, :, :], A6[:, :].rearrange("p (k t) -> p k t", k=KD), xh[:, :, :],
                                        ALU.subtract).then_inc(s["xl_ok"], 1)

            def rot(b):
                dve.wait_ge(s["qk_ps"], b + 1)
                if not (isinstance(b, int) and b == 0):
                    dve.wait_ge(s["lo_ok"], 2 * b)
                def heads(v):
                    return v.rearrange("p a (h n two) -> p a h n two", h=2 * NH, two=2)

                def table(v, which):
                    v = v[:, :, :].rearrange("p a (o n two) -> p a o n two", o=1, two=2)[:, :, :, :, which]
                    return v.to_broadcast([P, 2, 2 * NH, DK // 2])
                cs = cosT[:, :, :].rearrange("p a (o n) -> p a o n", o=1).to_broadcast([P, 2, 2 * NH, DK])
                nc.vector.tensor_tensor(rt1[:, :, :].rearrange("p a (h n) -> p a h n", n=DK),
                                        AQ[:, :, :].rearrange("p a (h n) -> p a h n", n=DK), cs, ALU.mult).then_inc(s["rt_ok"], 1)
                for even in range(2):
                    nc.vector.tensor_tensor(heads(rt2[:, :, :])[:, :, :, :, even], heads(AQ[:, :, :])[:, :, :, :, 1 - even],
                                            table(sinT, even), ALU.mult).then_inc(s["rt_ok"], 1)

            def qa_evac(b):
                for u in (1, 3):
                    dve.wait_ge(s["qa_ps"], 4 * b + u + 1)
                    dst = (QA, KA)[u // 2][:, 4:8, 0:S]
                    src = AQ[:, u % 2, :].bitcast(F16)[:, 0:4 * SR].rearrange("p (j t) -> p j t", j=4)[:, :, 0:S]
                    nc.vector.tensor_copy(dst, src).then_inc(s["qa_ev"], 1)

            def maxima(b):
                u = 0
                for r in range(2):
                    for par in range(2):
                        u += 1
                        dve.wait_ge(s["s_ps"], 8 * b + u)
                        nc.vector.tensor_reduce(mx_m[:, par, 4 * r:4 * r + 4],
                                                AS[par][:, :].rearrange("p (j t) -> p j t", j=4), AX.X, ALU.max).then_inc(s["s_max"], 1)
                for c0, (a0, n, gap) in zip((0, 3), TAIL_UNITS):
                    for par in range(2):
                        u += 1
                        dve.wait_ge(s["s_ps"], 8 * b + u)
                        nc.vector.tensor_reduce(mx_t[:, par, c0:c0 + n],
                                                AS[par][:, 0:n * S].rearrange("p (j t) -> p j t", j=n), AX.X, ALU.max).then_inc(s["s_max"], 1)

            def m_rows(b):
                dve.wait_ge(s["mt_ps"], b + 1)
                nc.vector.tensor_scalar(mT_m[:, :], A6[0:2 * PAIRS, 0:P], -1.0 / MSCALE, None, ALU.mult).then_inc(s["mt_ok"], 1)
                nc.vector.tensor_scalar(mT_t[:, :], A6[0:8, P:2 * P], -1.0 / MSCALE, None, ALU.mult).then_inc(s["mt_ok"], 1)

            def w_low(b, par):
                dve.wait_ge(s["whi"], b + 1)
                nc.vector.scalar_tensor_tensor(out=W1L[:, bass.ds(b, 1), :], in0=stg[:, 0:1, :], scalar=WSCALE,
                                               in1=W1H[:, bass.ds(b, 1), :], op0=ALU.mult, op1=ALU.subtract)
                nc.vector.scalar_tensor_tensor(out=W2L[:, bass.ds(b * 4, 4), :], in0=stg[:, 1, :].rearrange("p (a f) -> p a f", a=4),
                                               scalar=WSCALE, in1=W2H[:, bass.ds(b * 4, 4), :],
                                               op0=ALU.mult, op1=ALU.subtract).then_inc(s["wlo"], 1)

            def o_norm(b, link):
                dve.wait_ge(s["pv_ps"], b + 1)
                nc.vector.reciprocal(rec[:, 0, :], AT[0][:, 0:NH * (DK + 1)].rearrange("p (h d) -> p h d", h=NH)[:, :, DK])
                link(nc.vector.reciprocal(rec[0:TAIL, 1, :],
                                          AT[1][0:TAIL, 0:NH * (DK + 1)].rearrange("p (h d) -> p h d", h=NH)[:, :, DK]))
                for half, n in ((0, P), (1, TAIL)):
                    o = AT[half][0:n, 0:NH * (DK + 1)].rearrange("p (h d) -> p h d", h=NH)[:, :, 0:DK]
                    ins = nc.vector.tensor_tensor(On[0:n, half, :].rearrange("p (h d) -> p h d", h=NH), o,
                                                  rec[0:n, half, :].rearrange("p (h a) -> p h a", a=1).to_broadcast([n, NH, DK]),
                                                  ALU.mult)
                    ins.then_inc(s["on_ok"], 1)

            def o_low(b):
                dve.wait_ge(s["oh_ok"], b + 1)
                nc.vector.tensor_tensor(ol[:, :, :], A7[:, :].rearrange("p (k t) -> p k t", k=KD), oh[:, :, :],
                                        ALU.subtract).then_inc(s["ol_ok"], 1)

            def residual(b, par, link):
                dve.wait_ge(s["pj_ps"], b + 1)
                if not (isinstance(b, int) and b == 0):
                    dve.wait_ge(s["h2_out"], 32 * b)
                    dve.wait_ge(s["scat0"], 64 * b)
                ins = nc.vector.scalar_tensor_tensor(out=H2[:, :, :], in0=A7[:, :].rearrange("p (a t) -> p a t", a=2),
                                                     scalar=1.0 / WSCALE, in1=H[:, par], op0=ALU.mult, op1=ALU.add)
                ins.then_inc(s["h2_ok"], 1)
                dve.wait_ge(s["h2_ok"], b + 1)
                stats(link, H2, st2, mv2, ve2).then_inc(s["ve2_ok"], 1)

            def norm2_apply(b):
                dve.wait_ge(s["rs2_ok"], b + 1)
                normed(H2, mv2, rs2, XR[:, :, 0, 0:D]).then_inc(s["x2_ok"], 1)

            def routing(b, link):
                dve.wait_ge(s["lg_ps"], b + 1)
                link(nc.vector.tensor_copy(lg[:, :, :], A7[:, 0:2 * E].rearrange("p (a e) -> p a e", a=2)), alone=True)
                for half in range(2):
                    ins = nc.vector.max(m8[:, half, :], lg[:, half, :])
                link(ins, alone=True)
                for half in range(2):
                    ins = nc.vector.max_index(i8[:, half, :], m8[:, half, :], lg[:, half, :])
                link(ins)
                nc.vector.tensor_tensor(df[:, :, :], m8[:, :, 1:2], m8[:, :, 0:1], ALU.subtract).then_inc(s["df_ok"], 1)
                link(nc.vector.tensor_tensor(idf[:, :, :], i8[:, :, 0:2],
                                             route_c[:, 16:18].rearrange("p (a o) -> p a o", o=1).to_broadcast([P, 2, 2]), ALU.add))
                for half in range(2):
                    for c in range(2):
                        ins = nc.vector.tensor_scalar(onehot[:, half, c, :], route_c[:, 0:E], idf[:, half, c:c + 1], None, ALU.is_equal)
                link(ins)
                link(nc.vector.tensor_tensor(cnt[:, :, :], onehot[:, :, 0, :], onehot[:, :, 1, :], ALU.add))
                link(nc.vector.tensor_tensor(run[:, 1, :], run[:, 0, :], cnt[:, 0, :], ALU.add))
                nc.vector.tensor_copy(runb[:, :, :], run[:, :, :]).then_inc(s["cnt_ok"], 1)
                dve.wait_ge(s["cnt_ok"], b + 1)
                nc.vector.tensor_tensor(run[:, 0, :], run[:, 1, :], cnt[:, 1, :], ALU.add)
                dve.wait_ge(s["rk_ps"], b + 1)
                link(nc.vector.tensor_tensor(rkb[:, :, :], A7[:, 32:32 + 2 * E].rearrange("p (a e) -> p a e", a=2),
                                             route_c[:, 8:16].rearrange("p (o e) -> p o e", o=1).to_broadcast([P, 2, E]), ALU.add))
                for c in range(2):
                    ins = nc.vector.tensor_tensor(prod[:, :, c, :], onehot[:, :, c, :], rkb[:, :, :], ALU.mult)
                link(ins)
                link(nc.vector.tensor_reduce(slotf[:, :, :], prod[:, :, :, :], AX.X, ALU.add))
                nc.vector.tensor_copy(slotu[:, :, :], slotf[:, :, :]).then_inc(s["slot_ok"], 1)
                dve.wait_ge(s["ed_ok"], b + 1)
                link(nc.vector.tensor_scalar(e1[:, :, :], ed[:, :, :], 1.0, None, ALU.add))
                link(nc.vector.reciprocal(XR[:, :, 0, D:D + 1], e1[:, :, :]))
                nc.vector.tensor_tensor(XR[:, :, 1, D:D + 1], XR[:, :, 0, D:D + 1], ed[:, :, :], ALU.mult)
                link(nc.vector.tensor_copy(XR[:, :, :, D + 1:D + 2], dest[:, :, :].rearrange("p a (c o) -> p a c o", o=1)))
                nc.vector.tensor_scalar(dest[:, :, :], dest[:, :, :], float(2 * S), None, ALU.add).then_inc(s["row_ok"], 1)
                dve.wait_ge(s["row_ok"], b + 1)

            RB = 16

            def first():
                norm1(0, 0)
                norm1_apply(0, 0)
                x_low(0)
                rot(0)
                qa_evac(0)
                maxima(0)
                m_rows(0)
                norm1(1, 1)
                norm1_apply(1, 1)
                w_low(0, 0)

            def step(b, par):
                link = Chain(dve, s["bch"], (b - 1) * RB, s["cmem"])
                x_low(b)
                rot(b)
                o_norm(b - 1, link)
                qa_evac(b)
                o_low(b - 1)
                maxima(b)
                m_rows(b)
                residual(b - 1, 1 - par, link)
                more = not (isinstance(b, int) and b == NB - 1)
                if more:
                    norm1(b + 1, 1 - par)
                norm2_apply(b - 1)
                if more:
                    norm1_apply(b + 1, 1 - par)
                routing(b - 1, link)
                assert link.n == RB, link.n
                w_low(b, par)

            def last():
                b = NB - 1
                link = Chain(dve, s["bch"], b * RB, s["cmem"])
                o_norm(b, link)
                o_low(b)
                residual(b, 1, link)
                norm2_apply(b)
                routing(b, link)

            loop(dve, step, first, last)
            nc.vector.tensor_copy(a["total"][:, :], run[:, 0, :]).then_inc(s["actm"], 1)

        @block.tensor
        def _(pe):
            pe.wait_ge(s["const_in"], 16 * (len(CONSTS) + 1))
            pe.wait_ge(s["wcv"], 4)
            pe.wait_ge(s["cmem"], 2)
            mm = nc.tensor.matmul

            def three(out, xh_, xl_, wh_, wl_, start, stop):
                mm(out, xh_, wh_, start=start, stop=False)
                mm(out, xh_, wl_, start=False, stop=False)
                return mm(out, xl_, wh_, start=False, stop=stop)

            def x_t(b):
                pe.wait_ge(s["xn_ok"], b + 1)
                if not (isinstance(b, int) and b == 0):
                    pe.wait_ge(s["mt_ok"], 2 * b)
                for k in range(KD):
                    for half in range(2):
                        ins = nc.tensor.transpose(A6[:, k * 2 * P + half * P:k * 2 * P + half * P + P],
                                                  xn[:, half, k * P:(k + 1) * P], ident[:, :])
                ins.then_inc(s["xT_ps"], 1)

            def qkv(b):
                pe.wait_ge(s["xl_ok"], b + 1)
                if not (isinstance(b, int) and b == 0):
                    pe.wait_ge(s["qa_ev"], 4 * b)
                for half in range(2):
                    for k in range(KD):
                        t = slice(half * P, half * P + P)
                        ins = three(AQ[:, half, :], xh[:, k, t], xl[:, k, t], wq_h[:, k, 0:2 * D], wq_l[:, k, 0:2 * D],
                                    k == 0, k == KD - 1)
                ins.then_inc(s["qk_ps"], 1)
                for half in range(2):
                    for k in range(KD):
                        t = slice(half * P, half * P + P)
                        ins = three(A6[:, half * D:(half + 1) * D], xh[:, k, t], xl[:, k, t],
                                    wq_h[:, k, 2 * D:3 * D], wq_l[:, k, 2 * D:3 * D], k == 0, k == KD - 1)
                ins.then_inc(s["v_ps"], 1)

            def qa_t(b):
                pe.wait_ge(s["lo_ok"], 2 * b + 2)
                pe.wait_ge(s["rt_ok"], 3 * b + 3)
                for u in range(4):
                    if u >= 2:
                        pe.wait_ge(s["qa_ev"], 4 * b + 2)
                    q, j0 = u // 2, 4 * (u % 2)
                    out = AQ[:, u % 2, :].bitcast(F16)
                    for j in range(4):
                        for half, n in ((0, P), (1, TAIL)):
                            src = blk[0:n, half, q, 2 * (j0 + j):2 * (j0 + j) + 2, :].rearrange("p h d -> p (h d)")
                            ins = nc.tensor.transpose(out[:, j * SR + half * P:j * SR + half * P + n], src, ident_h[0:n, 0:n])
                    ins.then_inc(s["qa_ps"], 1)

            def scores(b):
                pe.wait_ge(s["qa_ev"], 4 * b + 4)
                u = 0
                for r in range(2):
                    for par in range(2):
                        u += 1
                        wait_bank(b, u)
                        mm(AS[par][:, :], ident_b[:, :], mask_m[:, :, :].rearrange("p j t -> p (j t)"), start=True, stop=False,
                           skip_group_check=True)
                        rows = slice(64 * par, 64 * par + 64)
                        for j in range(4):
                            ins = mm(AS[par][:, j * P:(j + 1) * P], QA[rows, 4 * r + j, 0:P], KA[rows, 4 * r + j, 0:P],
                                     start=False, stop=(j == 3), skip_group_check=True)
                        ins.then_inc(s["s_ps"], 1)
                for a0, n, gap in TAIL_UNITS:
                    for par in range(2):
                        u += 1
                        wait_bank(b, u)
                        mm(AS[par][:, 0:n * S], ident_b[:, :], mask_t[:, 0:n, :].rearrange("p j t -> p (j t)"),
                           start=True, stop=False, skip_group_check=True)
                        rows = slice(64 * par, 64 * par + 64)
                        for g in range(2):
                            for j in range(n):
                                jj = a0 + g * gap + j
                                ins = mm(AS[par][64 * g:64 * g + TAIL, j * S:(j + 1) * S], QA[rows, jj, P:S], KA[rows, jj, 0:S],
                                         start=False, stop=True, skip_group_check=True)
                        ins.then_inc(s["s_ps"], 1)

            def wait_bank(b, u):
                if isinstance(b, int) and b == 0 and u <= 2:
                    return
                pe.wait_ge(s["s_max"], 8 * b + (u - 2))

            def m_t(b):
                pe.wait_ge(s["s_max"], 8 * b + 8)
                pe.wait_ge(s["v_ok"], 2 * b + 2)
                nc.tensor.transpose(A6[0:2 * PAIRS, 0:P], mx_m[:, :, :].rearrange("p a j -> p (a j)"), ident[:, :])
                nc.tensor.transpose(A6[0:8, P:2 * P], mx_t[:, :, :].rearrange("p a j -> p (a j)"), ident[:, :]).then_inc(s["mt_ps"], 1)

            def scores_t(b):
                if not (isinstance(b, int) and b == 0):
                    pe.wait_ge(s["on_ok"], 2 * b)
                wait_apart(pe, s["mrow"], 160 * b + 160, s["cmem"])
                u = 0
                for a0, n in ST_UNITS:
                    for par in range(2):
                        u += 1
                        if u > 2:
                            wait_apart(pe, s["exp_ok"], 8 * b + u - 2, s["cmem"])
                        rows = slice(64 * par, 64 * par + 64)
                        for j in range(n):
                            ins = mm(AT[par][:, j * S:(j + 1) * S], KA[rows, a0 + j, 0:P], QA[rows, a0 + j, 0:S],
                                     start=True, stop=True, skip_group_check=True)
                        ins.then_inc(s["st_ps"], 1)
                for par in range(2):
                    u += 1
                    wait_apart(pe, s["exp_ok"], 8 * b + u - 2, s["cmem"])
                    rows = slice(64 * par, 64 * par + 64)
                    for j in range(PAIRS):
                        ins = mm(AT[par][0:TAIL, j * TAIL:(j + 1) * TAIL], KA[rows, j, P:S], QA[rows, j, P:S],
                                 start=True, stop=True, skip_group_check=True)
                    ins.then_inc(s["st_ps"], 1)

            def values(b, par):
                pe.wait_ge(s["sel_ok"], 7 * b + 7)
                pe.wait_ge(s["v_ok"], 2 * b + 2)
                pe.wait_ge(s["exp_ok"], 8 * b + 8)
                w = DK + 1
                for h in range(NH):
                    mm(AT[0][:, h * w:(h + 1) * w], PT[:, h % 2, h // 2, 0:P], V[:, par, 0, h, :], start=True, stop=True,
                       skip_group_check=True)
                for h in range(NH):
                    mm(AT[1][0:TAIL, h * w:(h + 1) * w], PT[:, h % 2, h // 2, P:S], V[:, par, 0, h, :], start=True, stop=False,
                       skip_group_check=True)
                    ins = mm(AT[1][0:TAIL, h * w:(h + 1) * w], PTt[0:TAIL, h % 2, h // 2, :], V[0:TAIL, par, 1, h, :],
                             start=False, stop=True, skip_group_check=True)
                ins.then_inc(s["pv_ps"], 1)

            def o_t(b):
                pe.wait_ge(s["on_ok"], 2 * b + 2)
                if not (isinstance(b, int) and b == 0):
                    pe.wait_ge(s["slot_ok"], b)
                for k in range(KD):
                    for half in range(2):
                        ins = nc.tensor.transpose(A7[:, k * 2 * P + half * P:k * 2 * P + half * P + P],
                                                  On[:, half, k * P:(k + 1) * P], ident[:, :])
                ins.then_inc(s["ot_ps"], 1)

            def project(b):
                pe.wait_ge(s["ol_ok"], b + 1)
                for half in range(2):
                    for k in range(KD):
                        t = slice(half * P, half * P + P)
                        ins = three(A7[:, half * D:(half + 1) * D], oh[:, k, t], ol[:, k, t], wo_h[:, k, :], wo_l[:, k, :],
                                    k == 0, k == KD - 1)
                ins.then_inc(s["pj_ps"], 1)

            def x2_t(b):
                pe.wait_ge(s["x2_ok"], b + 1)
                for k in range(KD):
                    for half in range(2):
                        ins = nc.tensor.transpose(A7[:, k * 2 * P + half * P:k * 2 * P + half * P + P],
                                                  XR[:, half, 0, k * P:(k + 1) * P], ident[:, :])
                ins.then_inc(s["x2t_ps"], 1)

            def logits(b):
                pe.wait_ge(s["x2t_ok"], b + 1)
                for half in range(2):
                    for k in range(KD):
                        ins = mm(A7[:, half * E:(half + 1) * E], x2T[:, k, half * P:(half + 1) * P], rw[:, k, :],
                                 start=(k == 0), stop=(k == KD - 1))
                ins.then_inc(s["lg_ps"], 1)

            def ranks(b):
                pe.wait_ge(s["cnt_ok"], b + 1)
                for half in range(2):
                    out = A7[:, 32 + half * E:32 + (half + 1) * E]
                    mm(out, upper[:, :], cnt[:, half, :], start=True, stop=False)
                    ins = mm(out, ones_b[:, :], runb[:, half, :], start=False, stop=True)
                ins.then_inc(s["rk_ps"], 1)

            def first():
                x_t(0)
                qkv(0)
                qa_t(0)
                scores(0)
                m_t(0)

            def step(b, par):
                x_t(b)
                scores_t(b - 1)
                qkv(b)
                values(b - 1, 1 - par)
                qa_t(b)
                o_t(b - 1)
                scores(b)
                m_t(b)
                project(b - 1)
                x2_t(b - 1)
                logits(b - 1)
                ranks(b - 1)

            def last():
                b = NB - 1
                scores_t(b)
                values(b, 1)
                o_t(b)
                project(b)
                x2_t(b)
                logits(b)
                ranks(b)

            loop(pe, step, first, last)


def stage_experts(nc, a, wts):
    W1H, W1L, W2H, W2L = wts
    with ExitStack() as ctx:
        sb = lambda n, s, d: ctx.enter_context(nc.sbuf_tensor(n, s, d))
        sem = lambda n: ctx.enter_context(nc.semaphore(n))
        ident = sb("ident2", [P, P], F32)
        ones = sb("ones2", [P, P], F32)
        gam = sb("gam", [P, E, D], F32)
        bet = sb("bet", [P, E, D], F32)
        b2s = sb("b2s", [P, E, D], F32)
        b1s = sb("b1s", [P, E * KF], F32)
        pad = sb("pad", [P, XROW], F32)
        tc_ = sb("tc_", [1, TILES * E + E], F32)
        ctot = sb("ctot", [P, E], F32)
        ni = sb("ni", [1, 2, E], I32)
        ntf = sb("ntf", [1, E], F32)
        cum = sb("cum", [1, E], F32)
        gap = sb("gap", [1, E], F32)
        ge = sb("ge", [1, TILES, E], F32)
        gp = sb("gp", [1, TILES, E], F32)
        tf = sb("tf", [1, 3, TILES], F32)
        zf = sb("zf", [1, E], F32)
        table = sb("table", [1, 2 * TILES + E], I32)
        X = sb("X", [P, 2, XROW], F32)
        xh = sb("xh2", [P, KD, P], F16)
        xl = sb("xl2", [P, KD, P], F16)
        hf = sb("hf", [P, 2, KF, P], F32)
        hh = sb("hh", [P, KF, P], F16)
        hl = sb("hl", [P, KF, P], F16)
        xb = sb("xb", [P, D], F32)
        r = sb("r", [P, D], F32)
        st = sb("st", [P, 6], F32)
        mv = sb("mv", [P, 2], F32)
        rs = sb("rs", [P, 1], F32)
        rg = sb("rg", [P, 1], F32)
        ve = sb("ve", [P, 1], F32)
        mhalf = sb("mhalf2", [P, 1], F32)
        nrm = sb("nrm", [P, D], F32)
        y1 = sb("y1", [P, D], F32)
        y = sb("y", [P, 2, D], F32)
        du = sb("du", [P, 2, 1], U32)
        XT = [ctx.enter_context(nc.psum_tensor(f"XT{i}", [P, 512], F32)) for i in range(2)]
        HP = [ctx.enter_context(nc.psum_tensor(f"HP{i}", [P, 4, P], F32)) for i in range(4)]
        OP = [ctx.enter_context(nc.psum_tensor(f"OP{i}", [P, 512], F32)) for i in range(2)]
        names = ("ve_ok rs_ok half_ok c_in tab tot_ps pad_ok pads x_in0 x_in1 xt_ps xh_ok xl_ok h_ps h_ok hh_ok hl_ok o_ps xb_ok r_ok "
                 "dch nrm_ok y1_ok y_ok y_out0 y_out1 x_used").split()
        s = {n: sem(n) for n in names}
        x_in = [s["x_in0"], s["x_in1"]]
        y_out = [s["y_out0"], s["y_out1"]]
        block = ctx.enter_context(nc.Block())

        def tiles(eng, one):
            one(0, 0)
            one(1, 1)
            with eng.Fori(1, TILES // 2) as g:
                one(g * 2, 0)
                one(g * 2 + 1, 1)
            if TILES % 2:
                one(TILES - 1, 0)

        def early(t, n):
            return isinstance(t, int) and t < n

        def expert_of(eng, t, per):
            e = eng.value_load(table[0:1, bass.ds(t, 1)], min_val=0, max_val=E - 1)
            return e

        @block.sync
        def _(sp):
            sp.dma_start(ident[:, :], a["ident"]).then_inc(s["c_in"], 16)
            sp.dma_start(pad[:, :], a["pad"]).then_inc(s["c_in"], 16)
            sp.dma_start(tc_[:, :], a["tile_c"]).then_inc(s["c_in"], 16)
            sp.dma_start(b1s[:, :], a["b1_t"]).then_inc(s["c_in"], 16)
            for dst, n in ((gam, "gamma"), (bet, "beta"), (b2s, "b2")):
                sp.dma_start(dst[:, :, :].rearrange("p e d -> p (e d)"),
                             a[n].rearrange("(o e) d -> o (e d)", o=1).to_broadcast([P, E * D])).then_inc(s["c_in"], 16)
            sp.wait_ge(s["tab"], 1)
            sp.wait_ge(s["c_in"], 16 * 7)
            for e in range(E):
                z = sp.value_load(table[0:1, 2 * TILES + e:2 * TILES + e + 1], min_val=0, max_val=E * REG - P)
                sp.dma_start(a["slots"][bass.ds(z, P), :], pad[:, :]).then_inc(s["pads"], 16)
            sp.dma_start(a["slots"][E * REG:E * REG + P, :], pad[:, :]).then_inc(s["pads"], 16)
            sp.wait_ge(s["pads"], 16 * (E + 1))

            def one(t, par):
                if not early(t, 2):
                    sp.wait_ge(s["x_used"], t - 1)
                row = sp.value_load(table[0:1, bass.ds(t + TILES, 1)], min_val=0, max_val=E * REG)
                sp.dma_start(X[:, par, :], a["slots"][bass.ds(row, P), :]).then_inc(x_in[par], 16)
            tiles(sp, one)

        def x_arrived(eng, t, par):
            eng.wait_ge(x_in[par], 16 * (t // 2 + 1) if isinstance(t, int) else (t + (2 - par)) * 8)

        @block.tensor
        def _(pe):
            mm = nc.tensor.matmul
            pe.wait_ge(s["c_in"], 16 * 7)
            pe.wait_ge(s["pad_ok"], 1)
            mm(XT[0][:, 0:E], ones[:, :], a["total"][:, :], start=True, stop=True).then_inc(s["tot_ps"], 1)
            pe.wait_ge(s["tab"], 1)

            def turn(t, par):
                x_arrived(pe, t, par)
                if not early(t, 2):
                    pe.wait_ge(s["xl_ok"], t - 1)
                for k in range(KD):
                    ins = nc.tensor.transpose(XT[par][:, k * P:(k + 1) * P], X[:, par, k * P:(k + 1) * P], ident[:, :])
                ins.then_inc(s["xt_ps"], 1)

            def up(t, par):
                e = expert_of(pe, t, 0)
                pe.wait_ge(s["xl_ok"], t + 1)
                for hb in range(2):
                    if not early(t, 2):
                        pe.wait_ge(s["h_ok"], (t - 2) * 2 + hb + 1)
                    for f in range(4):
                        for k in range(KD):
                            off = k * FF + (hb * 4 + f) * P
                            wh = W1H[:, :, :].rearrange("p a f -> p (a f)")[:, bass.ds(e * (KD * FF) + off, P)]
                            wl = W1L[:, :, :].rearrange("p a f -> p (a f)")[:, bass.ds(e * (KD * FF) + off, P)]
                            out = HP[par * 2 + hb][:, f, :]
                            mm(out, wh, xh[:, k, :], start=(k == 0), stop=False)
                            mm(out, wh, xl[:, k, :], start=False, stop=False)
                            ins = mm(out, wl, xh[:, k, :], start=False, stop=(k == KD - 1))
                    ins.then_inc(s["h_ps"], 1)

            def down(t, par):
                e = expert_of(pe, t, 0)
                if not early(t, 2):
                    pe.wait_ge(s["r_ok"], t - 1)
                pe.wait_ge(s["hl_ok"], 2 * t + 2)
                for f in range(KF):
                    wh = W2H[:, :, :].rearrange("p a f -> p (a f)")[:, bass.ds(e * (KF * D) + f * D, D)]
                    wl = W2L[:, :, :].rearrange("p a f -> p (a f)")[:, bass.ds(e * (KF * D) + f * D, D)]
                    mm(OP[par][:, 0:D], hh[:, f, :], wh, start=(f == 0), stop=False)
                    mm(OP[par][:, 0:D], hh[:, f, :], wl, start=False, stop=False)
                    ins = mm(OP[par][:, 0:D], hl[:, f, :], wh, start=False, stop=(f == KF - 1))
                ins.then_inc(s["o_ps"], 1)

            turn(0, 0)
            up(0, 0)
            turn(1, 1)
            up(1, 1)
            down(0, 0)
            with pe.Fori(1, TILES // 2) as g:
                turn(g * 2, 0)
                up(g * 2, 0)
                down(g * 2 - 1, 1)
                turn(g * 2 + 1, 1)
                up(g * 2 + 1, 1)
                down(g * 2, 0)
            t = TILES // 2 * 2
            turn(t, 0)
            up(t, 0)
            down(t - 1, 1)
            down(t, 0)

        @block.scalar
        def _(act):
            act.wait_ge(s["tab"], 1)
            act.wait_ge(s["c_in"], 16 * 7)

            def one(t, par):
                act.wait_ge(s["xt_ps"], t + 1)
                if not early(t, 1):
                    act.wait_ge(s["h_ps"], 2 * t)
                nc.scalar.activation(xh[:, :, :], XT[par][:, 0:D].rearrange("p (k t) -> p k t", k=KD), ACT.Copy).then_inc(s["xh_ok"], 1)
                e = expert_of(act, t, 0)
                for hb in range(2):
                    act.wait_ge(s["h_ps"], 2 * t + hb + 1)
                    if not early(t, 2):
                        act.wait_ge(s["hl_ok"], (t - 2) * 2 + hb + 1)
                    for f in range(4):
                        ins = nc.scalar.activation(hf[:, par, hb * 4 + f, :], HP[par * 2 + hb][:, f, :], ACT.Gelu,
                                                   bias=b1s[:, bass.ds(e * KF + (hb * 4 + f), 1)], scale=1.0 / WSCALE)
                    ins.then_inc(s["h_ok"], 1)
            tiles(act, one)

        @block.vector
        def _(dve):
            link = Chain(dve, s["dch"], 0)
            nc.vector.memset(ones[:, :], 1.0).then_inc(s["pad_ok"], 1)
            dve.wait_ge(s["c_in"], 16 * 7)
            dve.wait_ge(s["tot_ps"], 1)
            link(nc.vector.tensor_copy(ctot[:, :], XT[0][:, 0:E]))
            link(nc.vector.tensor_scalar(ntf[:, :], ctot[0:1, :], float(P - 1), None, ALU.add))
            link(nc.vector.tensor_copy(ni[:, 0, :], ntf[:, :]))
            link(nc.vector.tensor_single_scalar(ni[:, 1, :], ni[:, 0, :], 7, ALU.arith_shift_right))
            link(nc.vector.tensor_copy(ntf[:, :], ni[:, 1, :]))
            link(nc.vector.tensor_copy(cum[:, 0:1], ntf[:, 0:1]))
            for e in range(1, E):
                link(nc.vector.tensor_tensor(cum[:, e:e + 1], cum[:, e - 1:e], ntf[:, e:e + 1], ALU.add))
            link(nc.vector.tensor_scalar(gap[:, :], ntf[:, :], -float(P), float(REG), ALU.mult, ALU.add))
            tn = tc_[:, 0:TILES * E].rearrange("o (t e) -> o t e", e=E)
            link(nc.vector.tensor_tensor(ge[:, :, :], tn, cum[:, :].rearrange("o (a e) -> o a e", a=1).to_broadcast([1, TILES, E]),
                                         ALU.is_ge))
            link(nc.vector.tensor_tensor(gp[:, :, :], ge[:, :, :],
                                         gap[:, :].rearrange("o (a e) -> o a e", a=1).to_broadcast([1, TILES, E]), ALU.mult))
            link(nc.vector.tensor_reduce(tf[:, 0, :], ge[:, :, :], AX.X, ALU.add))
            link(nc.vector.tensor_reduce(tf[:, 1, :], gp[:, :, :], AX.X, ALU.add))
            link(nc.vector.scalar_tensor_tensor(out=tf[:, 1, :], in0=tn[:, :, 0], scalar=float(P), in1=tf[:, 1, :],
                                                op0=ALU.mult, op1=ALU.add))
            link(nc.vector.tensor_scalar(tf[:, 2, :], tf[:, 0, :], float(E) - 0.5, None, ALU.is_lt))
            for j in range(2):
                ins = nc.vector.tensor_tensor(tf[:, j, :], tf[:, j, :], tf[:, 2, :], ALU.mult)
            link(ins)
            link(nc.vector.tensor_scalar(tf[:, 2, :], tf[:, 2, :], -float(E * REG), float(E * REG), ALU.mult, ALU.add))
            link(nc.vector.tensor_tensor(tf[:, 1, :], tf[:, 1, :], tf[:, 2, :], ALU.add))
            link(nc.vector.tensor_tensor(zf[:, :], ctot[0:1, :], tc_[:, TILES * E:], ALU.add))
            nc.vector.tensor_copy(table[:, 0:2 * TILES], tf[:, 0:2, :].rearrange("o a t -> o (a t)"))
            nc.vector.tensor_copy(table[:, 2 * TILES:], zf[:, :]).then_inc(s["tab"], 1)
            base = link.n
            dve.wait_ge(s["tab"], 1)

            def split(t, par):
                dve.wait_ge(s["xh_ok"], t + 1)
                nc.vector.tensor_tensor(xl[:, :, :], XT[par][:, 0:D].rearrange("p (k t) -> p k t", k=KD), xh[:, :, :],
                                        ALU.subtract).then_inc(s["xl_ok"], 1)

            def split_h(t, par):
                if not early(t, 1):
                    dve.wait_ge(s["o_ps"], t)
                for hb in range(2):
                    dve.wait_ge(s["h_ok"], 2 * t + hb + 1)
                    f = slice(4 * hb, 4 * hb + 4)
                    nc.vector.tensor_copy(hh[:, f, :], hf[:, par, f, :]).then_inc(s["hh_ok"], 1)
                    dve.wait_ge(s["hh_ok"], 2 * t + hb + 1)
                    nc.vector.tensor_tensor(hl[:, f, :], hf[:, par, f, :], hh[:, f, :], ALU.subtract).then_inc(s["hl_ok"], 1)

            CH = 3

            def finish(t, par):
                ch = Chain(dve, s["dch"], base + t * CH, s["tab"])
                dve.wait_ge(s["o_ps"], t + 1)
                dve.wait_ge(s["xb_ok"], t + 1)
                nc.vector.scalar_tensor_tensor(out=r[:, :], in0=OP[par][:, 0:D], scalar=1.0 / WSCALE, in1=xb[:, :],
                                               op0=ALU.mult, op1=ALU.add).then_inc(s["r_ok"], 1)
                dve.wait_ge(s["r_ok"], t + 1)
                ch(nc.vector.bn_stats(st[:, :], r[:, :]), alone=True)
                ch(nc.vector.bn_aggr(mv[:, :], st[:, :]))
                nc.vector.tensor_scalar(ve[:, :], mv[:, 1:2], MOE_EPS, None, ALU.add).then_inc(s["ve_ok"], 1)
                dve.wait_ge(s["rs_ok"], t + 1)
                ch(nc.vector.tensor_tensor(rg[:, :], rs[:, :], X[:, par, D:D + 1], ALU.mult))
                if not early(t, 1):
                    dve.wait_ge(s["y1_ok"], t)
                nc.vector.tensor_scalar(nrm[:, :], r[:, :], mv[:, 0:1], rg[:, :], ALU.subtract, ALU.mult).then_inc(s["nrm_ok"], 1)
                if not early(t, 2):
                    dve.wait_ge(y_out[par], 16 * (t // 2) if isinstance(t, int) else (t - par) * 8)
                e = expert_of(dve, t, 0)
                nc.vector.tensor_copy(du[:, par, :], X[:, par, D + 1:D + 2])
                dve.wait_ge(s["y1_ok"], t + 1)
                nc.vector.scalar_tensor_tensor(out=y[:, par, :], in0=bet[:, :, :].rearrange("p e d -> p (e d)")[:, bass.ds(e * D, D)],
                                               scalar=X[:, par, D:D + 1], in1=y1[:, :], op0=ALU.mult, op1=ALU.add).then_inc(s["y_ok"], 1)

            split(0, 0)
            split_h(0, 0)
            split(1, 1)
            with dve.Fori(1, TILES // 2) as g:
                split_h(g * 2 - 1, 1)
                finish(g * 2 - 2, 0)
                split(g * 2, 0)
                split_h(g * 2, 0)
                finish(g * 2 - 1, 1)
                split(g * 2 + 1, 1)
            t = TILES // 2 * 2
            split_h(t - 1, 1)
            finish(t - 2, 0)
            split(t, 0)
            split_h(t, 0)
            finish(t - 1, 1)
            finish(t, 0)

        @block.gpsimd
        def _(pool):
            nc.gpsimd.memset(mhalf[:, :], -0.5).then_inc(s["half_ok"], 1)
            pool.wait_ge(s["half_ok"], 1)
            pool.wait_ge(s["tab"], 1)
            pool.wait_ge(s["c_in"], 16 * 7)

            def one(t, par):
                e = expert_of(pool, t, 0)
                x_arrived(pool, t, par)
                if not early(t, 1):
                    pool.wait_ge(s["r_ok"], t)
                nc.gpsimd.tensor_tensor(xb[:, :], X[:, par, 0:D], b2s[:, :, :].rearrange("p e d -> p (e d)")[:, bass.ds(e * D, D)],
                                        ALU.add).then_inc(s["xb_ok"], 1)
                pool.wait_ge(s["ve_ok"], t + 1)
                nc.gpsimd.tensor_tensor(rs[:, :], ve[:, :], mhalf[:, :], ALU.pow).then_inc(s["rs_ok"], 1)
                pool.wait_ge(s["nrm_ok"], t + 1)
                if not early(t, 1):
                    pool.wait_ge(s["y_ok"], t)
                nc.gpsimd.tensor_tensor(y1[:, :], nrm[:, :], gam[:, :, :].rearrange("p e d -> p (e d)")[:, bass.ds(e * D, D)],
                                        ALU.mult).then_inc(s["y1_ok"], 1)
                wait_apart(pool, s["y_ok"], t + 1, s["tab"])
                nc.gpsimd.indirect_dma_start(
                    out=a["y_rows"], out_offset=bass.IndirectOffsetOnAxis(ap=du[:, par, :], axis=0),
                    in_=y[:, par, :], in_offset=None, bounds_check=2 * N - 1, oob_is_err=False,
                    engine_sem=s["x_used"]).then_inc(y_out[par], 16)
            tiles(pool, one)
            pool.wait_ge(y_out[0], 16 * ((TILES + 1) // 2))
            pool.wait_ge(y_out[1], 16 * (TILES // 2))


def stage_combine(nc, a):
    PR = 120
    ROWS = N // PR
    NCH = 11
    RC = ROWS // NCH
    with ExitStack() as ctx:
        sb = lambda n, s, d: ctx.enter_context(nc.sbuf_tensor(n, s, d))
        sem = lambda n: ctx.enter_context(nc.semaphore(n))
        h = sb("hc", [PR, ROWS, D], F32)
        y = sb("yc", [PR, ROWS, 2, D], F32)
        s_in = [sem(f"c_in{i}") for i in range(NCH)]
        sum_ok = sem("sum_ok")
        half_ok = sem("half_ok")
        out_done = sem("out_done")
        block = ctx.enter_context(nc.Block())
        hv = a["h2_rows"].rearrange("(p r) d -> p r d", p=PR)
        yv = a["y_rows"].rearrange("(p r c) d -> p r c d", p=PR, c=2)
        ov = a["out"].rearrange("b s d -> (b s) d").rearrange("(p r) d -> p r d", p=PR)

        @block.sync
        def _(sp):
            for i in range(NCH):
                r = slice(i * RC, (i + 1) * RC)
                sp.dma_start(y[:, r], yv[:, r]).then_inc(s_in[i], 16)
                sp.dma_start(h[:, r, :], hv[:, r, :]).then_inc(s_in[i], 16)

        @block.vector
        def _(dve):
            for i in range(NCH):
                r = slice(i * RC, (i + 1) * RC)
                dve.wait_ge(s_in[i], 32)
                nc.vector.tensor_tensor(h[:, r, :], h[:, r, :], y[:, r, 0, :], ALU.add).then_inc(half_ok, 1)
                dve.wait_ge(half_ok, i + 1)
                nc.vector.tensor_tensor(h[:, r, :], h[:, r, :], y[:, r, 1, :], ALU.add).then_inc(sum_ok, 1)

        @block.scalar
        def _(act):
            for i in range(NCH):
                r = slice(i * RC, (i + 1) * RC)
                act.wait_ge(sum_ok, i + 1)
                act.dma_start(ov[:, r, :], h[:, r, :]).then_inc(out_done, 16)
            act.wait_ge(out_done, 16 * NCH)


def build(nc, a):
    with ExitStack() as ctx:
        a["total"] = ctx.enter_context(nc.sbuf_tensor("total", [P, E], F32))
        stage_patches(nc, a["patch_t"], a["tok_w"], a["tok_b"], a["pe_rows"])
        with ExitStack() as w:
            sb = lambda n, s: w.enter_context(nc.sbuf_tensor(n, s, F16))
            wts = (sb("W1H", [P, E * KD, FF]), sb("W1L", [P, E * KD, FF]),
                   sb("W2H", [P, E * KF, D]), sb("W2L", [P, E * KF, D]))
            stage_attention(nc, a, wts)
            stage_experts(nc, a, wts)
        stage_combine(nc, a)


def constants():
    def bf16_bits(v):
        return (np.ascontiguousarray(v, dtype=np.float32).view(np.uint32) >> 16).astype(np.uint16)

    c = {}
    c["ident"] = np.eye(P, dtype=np.float32)
    c["ident_h"] = np.eye(P, dtype=np.float16)
    c["ident_b"] = bf16_bits(np.eye(P))
    q = np.arange(P)
    m = np.where(q[None, :] > q[:, None], np.float32(NEG), np.float32(0))
    c["mask_m"] = bf16_bits(np.repeat(m[:, None, :], 4, axis=1))
    mt = np.zeros((P, S), np.float32)
    for g in (0, 64):
        for i in range(TAIL):
            mt[g + i, P + i + 1:] = NEG
    c["mask_t"] = bf16_bits(np.repeat(mt[:, None, :], 3, axis=1))
    inv = (np.float32(10000.0) ** (np.arange(0, DK, 2, dtype=np.float32) / np.float32(DK))).astype(np.float32)
    ang = (np.arange(S, dtype=np.float32)[:, None] / inv[None, :]).astype(np.float32)
    cos, sin = np.cos(ang).astype(np.float32), np.sin(ang).astype(np.float32)
    ct = np.zeros((P, 2, DK // 2, 2), np.float32)
    st = np.zeros_like(ct)
    for half, n in ((0, P), (1, TAIL)):
        cc, ss = cos[half * P:half * P + n], sin[half * P:half * P + n]
        ct[:n, half] = cc[:, :, None]
        st[:n, half, :, 0] = -ss
        st[:n, half, :, 1] = ss
    c["cosT"] = (ct / np.float32(WSCALE)).reshape(P, 2, DK)
    c["sinT"] = (st / np.float32(WSCALE)).reshape(P, 2, DK)
    c["upper"] = bf16_bits(np.triu(np.ones((P, P), np.float32), 1))
    c["ones_b"] = bf16_bits(np.ones((P, P)))
    r = np.zeros((P, 24), np.float32)
    r[:, 0:E] = np.arange(E)
    r[:, 8:16] = np.arange(E) * REG
    r[TAIL:, 17] = 100.0
    for half in range(2):
        for k in range(2):
            r[:, 18 + 2 * half + k] = 2 * (half * P + q) + k
    c["route_c"] = r
    pad = np.zeros((P, XROW), np.float32)
    pad[:, D + 1] = 1.0e6
    c["pad"] = pad
    t = np.zeros((1, TILES * E + E), np.float32)
    t[0, :TILES * E] = np.repeat(np.arange(TILES), E)
    t[0, TILES * E:] = np.arange(E) * REG
    c["tile_c"] = t
    return c


def kernel(**inputs):
    import numpy as _np
    import concourse.bacc as _bacc
    from concourse import mybir as _mybir
    from concourse.bass_utils import run_bass_kernel_spmd as _run

    g = {k: _np.asarray(v) for k, v in inputs.items()}
    x = g["x"].reshape(NB, CH, GRID, PATCH, GRID, PATCH)
    arrays = {
        "patch_t": x.transpose(1, 3, 5, 0, 2, 4).reshape(CH * PATCH * PATCH, NB * NPATCH),
        "txt": g["txt"], "tok_w": g["L0_tok_W"], "tok_b": g["L0_tok_b"], "cls": g["L0_tok_cls_token"],
        "wqkv_t": g["L0_attn_W_qkv"].T, "wo_t": g["L0_attn_W_o"].T, "router": g["L0_ffn_router_w"],
        "w1": g["L0_ffn_w1"], "w2": g["L0_ffn_w2"], "b2": g["L0_ffn_b2"],
        "b1_t": g["L0_ffn_b1"].reshape(E, KF, P).transpose(2, 0, 1).reshape(P, E * KF),
        "gamma": g["L0_ffn_gamma"], "beta": g["L0_ffn_beta"],
    }
    arrays.update(constants())
    arrays = {n: _np.ascontiguousarray(v) for n, v in arrays.items()}
    nc = _bacc.Bacc("TRN2", target_bir_lowering=False, num_devices=1)
    a = {n: nc.dram_tensor("in_" + n, v.shape, _mybir.dt.from_np(v.dtype), kind="ExternalInput").ap() for n, v in arrays.items()}
    a["out"] = nc.dram_tensor("out_0", (NB, S, D), _mybir.dt.float32, kind="ExternalOutput").ap()
    a["pe_rows"] = nc.dram_tensor("pe_rows", (NB * NPATCH, D), _mybir.dt.float32).ap()
    a["h2_rows"] = nc.dram_tensor("h2_rows", (N, D), _mybir.dt.float32).ap()
    a["slots"] = nc.dram_tensor("slots", (E * REG + P, XROW), _mybir.dt.float32).ap()
    a["y_rows"] = nc.dram_tensor("y_rows", (2 * N, D), _mybir.dt.float32).ap()
    build(nc, a)
    r = _run(nc, [{"in_" + n: v for n, v in arrays.items()}], core_ids=[0])
    return r.results[0]["out_0"]
```

```python
from contextlib import ExitStack

import numpy as np
import concourse.bass as bass
from concourse import mybir

F32 = mybir.dt.float32
F16 = mybir.dt.float16
BF16 = mybir.dt.bfloat16
I32 = mybir.dt.int32
U32 = mybir.dt.uint32
ALU = mybir.AluOpType
ACT = mybir.ActivationFunctionType
AX = mybir.AxisListType

P = 128
NB, CH, IMG, PATCH = 16, 3, 96, 16
GRID = IMG // PATCH
NPATCH = GRID * GRID
KP = CH * PATCH * PATCH // P
D = 256
KD = D // P
TXT = 128
S = 1 + NPATCH + TXT
SR = S + 1
TAIL = S - P
HEAD = 1 + NPATCH
NH, DK = 16, 16
PAIRS = NH // 2
E, FF = 8, 1024
KF = FF // P
N = NB * S
REG = N + P
XROW = D + 2
TILES = (2 * N + E * (P - 1)) // P
WSCALE = 64.0
NEG = -1.0e30
LN1_EPS = 1e-5
MOE_EPS = 1e-6
MSCALE = 16.0
TAIL_UNITS = [(0, 3, 3), (6, 1, 1)]
ST_UNITS = [(0, 3), (3, 3), (6, 2)]
SLOT = 64


def wait_apart(eng, sem, value, stood):
    if not isinstance(value, int):
        value = eng.to_reg(value)
    eng.wait_ge(stood, 1)
    eng.wait_ge(sem, value)


class Chain:

    def __init__(self, eng, sem, base, stood=None):
        self.eng, self.sem, self.base, self.stood, self.n = eng, sem, base, stood, 0

    def __call__(self, ins, alone=False):
        self.n += 1
        ins.then_inc(self.sem, 1)
        if alone:
            wait_apart(self.eng, self.sem, self.base + self.n, self.stood)
        else:
            self.eng.wait_ge(self.sem, self.base + self.n)


def stage_patches(nc, patch_t, tok_w, tok_b, pe_rows):
    tiles = [(t * P, min(P, NB * NPATCH - t * P)) for t in range(-(-NB * NPATCH // P))]
    with ExitStack() as ctx:
        sb = lambda n, s, d: ctx.enter_context(nc.sbuf_tensor(n, s, d))
        sem = lambda n: ctx.enter_context(nc.semaphore(n))
        pt = sb("pt", [P, KP, NB * NPATCH], F32)
        pw = sb("pw", [P, KP, D], F32)
        pb = sb("pb", [P, D], F32)
        emb = sb("emb", [P, len(tiles), D], F32)
        acc = [ctx.enter_context(nc.psum_tensor(f"pacc{i}", [P, 512], F32)) for i in range(len(tiles))]
        w_in = sem("w_in")
        x_in = [sem(f"x_in{k}") for k in range(KP)]
        b_in = sem("b_in")
        emb_mm = sem("emb_mm")
        emb_ok = sem("emb_ok")
        pe_out = sem("pe_out")
        block = ctx.enter_context(nc.Block())

        @block.sync
        def _(sp):
            for k in range(KP):
                sp.dma_start(pt[:, k, :], patch_t[k * P:(k + 1) * P, :]).then_inc(x_in[k], 16)
            for t, (r0, n) in enumerate(tiles):
                sp.wait_ge(emb_ok, t + 1)
                sp.dma_start(pe_rows[r0:r0 + n, :], emb[0:n, t, :]).then_inc(pe_out, 16)
            sp.wait_ge(pe_out, 16 * len(tiles))

        @block.scalar
        def _(act):
            act.dma_start(pw[:, :, :], tok_w.rearrange("(k p) d -> p k d", p=P)).then_inc(w_in, 16)
            act.dma_start(pb[:, :], tok_b.rearrange("(a d) -> a d", a=1).to_broadcast([P, D])).then_inc(b_in, 16)

        @block.tensor
        def _(pe):
            pe.wait_ge(w_in, 16)
            for k in range(KP):
                pe.wait_ge(x_in[k], 16)
                for t, (r0, n) in enumerate(tiles):
                    mm = nc.tensor.matmul(acc[t][0:n, 0:D], pt[:, k, r0:r0 + n], pw[:, k, :],
                                          start=(k == 0), stop=(k == KP - 1))
                    if k == KP - 1:
                        mm.then_inc(emb_mm, 1)

        @block.vector
        def _(dve):
            dve.wait_ge(b_in, 16)
            for t, (r0, n) in enumerate(tiles):
                dve.wait_ge(emb_mm, t + 1)
                nc.vector.tensor_tensor(emb[0:n, t, :], acc[t][0:n, 0:D], pb[0:n, :], ALU.add).then_inc(emb_ok, 1)


def stage_attention(nc, a, wts):
    W1H, W1L, W2H, W2L = wts
    with ExitStack() as ctx:
        sb = lambda n, s, d: ctx.enter_context(nc.sbuf_tensor(n, s, d))
        ps = lambda n, s, d=F32: ctx.enter_context(nc.psum_tensor(n, s, d))
        sem = lambda n: ctx.enter_context(nc.semaphore(n))

        ident = sb("ident", [P, P], F32)
        ident_h = sb("ident_h", [P, P], F16)
        ident_b = sb("ident_b", [P, P], BF16)
        mask_m = sb("mask_m", [P, P], BF16)
        mask_t = sb("mask_t", [P, S], BF16)
        cosT = sb("cosT", [P, 2, DK], F32)
        sinT = sb("sinT", [P, 2, DK], F32)
        upper = sb("upper", [P, P], BF16)
        ones_b = sb("ones_b", [P, P], BF16)
        route_c = sb("route_c", [P, 24], F32)
        wq_h = sb("wq_h", [P, KD, 3 * D], F16)
        wq_l = sb("wq_l", [P, KD, 3 * D], F16)
        wo_h = sb("wo_h", [P, KD, D], F16)
        wo_l = sb("wo_l", [P, KD, D], F16)
        rw = sb("rw", [P, KD, E], F32)
        mhalf = sb("mhalf", [P, 2, 1], F32)
        H = sb("H", [P, 2, 2, D], F32)
        st1 = sb("st1", [P, 2, 6], F32)
        mv1 = sb("mv1", [P, 2, 2], F32)
        ve1 = sb("ve1", [P, 2, 1], F32)
        rs1 = sb("rs1", [P, 2, 1], F32)
        xh = sb("xh", [P, KD, 2 * P], F16)
        xl = sb("xl", [P, KD, 2 * P], F16)
        rt1 = sb("rt1", [P, 2, 2 * D], F32)
        rt2 = sb("rt2", [P, 2, 2 * D], F32)
        xn = rt2[:, :, 0:D]
        blk = sb("blk", [P, 2, 2, NH, SLOT], F16)
        V = sb("V", [P, 2, 2, NH, DK + 1], F32)
        QA = sb("QA", [P, 2, PAIRS, SR], F16)
        KA = sb("KA", [P, 2, PAIRS, SR], F16)
        mx_m = sb("mx_m", [P, 2, PAIRS], F32)
        mx_t = sb("mx_t", [P, 2, 4], F32)
        mT_m = sb("mT_m", [2 * PAIRS, P], F16)
        mT_t = sb("mT_t", [8, P], F16)
        PT = sb("PT", [P, 2, PAIRS, S], F32)
        PTt = sb("PTt", [P, 2, PAIRS, TAIL], F32)
        rec = sb("rec", [P, 2, NH], F32)
        On = sb("On", [P, 2, D], F32)
        ohl = sb("ohl", [P, 2, KD, 2 * P], F16)
        oh, ol = ohl[:, 0], ohl[:, 1]
        x2T = ohl[:, :, :, :].rearrange("p a k t -> p (a k t)").bitcast(F32).rearrange("p (k t) -> p k t", k=KD)
        HR = sb("HR", [P, 2, D], F32)
        st2 = sb("st2", [P, 2, 6], F32)
        mv2 = sb("mv2", [P, 2, 2], F32)
        ve2 = sb("ve2", [P, 2, 1], F32)
        rs2 = sb("rs2", [P, 2, 1], F32)
        XR = sb("XR", [P, 2, 2, XROW], F32)
        lg = sb("lg", [P, 2, E], F32)
        m8 = sb("m8", [P, 2, 8], F32)
        i8 = sb("i8", [P, 2, 8], U32)
        idf = sb("idf", [P, 2, 2], F32)
        df = sb("df", [P, 2, 1], F32)
        ed = sb("ed", [P, 2, 1], F32)
        e1 = sb("e1", [P, 2, 1], F32)
        onehot = sb("onehot", [P, 2, 2, E], F32)
        cnt = sb("cnt", [P, 2, E], BF16)
        run = sb("run", [P, 2, E], F32)
        runb = sb("runb", [P, 2, E], BF16)
        rkb = sb("rkb", [P, 2, E], F32)
        prod = sb("prod", [P, 2, 2, E], F32)
        slotf = sb("slotf", [P, 2, 2], F32)
        slotu = sb("slotu", [P, 2, 2], U32)
        dest = sb("dest", [P, 2, 2], F32)
        stg = sb("stg", [P, 2, FF], F32)
        small = PT[:, :, :, :].rearrange("p a j t -> p (a j t)")
        wq32 = small[:, 0:3 * D * KD].rearrange("p (k f) -> p k f", k=KD)
        wo32 = small[:, 3 * D * KD:(3 * D + D // 1) * KD].rearrange("p (k f) -> p k f", k=KD)

        A6 = ps("A6", [P, 512])
        A7 = ps("A7", [P, 512])
        AQ = ps("AQ", [P, 2, 512])
        AS = [ps("AS0", [P, 512]), ps("AS1", [P, 512])]
        AT = [ps("AT0", [P, 512]), ps("AT1", [P, 512])]

        names = ("const_in qwo_in h_in0 h_in1 hr_in wst cleared ready wcv whi wlo "
                 "ve1_ok rs1_ok xn_ok xT_ps xh_ok xl_ok qk_ps v_ps v_ok rt_ok rope_ok hi_ok lo_ok "
                 "qa_ps qa_ev s_ps s_max mt_ps mt_ok mrow st_ps exp_ok sel_ok pv_ps on_ok "
                 "ot_ps oh_ok ol_ok pj_ps h2_ok h2_out ve2_ok rs2_ok x2_ok x2b_ok x2t_ps x2t_ok "
                 "lg_ps df_ok ed_ok cnt_ok rk_ps slot_ok row_ok scattered norm_step route_step").split()
        s = {n: sem(n) for n in names}
        h_in = [s["h_in0"], s["h_in1"]]
        block = ctx.enter_context(nc.Block())

        def await_(eng, name, value):
            if isinstance(value, int) and value <= 0:
                return
            eng.wait_ge(s[name], value)

        def there(b):
            return not isinstance(b, int) or 0 <= b < NB

        def rounds(eng, one):
            for b in range(3):
                one(b, b % 2)
            with eng.Fori(0, (NB - 4) // 2) as g:
                one(g * 2 + 3, 1)
                one(g * 2 + 4, 0)
            for b in range(NB - 1, NB + 3):
                one(b, b % 2)

        CONSTS = [(ident, "ident"), (ident_h, "ident_h"), (ident_b, "ident_b"), (mask_m, "mask_m"), (mask_t, "mask_t"),
                  (cosT, "cosT"), (sinT, "sinT"), (upper, "upper"), (ones_b, "ones_b"), (route_c, "route_c")]

        @block.sync
        def _(sp):
            sp.dma_start(wq32, a["wqkv_t"].rearrange("(k p) f -> p k f", p=P)).then_inc(s["qwo_in"], 16)
            sp.dma_start(wo32, a["wo_t"].rearrange("(k p) f -> p k f", p=P)).then_inc(s["qwo_in"], 16)
            for t, n in CONSTS:
                dst = t[:].bitcast(mybir.dt.uint16) if t.dtype == BF16 else t[:]
                sp.dma_start(dst, a[n]).then_inc(s["const_in"], 16)
            sp.dma_start(rw[:, :, :], a["router"].rearrange("(k p) e -> p k e", p=P)).then_inc(s["const_in"], 16)
            txt = a["txt"].rearrange("b t d -> (b t) d")

            def load_rows(dst, b, landed):
                sp.dma_start(dst[0:1, 0, :], a["cls"].rearrange("a b d -> (a b) d")).then_inc(landed, 16)
                sp.dma_start(dst[1:HEAD, 0, :], a["pe_rows"][bass.ds(b * NPATCH, NPATCH), :]).then_inc(landed, 16)
                sp.dma_start(dst[HEAD:P, 0, :], txt[bass.ds(b * TXT, P - HEAD), :]).then_inc(landed, 16)
                sp.dma_start(dst[0:TAIL, 1, :], txt[bass.ds(b * TXT + P - HEAD, TAIL), :]).then_inc(landed, 16)

            def load_w(b):
                sp.dma_start(stg[:, 0:1, :], a["w1"].rearrange("e (k p) f -> p (e k) f", p=P)[:, bass.ds(b, 1), :])\
                  .then_inc(s["wst"], 16)
                sp.dma_start(stg[:, 1, :].rearrange("p (a f) -> p a f", a=4),
                             a["w2"].rearrange("e (k p) f -> p (e k) f", p=P)[:, bass.ds(b * 4, 4), :]).then_inc(s["wst"], 16)

            def move_maxima(b, par):
                sp.wait_ge(s["mt_ok"], 2 * b + 2)
                sp.dma_start(QA[48:49, par, :, 0:P], mT_m[0:PAIRS, :]).then_inc(s["mrow"], 16)
                sp.dma_start(QA[112:113, par, :, 0:P], mT_m[PAIRS:2 * PAIRS, :]).then_inc(s["mrow"], 16)
                for odd in range(2):
                    row = QA[48 + 64 * odd:49 + 64 * odd, par, :, P:S]
                    for a0, n, gap in TAIL_UNITS:
                        c = 4 * odd + (0 if a0 == 0 else 3)
                        sp.dma_start(row[:, a0:a0 + n, :], mT_t[c:c + n, 0:TAIL]).then_inc(s["mrow"], 16)
                        sp.dma_start(row[:, a0 + gap:a0 + gap + n, :], mT_t[c:c + n, 64:64 + TAIL]).then_inc(s["mrow"], 16)

            def store_h2(b):
                sp.wait_ge(s["h2_ok"], b + 1)
                sp.dma_start(a["h2_rows"][bass.ds(b * S, P), :], HR[:, 0, :]).then_inc(s["h2_out"], 16)
                sp.dma_start(a["h2_rows"][bass.ds(b * S + P, TAIL), :], HR[0:TAIL, 1, :]).then_inc(s["h2_out"], 16)

            sp.wait_ge(s["cleared"], 1)
            load_rows(H[:, 0], 0, h_in[0])
            load_w(0)

            def one(b, par):
                if there(b + 1):
                    await_(sp, "xn_ok", b)
                    load_rows(H[:, 1 - par], b + 1, h_in[1 - par])
                if there(b - 3):
                    store_h2(b - 3)
                if there(b - 2):
                    normed, stored = b - 2, 32 * (b - 2)
                    if not isinstance(b, int):
                        normed, stored = sp.to_reg(normed), sp.to_reg(stored)
                    await_(sp, "x2_ok", normed)
                    await_(sp, "h2_out", stored)
                    load_rows(HR, b - 2, s["hr_in"])
                if there(b - 1):
                    move_maxima(b - 1, 1 - par)
                if there(b + 1) and there(b):
                    await_(sp, "wlo", b + 1)
                    load_w(b + 1)

            rounds(sp, one)
            sp.wait_ge(s["h2_out"], 32 * NB)

        @block.gpsimd
        def _(pool):
            nc.gpsimd.memset(H[:, :, 1, :], 0.0)
            nc.gpsimd.memset(HR[:, 1, :], 0.0)
            nc.gpsimd.memset(On[:, 1, :], 0.0)
            nc.gpsimd.memset(V[:, :, :, :, DK:DK + 1], 1.0)
            nc.gpsimd.memset(run[:, :, :], 0.0)
            nc.gpsimd.memset(mhalf[:, :, :], -0.5)
            nc.gpsimd.memset(blk[:, :, 0, :, 48:SLOT], 0.0)
            nc.gpsimd.memset(blk[:, :, 1, :, 48:49], MSCALE)
            nc.gpsimd.memset(blk[:, :, 1, :, 49:SLOT], 0.0).then_inc(s["cleared"], 1)
            pool.wait_ge(s["const_in"], 16 * (len(CONSTS) + 1))
            nc.gpsimd.tensor_copy(dest[:, :, :], route_c[:, 18:22].rearrange("p (a b) -> p a b", a=2)).then_inc(s["ready"], 1)
            pool.wait_ge(s["cleared"], 1)

            def rsqrt(ve, rs, done, wanted, b):
                pool.wait_ge(s[wanted], b + 1)
                nc.gpsimd.tensor_tensor(rs[:, :, :], ve[:, :, :], mhalf[:, :, :], ALU.pow).then_inc(s[done], 1)

            def rope(b):
                pool.wait_ge(s["rt_ok"], 3 * b + 3)
                await_(pool, "hi_ok", 4 * b)
                nc.gpsimd.tensor_tensor(rt1[:, :, :], rt1[:, :, :], rt2[:, :, :], ALU.add).then_inc(s["rope_ok"], 1)

            def lows(b):
                pool.wait_ge(s["hi_ok"], 4 * b + 4)
                r = rt1[:, :, :].rearrange("p a (q h d) -> p a q h d", q=2, h=NH)
                for q, slot in ((0, 2), (1, 1)):
                    nc.gpsimd.tensor_tensor(blk[:, :, q, :, slot * DK:(slot + 1) * DK], r[:, :, q],
                                            blk[:, :, q, :, 0:DK], ALU.subtract).then_inc(s["lo_ok"], 1)

            def select(b, units):
                for u in units:
                    a0, n = ST_UNITS[u // 2]
                    wait_apart(pool, s["exp_ok"], 8 * b + u + 1, s["cleared"])
                    v = PT[:, u % 2, a0:a0 + n, 0:P]
                    nc.gpsimd.affine_select(out=v, in_=v, compare_op=ALU.is_ge, fill=0.0, base=0,
                                            pattern=[[0, n], [1, P]], channel_multiplier=-1).then_inc(s["sel_ok"], 1)

            def select_tail(b):
                wait_apart(pool, s["exp_ok"], 8 * b + 8, s["cleared"])
                v = PTt[0:TAIL, :, :, :].rearrange("p a j t -> p (a j) t")
                nc.gpsimd.affine_select(out=v, in_=v, compare_op=ALU.is_ge, fill=0.0, base=0,
                                        pattern=[[0, 2 * PAIRS], [1, TAIL]], channel_multiplier=-1).then_inc(s["sel_ok"], 1)

            def scatter(b):
                wait_apart(pool, s["row_ok"], b + 1, s["cleared"])
                pool.wait_ge(s["x2b_ok"], b + 1)
                pool.wait_ge(s["slot_ok"], b + 1)
                for half, n in ((0, P), (1, TAIL)):
                    for c in range(2):
                        nc.gpsimd.indirect_dma_start(
                            out=a["slots"], out_offset=bass.IndirectOffsetOnAxis(ap=slotu[0:n, half, c:c + 1], axis=0),
                            in_=XR[0:n, half, c, :], in_offset=None).then_inc(s["scattered"], 16)

            rsqrt(ve1, rs1, "rs1_ok", "ve1_ok", 0)

            def one(b, par):
                if there(b - 3):
                    rsqrt(ve2, rs2, "rs2_ok", "ve2_ok", b - 3)
                if there(b - 2):
                    select(b - 2, range(6))
                    select_tail(b - 2)
                if there(b):
                    rope(b)
                if there(b + 1) and there(b):
                    rsqrt(ve1, rs1, "rs1_ok", "ve1_ok", b + 1)
                if there(b):
                    lows(b)
                if there(b - 3):
                    scatter(b - 3)

            rounds(pool, one)
            pool.wait_ge(s["scattered"], 64 * NB)

        @block.scalar
        def _(act):
            act.wait_ge(s["qwo_in"], 32)
            nc.scalar.activation(wq_h[:, :, :], wq32, ACT.Copy, scale=WSCALE).then_inc(s["wcv"], 1)
            nc.scalar.activation(wo_h[:, :, :], wo32, ACT.Copy, scale=WSCALE).then_inc(s["wcv"], 1)
            act.wait_ge(s["cleared"], 1)
            act.wait_ge(s["wcv"], 4)

            def x_high(b):
                act.wait_ge(s["xT_ps"], b + 1)
                nc.scalar.activation(xh[:, :, :], A6[:, :].rearrange("p (k t) -> p k t", k=KD), ACT.Copy).then_inc(s["xh_ok"], 1)

            def v_copy(b, par):
                act.wait_ge(s["v_ps"], b + 1)
                await_(act, "pv_ps", b - 1)
                for half in range(2):
                    nc.scalar.activation(V[:, par, half, :, 0:DK],
                                         A6[:, half * D:(half + 1) * D].rearrange("p (h d) -> p h d", h=NH),
                                         ACT.Copy, scale=1.0 / WSCALE).then_inc(s["v_ok"], 1)

            def highs(b):
                act.wait_ge(s["rope_ok"], b + 1)
                await_(act, "qa_ps", 4 * b)
                r = rt1[:, :, :].rearrange("p a (q h d) -> p a q h d", q=2, h=NH)
                for q, slot in ((0, 0), (1, 0), (0, 1), (1, 2)):
                    nc.scalar.activation(blk[:, :, q, :, slot * DK:(slot + 1) * DK], r[:, :, q], ACT.Copy).then_inc(s["hi_ok"], 1)

            def qa_evac(b, par):
                for u in (0, 2):
                    act.wait_ge(s["qa_ps"], 4 * b + u + 1)
                    await_(act, "st_ps", 8 * (b - 1))
                    dst = (QA, KA)[u // 2][:, par, 0:4, 0:S]
                    src = AQ[:, u % 2, :].bitcast(F16)[:, 0:4 * SR].rearrange("p (j t) -> p j t", j=4)[:, :, 0:S]
                    nc.scalar.activation(dst, src, ACT.Copy).then_inc(s["qa_ev"], 1)

            def exps(b):
                await_(act, "pv_ps", b)
                u = 0
                for a0, n in ST_UNITS:
                    for odd in range(2):
                        u += 1
                        act.wait_ge(s["st_ps"], 8 * b + u)
                        nc.scalar.activation(PT[:, odd, a0:a0 + n, :],
                                             AT[odd][:, 0:n * S].rearrange("p (j t) -> p j t", j=n),
                                             ACT.Exp, scale=DK ** -0.5).then_inc(s["exp_ok"], 1)
                for odd in range(2):
                    u += 1
                    act.wait_ge(s["st_ps"], 8 * b + u)
                    nc.scalar.activation(PTt[0:TAIL, odd, :, :],
                                         AT[odd][0:TAIL, 0:PAIRS * TAIL].rearrange("p (j t) -> p j t", j=PAIRS),
                                         ACT.Exp, scale=DK ** -0.5).then_inc(s["exp_ok"], 1)

            def w_high(b):
                act.wait_ge(s["wst"], 32 * b + 32)
                nc.scalar.activation(W1H[:, bass.ds(b, 1), :], stg[:, 0:1, :], ACT.Copy, scale=WSCALE)
                nc.scalar.activation(W2H[:, bass.ds(b * 4, 4), :], stg[:, 1, :].rearrange("p (a f) -> p a f", a=4),
                                     ACT.Copy, scale=WSCALE).then_inc(s["whi"], 1)

            def o_high(b):
                act.wait_ge(s["ot_ps"], b + 1)
                nc.scalar.activation(oh, A7[:, :].rearrange("p (k t) -> p k t", k=KD), ACT.Copy).then_inc(s["oh_ok"], 1)

            def x2_turned(b):
                act.wait_ge(s["x2t_ps"], b + 1)
                nc.scalar.activation(x2T, A7[:, :].rearrange("p (k t) -> p k t", k=KD), ACT.Copy).then_inc(s["x2t_ok"], 1)

            def x2_copy(b):
                act.wait_ge(s["x2_ok"], b + 1)
                nc.scalar.activation(XR[:, :, 1, 0:D], XR[:, :, 0, 0:D], ACT.Copy).then_inc(s["x2b_ok"], 1)

            def gate_exp(b):
                act.wait_ge(s["df_ok"], b + 1)
                nc.scalar.activation(ed[:, :, :], df[:, :, :], ACT.Exp).then_inc(s["ed_ok"], 1)

            def one(b, par):
                if there(b - 3):
                    o_high(b - 3)
                if there(b):
                    x_high(b)
                if there(b - 1):
                    qa_evac(b - 1, 1 - par)
                if there(b - 2):
                    exps(b - 2)
                if there(b - 3):
                    x2_turned(b - 3)
                    x2_copy(b - 3)
                if there(b):
                    w_high(b)
                    highs(b)
                if there(b - 3):
                    gate_exp(b - 3)
                if there(b):
                    v_copy(b, par)

            rounds(act, one)

        @block.vector
        def _(dve):
            dve.wait_ge(s["wcv"], 2)
            nc.vector.scalar_tensor_tensor(out=wq_l[:, :, :], in0=wq32, scalar=WSCALE, in1=wq_h[:, :, :],
                                           op0=ALU.mult, op1=ALU.subtract).then_inc(s["wcv"], 1)
            nc.vector.scalar_tensor_tensor(out=wo_l[:, :, :], in0=wo32, scalar=WSCALE, in1=wo_h[:, :, :],
                                           op0=ALU.mult, op1=ALU.subtract).then_inc(s["wcv"], 1)
            dve.wait_ge(s["const_in"], 16 * (len(CONSTS) + 1))
            dve.wait_ge(s["cleared"], 1)
            dve.wait_ge(s["ready"], 1)

            def stats(link, src, st, mv, ve):
                for half in range(2):
                    ins = nc.vector.bn_stats(st[:, half, :], src[:, half, :])
                link(ins, alone=True)
                for half in range(2):
                    ins = nc.vector.bn_aggr(mv[:, half, :], st[:, half, :])
                link(ins)
                return nc.vector.tensor_scalar(ve[:, :, :], mv[:, :, 1:2], LN1_EPS, None, ALU.add)

            def normed(src, mv, rs, dst):
                for half in range(2):
                    ins = nc.vector.tensor_scalar(dst[:, half], src[:, half, :], mv[:, half, 0:1], rs[:, half, :],
                                                  ALU.subtract, ALU.mult)
                return ins

            def norm1_stats(b, par):
                link = Chain(dve, s["norm_step"], b * 2, s["cleared"])
                dve.wait_ge(h_in[par], 64 * (b // 2 + 1) if isinstance(b, int) else (b + (2 - par)) * 32)
                stats(link, H[:, par], st1, mv1, ve1).then_inc(s["ve1_ok"], 1)

            def norm1_apply(b, par):
                await_(dve, "rope_ok", b)
                dve.wait_ge(s["rs1_ok"], b + 1)
                normed(H[:, par], mv1, rs1, xn).then_inc(s["xn_ok"], 1)

            def x_low(b):
                dve.wait_ge(s["xh_ok"], b + 1)
                nc.vector.tensor_tensor(xl[:, :, :], A6[:, :].rearrange("p (k t) -> p k t", k=KD), xh[:, :, :],
                                        ALU.subtract).then_inc(s["xl_ok"], 1)

            def rotate(b):
                dve.wait_ge(s["qk_ps"], b + 1)
                await_(dve, "lo_ok", 2 * b)

                def heads(v):
                    return v.rearrange("p a (h n two) -> p a h n two", h=2 * NH, two=2)

                def table(v, which):
                    v = v[:, :, :].rearrange("p a (o n two) -> p a o n two", o=1, two=2)[:, :, :, :, which]
                    return v.to_broadcast([P, 2, 2 * NH, DK // 2])
                cs = cosT[:, :, :].rearrange("p a (o n) -> p a o n", o=1).to_broadcast([P, 2, 2 * NH, DK])
                nc.vector.tensor_tensor(rt1[:, :, :].rearrange("p a (h n) -> p a h n", n=DK),
                                        AQ[:, :, :].rearrange("p a (h n) -> p a h n", n=DK), cs, ALU.mult).then_inc(s["rt_ok"], 1)
                for even in range(2):
                    nc.vector.tensor_tensor(heads(rt2[:, :, :])[:, :, :, :, even], heads(AQ[:, :, :])[:, :, :, :, 1 - even],
                                            table(sinT, even), ALU.mult).then_inc(s["rt_ok"], 1)

            def qa_evac(b, par):
                for u in (1, 3):
                    dve.wait_ge(s["qa_ps"], 4 * b + u + 1)
                    await_(dve, "st_ps", 8 * (b - 1))
                    dst = (QA, KA)[u // 2][:, par, 4:8, 0:S]
                    src = AQ[:, u % 2, :].bitcast(F16)[:, 0:4 * SR].rearrange("p (j t) -> p j t", j=4)[:, :, 0:S]
                    nc.vector.tensor_copy(dst, src).then_inc(s["qa_ev"], 1)

            def maxima(b):
                u = 0
                for r in range(2):
                    for odd in range(2):
                        u += 1
                        dve.wait_ge(s["s_ps"], 8 * b + u)
                        nc.vector.tensor_reduce(mx_m[:, odd, 4 * r:4 * r + 4],
                                                AS[odd][:, :].rearrange("p (j t) -> p j t", j=4), AX.X, ALU.max).then_inc(s["s_max"], 1)
                for c0, (a0, n, gap) in zip((0, 3), TAIL_UNITS):
                    for odd in range(2):
                        u += 1
                        dve.wait_ge(s["s_ps"], 8 * b + u)
                        nc.vector.tensor_reduce(mx_t[:, odd, c0:c0 + n],
                                                AS[odd][:, 0:n * S].rearrange("p (j t) -> p j t", j=n), AX.X, ALU.max).then_inc(s["s_max"], 1)

            def maxima_turned(b):
                dve.wait_ge(s["mt_ps"], b + 1)
                nc.vector.tensor_scalar(mT_m[:, :], A6[0:2 * PAIRS, 0:P], -1.0 / MSCALE, None, ALU.mult).then_inc(s["mt_ok"], 1)
                nc.vector.tensor_scalar(mT_t[:, :], A6[0:8, P:2 * P], -1.0 / MSCALE, None, ALU.mult).then_inc(s["mt_ok"], 1)

            def w_low(b):
                dve.wait_ge(s["whi"], b + 1)
                nc.vector.scalar_tensor_tensor(out=W1L[:, bass.ds(b, 1), :], in0=stg[:, 0:1, :], scalar=WSCALE,
                                               in1=W1H[:, bass.ds(b, 1), :], op0=ALU.mult, op1=ALU.subtract)
                nc.vector.scalar_tensor_tensor(out=W2L[:, bass.ds(b * 4, 4), :], in0=stg[:, 1, :].rearrange("p (a f) -> p a f", a=4),
                                               scalar=WSCALE, in1=W2H[:, bass.ds(b * 4, 4), :],
                                               op0=ALU.mult, op1=ALU.subtract).then_inc(s["wlo"], 1)

            RS = 15

            def o_norm(b):
                dve.wait_ge(s["pv_ps"], b + 1)
                await_(dve, "ot_ps", b)
                sums = [AT[half][:, 0:NH * (DK + 1)].rearrange("p (h d) -> p h d", h=NH) for half in range(2)]
                nc.vector.reciprocal(rec[:, 0, :], sums[0][:, :, DK]).then_inc(s["on_ok"], 1)
                nc.vector.reciprocal(rec[0:TAIL, 1, :], sums[1][0:TAIL, :, DK]).then_inc(s["on_ok"], 1)
                dve.wait_ge(s["on_ok"], 4 * b + 2)
                for half, n in ((0, P), (1, TAIL)):
                    nc.vector.tensor_tensor(On[0:n, half, :].rearrange("p (h d) -> p h d", h=NH), sums[half][0:n, :, 0:DK],
                                            rec[0:n, half, :].rearrange("p (h a) -> p h a", a=1).to_broadcast([n, NH, DK]),
                                            ALU.mult).then_inc(s["on_ok"], 1)

            def o_low(b):
                dve.wait_ge(s["oh_ok"], b + 1)
                nc.vector.tensor_tensor(ol, A7[:, :].rearrange("p (k t) -> p k t", k=KD), oh,
                                        ALU.subtract).then_inc(s["ol_ok"], 1)

            def residual(b, link):
                dve.wait_ge(s["pj_ps"], b + 1)
                dve.wait_ge(s["hr_in"], 64 * b + 64)
                nc.vector.scalar_tensor_tensor(out=HR[:, :, :], in0=A7[:, :].rearrange("p (a t) -> p a t", a=2),
                                               scalar=1.0 / WSCALE, in1=HR[:, :, :], op0=ALU.mult, op1=ALU.add).then_inc(s["h2_ok"], 1)
                dve.wait_ge(s["h2_ok"], b + 1)
                stats(link, HR, st2, mv2, ve2).then_inc(s["ve2_ok"], 1)

            def norm2_apply(b):
                await_(dve, "scattered", 64 * b)
                dve.wait_ge(s["rs2_ok"], b + 1)
                normed(HR, mv2, rs2, XR[:, :, 0, 0:D]).then_inc(s["x2_ok"], 1)

            def choose(b, link):
                dve.wait_ge(s["lg_ps"], b + 1)
                link(nc.vector.tensor_copy(lg[:, :, :], A7[:, 0:2 * E].rearrange("p (a e) -> p a e", a=2)), alone=True)
                for half in range(2):
                    ins = nc.vector.max(m8[:, half, :], lg[:, half, :])
                link(ins, alone=True)
                for half in range(2):
                    ins = nc.vector.max_index(i8[:, half, :], m8[:, half, :], lg[:, half, :])
                link(ins)
                nc.vector.tensor_tensor(df[:, :, :], m8[:, :, 1:2], m8[:, :, 0:1], ALU.subtract).then_inc(s["df_ok"], 1)
                link(nc.vector.tensor_tensor(idf[:, :, :], i8[:, :, 0:2],
                                             route_c[:, 16:18].rearrange("p (a o) -> p a o", o=1).to_broadcast([P, 2, 2]), ALU.add))
                for half in range(2):
                    for c in range(2):
                        ins = nc.vector.tensor_scalar(onehot[:, half, c, :], route_c[:, 0:E], idf[:, half, c:c + 1], None, ALU.is_equal)
                link(ins)
                link(nc.vector.tensor_tensor(cnt[:, :, :], onehot[:, :, 0, :], onehot[:, :, 1, :], ALU.add))
                link(nc.vector.tensor_tensor(run[:, 1, :], run[:, 0, :], cnt[:, 0, :], ALU.add))
                nc.vector.tensor_copy(runb[:, :, :], run[:, :, :]).then_inc(s["cnt_ok"], 1)
                dve.wait_ge(s["cnt_ok"], b + 1)
                nc.vector.tensor_tensor(run[:, 0, :], run[:, 1, :], cnt[:, 1, :], ALU.add)

            def place(b, link):
                dve.wait_ge(s["ed_ok"], b + 1)
                link(nc.vector.tensor_scalar(e1[:, :, :], ed[:, :, :], 1.0, None, ALU.add))
                link(nc.vector.reciprocal(XR[:, :, 0, D:D + 1], e1[:, :, :]))
                nc.vector.tensor_tensor(XR[:, :, 1, D:D + 1], XR[:, :, 0, D:D + 1], ed[:, :, :], ALU.mult)
                link(nc.vector.tensor_copy(XR[:, :, :, D + 1:D + 2], dest[:, :, :].rearrange("p a (c o) -> p a c o", o=1)))
                nc.vector.tensor_scalar(dest[:, :, :], dest[:, :, :], float(2 * S), None, ALU.add).then_inc(s["row_ok"], 1)
                dve.wait_ge(s["rk_ps"], b + 1)
                link(nc.vector.tensor_tensor(rkb[:, :, :], A7[:, 32:32 + 2 * E].rearrange("p (a e) -> p a e", a=2),
                                             route_c[:, 8:16].rearrange("p (o e) -> p o e", o=1).to_broadcast([P, 2, E]), ALU.add))
                for c in range(2):
                    ins = nc.vector.tensor_tensor(prod[:, :, c, :], onehot[:, :, c, :], rkb[:, :, :], ALU.mult)
                link(ins)
                link(nc.vector.tensor_reduce(slotf[:, :, :], prod[:, :, :, :], AX.X, ALU.add))
                nc.vector.tensor_copy(slotu[:, :, :], slotf[:, :, :]).then_inc(s["slot_ok"], 1)
                dve.wait_ge(s["row_ok"], b + 1)

            norm1_stats(0, 0)
            norm1_apply(0, 0)

            def one(b, par):
                link = Chain(dve, s["route_step"], (b - 3) * RS, s["cleared"])
                if there(b - 3):
                    o_low(b - 3)
                if there(b):
                    x_low(b)
                if there(b - 1):
                    qa_evac(b - 1, 1 - par)
                if there(b - 3):
                    residual(b - 3, link)
                if there(b - 3):
                    norm2_apply(b - 3)
                if there(b):
                    rotate(b)
                if there(b + 1) and there(b):
                    norm1_stats(b + 1, 1 - par)
                if there(b - 3):
                    choose(b - 3, link)
                if there(b):
                    w_low(b)
                if there(b - 2):
                    o_norm(b - 2)
                if there(b - 3):
                    place(b - 3, link)
                    assert link.n == RS, link.n
                if there(b - 1):
                    maxima(b - 1)
                if there(b + 1) and there(b):
                    norm1_apply(b + 1, 1 - par)
                if there(b - 1):
                    maxima_turned(b - 1)

            rounds(dve, one)
            nc.vector.tensor_copy(a["total"][:, :], run[:, 0, :])

        @block.tensor
        def _(pe):
            pe.wait_ge(s["const_in"], 16 * (len(CONSTS) + 1))
            pe.wait_ge(s["wcv"], 4)
            pe.wait_ge(s["cleared"], 1)
            mm = nc.tensor.matmul

            def three(out, xh_, xl_, wh_, wl_, start, stop):
                mm(out, xh_, wh_, start=start, stop=False)
                mm(out, xh_, wl_, start=False, stop=False)
                return mm(out, xl_, wh_, start=False, stop=stop)

            def turn(dst, src, done):
                for k in range(KD):
                    for half in range(2):
                        ins = nc.tensor.transpose(dst[:, k * 2 * P + half * P:k * 2 * P + half * P + P],
                                                  src[:, half, k * P:(k + 1) * P], ident[:, :])
                ins.then_inc(s[done], 1)

            def x_turn(b):
                pe.wait_ge(s["xn_ok"], b + 1)
                await_(pe, "mt_ok", 2 * (b - 1))
                if isinstance(b, int) and b == 1:
                    await_(pe, "v_ok", 2)
                turn(A6, xn, "xT_ps")

            def project_qk(b):
                pe.wait_ge(s["xl_ok"], b + 1)
                await_(pe, "qa_ev", 4 * b)
                for half in range(2):
                    for k in range(KD):
                        t = slice(half * P, half * P + P)
                        ins = three(AQ[:, half, :], xh[:, k, t], xl[:, k, t], wq_h[:, k, 0:2 * D], wq_l[:, k, 0:2 * D],
                                    k == 0, k == KD - 1)
                ins.then_inc(s["qk_ps"], 1)

            def project_v(b):
                for half in range(2):
                    for k in range(KD):
                        t = slice(half * P, half * P + P)
                        ins = three(A6[:, half * D:(half + 1) * D], xh[:, k, t], xl[:, k, t],
                                    wq_h[:, k, 2 * D:3 * D], wq_l[:, k, 2 * D:3 * D], k == 0, k == KD - 1)
                ins.then_inc(s["v_ps"], 1)

            def qa_turn(b):
                pe.wait_ge(s["lo_ok"], 2 * b + 2)
                for u in range(4):
                    if u == 2:
                        pe.wait_ge(s["qa_ev"], 4 * b + 2)
                    q, j0 = u // 2, 4 * (u % 2)
                    out = AQ[:, u % 2, :].bitcast(F16)
                    for j in range(4):
                        for half, n in ((0, P), (1, TAIL)):
                            src = blk[0:n, half, q, 2 * (j0 + j):2 * (j0 + j) + 2, :].rearrange("p h d -> p (h d)")
                            ins = nc.tensor.transpose(out[:, j * SR + half * P:j * SR + half * P + n], src, ident_h[0:n, 0:n])
                    ins.then_inc(s["qa_ps"], 1)

            def wait_bank(b, u):
                await_(pe, "s_max", 8 * b + (u - 2))

            def scores(b, par):
                pe.wait_ge(s["qa_ev"], 4 * b + 4)
                u = 0
                for r in range(2):
                    for odd in range(2):
                        u += 1
                        wait_bank(b, u)
                        mm(AS[odd][:, :].rearrange("p (j t) -> p j t", j=4), ident_b[:, :],
                           mask_m[:, :].rearrange("p (j t) -> p j t", j=1).to_broadcast([P, 4, P]), start=True, stop=False,
                           skip_group_check=True)
                        rows = slice(64 * odd, 64 * odd + 64)
                        for j in range(4):
                            ins = mm(AS[odd][:, j * P:(j + 1) * P], QA[rows, par, 4 * r + j, 0:P], KA[rows, par, 4 * r + j, 0:P],
                                     start=False, stop=(j == 3), skip_group_check=True)
                        ins.then_inc(s["s_ps"], 1)
                for a0, n, gap in TAIL_UNITS:
                    for odd in range(2):
                        u += 1
                        wait_bank(b, u)
                        mm(AS[odd][:, 0:n * S].rearrange("p (j t) -> p j t", j=n), ident_b[:, :],
                           mask_t[:, :].rearrange("p (j t) -> p j t", j=1).to_broadcast([P, n, S]),
                           start=True, stop=False, skip_group_check=True)
                        rows = slice(64 * odd, 64 * odd + 64)
                        for g in range(2):
                            for j in range(n):
                                jj = a0 + g * gap + j
                                ins = mm(AS[odd][64 * g:64 * g + TAIL, j * S:(j + 1) * S], QA[rows, par, jj, P:S],
                                         KA[rows, par, jj, 0:S], start=False, stop=True, skip_group_check=True)
                        ins.then_inc(s["s_ps"], 1)

            def maxima_turn(b):
                pe.wait_ge(s["s_max"], 8 * b + 8)
                await_(pe, "v_ok", 2 * (b + 2) if not isinstance(b, int) else 2 * min(b + 2, NB))
                nc.tensor.transpose(A6[0:2 * PAIRS, 0:P], mx_m[:, :, :].rearrange("p a j -> p (a j)"), ident[:, :])
                nc.tensor.transpose(A6[0:8, P:2 * P], mx_t[:, :, :].rearrange("p a j -> p (a j)"), ident[:, :]).then_inc(s["mt_ps"], 1)

            def scores_turned(b, par):
                await_(pe, "on_ok", 4 * b)
                wait_apart(pe, s["mrow"], 160 * b + 160, s["cleared"])
                u = 0
                for a0, n in ST_UNITS:
                    for odd in range(2):
                        u += 1
                        if u > 2:
                            wait_apart(pe, s["exp_ok"], 8 * b + u - 2, s["cleared"])
                        rows = slice(64 * odd, 64 * odd + 64)
                        for j in range(n):
                            ins = mm(AT[odd][:, j * S:(j + 1) * S], KA[rows, par, a0 + j, 0:P], QA[rows, par, a0 + j, 0:S],
                                     start=True, stop=True, skip_group_check=True)
                        ins.then_inc(s["st_ps"], 1)
                for odd in range(2):
                    u += 1
                    wait_apart(pe, s["exp_ok"], 8 * b + u - 2, s["cleared"])
                    rows = slice(64 * odd, 64 * odd + 64)
                    for j in range(PAIRS):
                        ins = mm(AT[odd][0:TAIL, j * TAIL:(j + 1) * TAIL], KA[rows, par, j, P:S], QA[rows, par, j, P:S],
                                 start=True, stop=True, skip_group_check=True)
                    ins.then_inc(s["st_ps"], 1)

            def values(b, par):
                pe.wait_ge(s["sel_ok"], 7 * b + 7)
                pe.wait_ge(s["exp_ok"], 8 * b + 8)
                w = DK + 1
                for h in range(NH):
                    mm(AT[0][:, h * w:(h + 1) * w], PT[:, h % 2, h // 2, 0:P], V[:, par, 0, h, :], start=True, stop=True,
                       skip_group_check=True)
                for h in range(NH):
                    mm(AT[1][0:TAIL, h * w:(h + 1) * w], PT[:, h % 2, h // 2, P:S], V[:, par, 0, h, :], start=True, stop=False,
                       skip_group_check=True)
                    ins = mm(AT[1][0:TAIL, h * w:(h + 1) * w], PTt[0:TAIL, h % 2, h // 2, :], V[0:TAIL, par, 1, h, :],
                             start=False, stop=True, skip_group_check=True)
                ins.then_inc(s["pv_ps"], 1)

            def o_turn(b):
                pe.wait_ge(s["on_ok"], 4 * b + 4)
                await_(pe, "slot_ok", b)
                turn(A7, On, "ot_ps")

            def project(b):
                pe.wait_ge(s["ol_ok"], b + 1)
                for half in range(2):
                    for k in range(KD):
                        t = slice(half * P, half * P + P)
                        ins = three(A7[:, half * D:(half + 1) * D], oh[:, k, t], ol[:, k, t], wo_h[:, k, :], wo_l[:, k, :],
                                    k == 0, k == KD - 1)
                ins.then_inc(s["pj_ps"], 1)

            def x2_turn(b):
                pe.wait_ge(s["x2_ok"], b + 1)
                turn(A7, XR[:, :, 0, 0:D], "x2t_ps")

            def logits(b):
                pe.wait_ge(s["x2t_ok"], b + 1)
                for half in range(2):
                    for k in range(KD):
                        ins = mm(A7[:, half * E:(half + 1) * E], x2T[:, k, half * P:(half + 1) * P], rw[:, k, :],
                                 start=(k == 0), stop=(k == KD - 1))
                ins.then_inc(s["lg_ps"], 1)

            def ranks(b):
                pe.wait_ge(s["cnt_ok"], b + 1)
                for half in range(2):
                    out = A7[:, 32 + half * E:32 + (half + 1) * E]
                    mm(out, upper[:, :], cnt[:, half, :], start=True, stop=False)
                    ins = mm(out, ones_b[:, :], runb[:, half, :], start=False, stop=True)
                ins.then_inc(s["rk_ps"], 1)

            def one(b, par):
                if there(b - 3):
                    o_turn(b - 3)
                if there(b):
                    x_turn(b)
                if there(b - 1):
                    qa_turn(b - 1)
                if there(b - 3):
                    project(b - 3)
                if there(b):
                    project_qk(b)
                if there(b - 2):
                    scores_turned(b - 2, par)
                if there(b - 3):
                    x2_turn(b - 3)
                if there(b):
                    project_v(b)
                if there(b - 3):
                    logits(b - 3)
                if there(b - 2):
                    values(b - 2, par)
                if there(b - 3):
                    ranks(b - 3)
                if there(b - 1):
                    scores(b - 1, 1 - par)
                    maxima_turn(b - 1)

            rounds(pe, one)


RING = 4


def stage_experts(nc, a, wts):
    W1H, W1L, W2H, W2L = wts
    with ExitStack() as ctx:
        sb = lambda n, s, d: ctx.enter_context(nc.sbuf_tensor(n, s, d))
        sem = lambda n: ctx.enter_context(nc.semaphore(n))
        ident = sb("ident2", [P, P], F32)
        ones = sb("ones2", [P, P], F32)
        gam = sb("gam", [P, E, D], F32)
        bet = sb("bet", [P, E, D], F32)
        b2s = sb("b2s", [P, E, D], F32)
        b1s = sb("b1s", [P, E * KF], F32)
        pad = sb("pad", [P, XROW], F32)
        tc_ = sb("tc_", [1, TILES * E + E], F32)
        ctot = sb("ctot", [P, E], F32)
        ni = sb("ni", [1, 2, E], I32)
        ntf = sb("ntf", [1, E], F32)
        cum = sb("cum", [1, E], F32)
        gap = sb("gap", [1, E], F32)
        ge = sb("ge", [1, TILES, E], F32)
        gp = sb("gp", [1, TILES, E], F32)
        tf = sb("tf", [1, 3, TILES], F32)
        zf = sb("zf", [1, E], F32)
        table = sb("table", [1, 2 * TILES + E], I32)
        X = sb("X", [P, RING, XROW], F32)
        gd = sb("gd", [P, RING, 2], F32)
        xh = sb("xh2", [P, 2, KD, P], F16)
        xl = sb("xl2", [P, 2, KD, P], F16)
        hf = sb("hf", [P, 2, KF, P], F32)
        hh = sb("hh", [P, 2, KF, P], F16)
        hl = sb("hl", [P, 2, KF, P], F16)
        xb = sb("xb", [P, 2, D], F32)
        r = sb("r", [P, D], F32)
        st = sb("st", [P, 6], F32)
        mv = sb("mv", [P, 2], F32)
        rs = sb("rs", [P, 1], F32)
        rg = sb("rg", [P, 1], F32)
        ve = sb("ve", [P, 1], F32)
        mhalf = sb("mhalf2", [P, 1], F32)
        nrm = sb("nrm", [P, D], F32)
        y1 = sb("y1", [P, D], F32)
        y = sb("y", [P, 2, D], F32)
        du = sb("du", [P, 2, 1], U32)
        XT = [ctx.enter_context(nc.psum_tensor(f"XT{i}", [P, 512], F32)) for i in range(2)]
        HP = [ctx.enter_context(nc.psum_tensor(f"HP{i}", [P, 4, P], F32)) for i in range(4)]
        OP = [ctx.enter_context(nc.psum_tensor(f"OP{i}", [P, 512], F32)) for i in range(2)]
        names = ("ve_ok rs_ok half_ok c_in tab tot_ps pad_ok pads xt_ps xh_ok xl_ok gd_ok h_ps h_ok hh_ok hl_ok o_ps xb_ok r_ok "
                 "setup_step norm_step2 nrm_ok y1_ok y_ok y_out0 y_out1").split()
        s = {n: sem(n) for n in names}
        x_in = [sem(f"x_in_{i}") for i in range(RING)]
        y_out = [s["y_out0"], s["y_out1"]]
        block = ctx.enter_context(nc.Block())

        def rounds(eng, one):
            for t in range(RING):
                one(t, t)
            with eng.Fori(1, TILES // RING) as g:
                for c in range(RING):
                    one(g * RING + c, c)
            for t in range(TILES // RING * RING, TILES + 3):
                one(t, t % RING)

        def there(t):
            return not isinstance(t, int) or 0 <= t < TILES

        def await_(eng, sem_, value):
            if isinstance(value, int) and value <= 0:
                return
            eng.wait_ge(sem_, value)

        def expert_of(eng, t):
            return eng.value_load(table[0:1, bass.ds(t, 1)], min_val=0, max_val=E - 1)

        def x_arrived(eng, t, c):
            eng.wait_ge(x_in[c], 16 * (t // RING + 1) if isinstance(t, int) else (t + (RING - c)) * (16 // RING))

        @block.sync
        def _(sp):
            sp.dma_start(ident[:, :], a["ident"]).then_inc(s["c_in"], 16)
            sp.dma_start(pad[:, :], a["pad"]).then_inc(s["c_in"], 16)
            sp.dma_start(tc_[:, :], a["tile_c"]).then_inc(s["c_in"], 16)
            sp.dma_start(b1s[:, :], a["b1_t"]).then_inc(s["c_in"], 16)
            for dst, n in ((gam, "gamma"), (bet, "beta"), (b2s, "b2")):
                sp.dma_start(dst[:, :, :].rearrange("p e d -> p (e d)"),
                             a[n].rearrange("(o e) d -> o (e d)", o=1).to_broadcast([P, E * D])).then_inc(s["c_in"], 16)
            sp.wait_ge(s["tab"], 1)
            sp.wait_ge(s["c_in"], 16 * 7)
            for e in range(E):
                z = sp.value_load(table[0:1, 2 * TILES + e:2 * TILES + e + 1], min_val=0, max_val=E * REG - P)
                sp.dma_start(a["slots"][bass.ds(z, P), :], pad[:, :]).then_inc(s["pads"], 16)
            sp.dma_start(a["slots"][E * REG:E * REG + P, :], pad[:, :]).then_inc(s["pads"], 16)
            sp.wait_ge(s["pads"], 16 * (E + 1))

            def load(t, c):
                row = sp.value_load(table[0:1, bass.ds(t + TILES, 1)], min_val=0, max_val=E * REG)
                free = t - (RING - 1)
                if not isinstance(t, int):
                    free = sp.to_reg(free)
                await_(sp, s["xt_ps"], free)
                await_(sp, s["gd_ok"], free)
                await_(sp, s["xb_ok"], free)
                sp.dma_start(X[:, c, :], a["slots"][bass.ds(row, P), :]).then_inc(x_in[c], 16)

            def one(t, c):
                if there(t):
                    load(t, c)
            rounds(sp, one)

        @block.tensor
        def _(pe):
            mm = nc.tensor.matmul
            pe.wait_ge(s["c_in"], 16 * 7)
            pe.wait_ge(s["pad_ok"], 1)
            mm(XT[0][:, 0:E], ones[:, :], a["total"][:, :], start=True, stop=True).then_inc(s["tot_ps"], 1)
            pe.wait_ge(s["tab"], 1)

            def turn(t, c):
                x_arrived(pe, t, c)
                await_(pe, s["xl_ok"], t - 1)
                for k in range(KD):
                    ins = nc.tensor.transpose(XT[c % 2][:, k * P:(k + 1) * P], X[:, c, k * P:(k + 1) * P], ident[:, :])
                ins.then_inc(s["xt_ps"], 1)

            def up(t, c):
                e = expert_of(pe, t)
                par = c % 2
                pe.wait_ge(s["xl_ok"], t + 1)
                for hb in range(2):
                    await_(pe, s["h_ok"], (t - 2) * 2 + hb + 1)
                    for f in range(4):
                        for k in range(KD):
                            off = k * FF + (hb * 4 + f) * P
                            wh = W1H[:, :, :].rearrange("p a f -> p (a f)")[:, bass.ds(e * (KD * FF) + off, P)]
                            wl = W1L[:, :, :].rearrange("p a f -> p (a f)")[:, bass.ds(e * (KD * FF) + off, P)]
                            out = HP[par * 2 + hb][:, f, :]
                            mm(out, wh, xh[:, par, k, :], start=(k == 0), stop=False)
                            mm(out, wh, xl[:, par, k, :], start=False, stop=False)
                            ins = mm(out, wl, xh[:, par, k, :], start=False, stop=(k == KD - 1))
                    ins.then_inc(s["h_ps"], 1)

            def down(t, c):
                e = expert_of(pe, t)
                par = c % 2
                await_(pe, s["r_ok"], t - 1)
                for f in range(KF):
                    if f % 4 == 0:
                        pe.wait_ge(s["hl_ok"], 2 * t + f // 4 + 1)
                    wh = W2H[:, :, :].rearrange("p a f -> p (a f)")[:, bass.ds(e * (KF * D) + f * D, D)]
                    wl = W2L[:, :, :].rearrange("p a f -> p (a f)")[:, bass.ds(e * (KF * D) + f * D, D)]
                    mm(OP[par][:, 0:D], hh[:, par, f, :], wh, start=(f == 0), stop=False)
                    mm(OP[par][:, 0:D], hh[:, par, f, :], wl, start=False, stop=False)
                    ins = mm(OP[par][:, 0:D], hl[:, par, f, :], wh, start=False, stop=(f == KF - 1))
                ins.then_inc(s["o_ps"], 1)

            turn(0, 0)

            def one(t, c):
                if there(t) and there(t + 1):
                    turn(t + 1, (c + 1) % RING)
                if there(t):
                    up(t, c)
                if there(t - 1):
                    down(t - 1, (c - 1) % RING)
            rounds(pe, one)

        @block.scalar
        def _(act):
            act.wait_ge(s["tab"], 1)
            act.wait_ge(s["c_in"], 16 * 7)

            def x_high(t, c):
                act.wait_ge(s["xt_ps"], t + 1)
                await_(act, s["h_ps"], 2 * (t - 1))
                nc.scalar.activation(xh[:, c % 2], XT[c % 2][:, 0:D].rearrange("p (k t) -> p k t", k=KD), ACT.Copy).then_inc(s["xh_ok"], 1)

            def gelu(t, c, hb, e):
                act.wait_ge(s["h_ps"], 2 * t + hb + 1)
                await_(act, s["hl_ok"], (t - 2) * 2 + hb + 1)
                par = c % 2
                for f in range(4):
                    ins = nc.scalar.activation(hf[:, par, hb * 4 + f, :], HP[par * 2 + hb][:, f, :], ACT.Gelu,
                                               bias=b1s[:, bass.ds(e * KF + (hb * 4 + f), 1)], scale=1.0 / WSCALE)
                ins.then_inc(s["h_ok"], 1)

            def gelu_high(t, c, hb):
                await_(act, s["o_ps"], t - 1)
                act.wait_ge(s["h_ok"], 2 * t + hb + 1)
                f = slice(4 * hb, 4 * hb + 4)
                nc.scalar.activation(hh[:, c % 2, f, :], hf[:, c % 2, f, :], ACT.Copy).then_inc(s["hh_ok"], 1)

            x_high(0, 0)

            def one(t, c):
                if there(t) and there(t + 1):
                    x_high(t + 1, (c + 1) % RING)
                if there(t):
                    e = expert_of(act, t)
                    for hb in range(2):
                        gelu(t, c, hb, e)
                        gelu_high(t, c, hb)
            rounds(act, one)

        @block.vector
        def _(dve):
            link = Chain(dve, s["setup_step"], 0)
            nc.vector.memset(ones[:, :], 1.0).then_inc(s["pad_ok"], 1)
            dve.wait_ge(s["c_in"], 16 * 7)
            dve.wait_ge(s["tot_ps"], 1)
            link(nc.vector.tensor_copy(ctot[:, :], XT[0][:, 0:E]))
            link(nc.vector.tensor_scalar(ntf[:, :], ctot[0:1, :], float(P - 1), None, ALU.add))
            link(nc.vector.tensor_copy(ni[:, 0, :], ntf[:, :]))
            link(nc.vector.tensor_single_scalar(ni[:, 1, :], ni[:, 0, :], 7, ALU.arith_shift_right))
            link(nc.vector.tensor_copy(ntf[:, :], ni[:, 1, :]))
            link(nc.vector.tensor_copy(cum[:, 0:1], ntf[:, 0:1]))
            for e in range(1, E):
                link(nc.vector.tensor_tensor(cum[:, e:e + 1], cum[:, e - 1:e], ntf[:, e:e + 1], ALU.add))
            link(nc.vector.tensor_scalar(gap[:, :], ntf[:, :], -float(P), float(REG), ALU.mult, ALU.add))
            tn = tc_[:, 0:TILES * E].rearrange("o (t e) -> o t e", e=E)
            link(nc.vector.tensor_tensor(ge[:, :, :], tn, cum[:, :].rearrange("o (a e) -> o a e", a=1).to_broadcast([1, TILES, E]),
                                         ALU.is_ge))
            link(nc.vector.tensor_tensor(gp[:, :, :], ge[:, :, :],
                                         gap[:, :].rearrange("o (a e) -> o a e", a=1).to_broadcast([1, TILES, E]), ALU.mult))
            link(nc.vector.tensor_reduce(tf[:, 0, :], ge[:, :, :], AX.X, ALU.add))
            link(nc.vector.tensor_reduce(tf[:, 1, :], gp[:, :, :], AX.X, ALU.add))
            link(nc.vector.scalar_tensor_tensor(out=tf[:, 1, :], in0=tn[:, :, 0], scalar=float(P), in1=tf[:, 1, :],
                                                op0=ALU.mult, op1=ALU.add))
            link(nc.vector.tensor_scalar(tf[:, 2, :], tf[:, 0, :], float(E) - 0.5, None, ALU.is_lt))
            for j in range(2):
                ins = nc.vector.tensor_tensor(tf[:, j, :], tf[:, j, :], tf[:, 2, :], ALU.mult)
            link(ins)
            link(nc.vector.tensor_scalar(tf[:, 2, :], tf[:, 2, :], -float(E * REG), float(E * REG), ALU.mult, ALU.add))
            link(nc.vector.tensor_tensor(tf[:, 1, :], tf[:, 1, :], tf[:, 2, :], ALU.add))
            link(nc.vector.tensor_tensor(zf[:, :], ctot[0:1, :], tc_[:, TILES * E:], ALU.add))
            nc.vector.tensor_copy(table[:, 0:2 * TILES], tf[:, 0:2, :].rearrange("o a t -> o (a t)"))
            nc.vector.tensor_copy(table[:, 2 * TILES:], zf[:, :]).then_inc(s["tab"], 1)
            dve.wait_ge(s["tab"], 1)

            def x_low(t, c):
                dve.wait_ge(s["xh_ok"], t + 1)
                nc.vector.tensor_tensor(xl[:, c % 2], XT[c % 2][:, 0:D].rearrange("p (k t) -> p k t", k=KD), xh[:, c % 2],
                                        ALU.subtract).then_inc(s["xl_ok"], 1)
                x_arrived(dve, t, c)
                await_(dve, s["y_ok"], t - (RING - 1))
                nc.vector.tensor_copy(gd[:, c, :], X[:, c, D:D + 2]).then_inc(s["gd_ok"], 1)

            def gelu_low(t, c, hb):
                f = slice(4 * hb, 4 * hb + 4)
                dve.wait_ge(s["hh_ok"], 2 * t + hb + 1)
                nc.vector.tensor_tensor(hl[:, c % 2, f, :], hf[:, c % 2, f, :], hh[:, c % 2, f, :], ALU.subtract).then_inc(s["hl_ok"], 1)

            CH = 3

            def residual(t, c, link):
                dve.wait_ge(s["o_ps"], t + 1)
                dve.wait_ge(s["xb_ok"], t + 1)
                nc.vector.scalar_tensor_tensor(out=r[:, :], in0=OP[c % 2][:, 0:D], scalar=1.0 / WSCALE, in1=xb[:, c % 2, :],
                                               op0=ALU.mult, op1=ALU.add).then_inc(s["r_ok"], 1)
                dve.wait_ge(s["r_ok"], t + 1)
                link(nc.vector.bn_stats(st[:, :], r[:, :]), alone=True)
                link(nc.vector.bn_aggr(mv[:, :], st[:, :]))
                nc.vector.tensor_scalar(ve[:, :], mv[:, 1:2], MOE_EPS, None, ALU.add).then_inc(s["ve_ok"], 1)

            def normed(t, c, link):
                dve.wait_ge(s["rs_ok"], t + 1)
                link(nc.vector.tensor_tensor(rg[:, :], rs[:, :], gd[:, c, 0:1], ALU.mult))
                await_(dve, s["y1_ok"], t)
                nc.vector.tensor_scalar(nrm[:, :], r[:, :], mv[:, 0:1], rg[:, :], ALU.subtract, ALU.mult).then_inc(s["nrm_ok"], 1)
                await_(dve, y_out[c % 2], 16 * (t // 2) if isinstance(t, int) else (t - c % 2) * 8)
                nc.vector.tensor_copy(du[:, c % 2, :], gd[:, c, 1:2])

            def shifted(t, c):
                e = expert_of(dve, t)
                dve.wait_ge(s["y1_ok"], t + 1)
                nc.vector.scalar_tensor_tensor(out=y[:, c % 2, :], in0=bet[:, :, :].rearrange("p e d -> p (e d)")[:, bass.ds(e * D, D)],
                                               scalar=gd[:, c, 0:1], in1=y1[:, :], op0=ALU.mult, op1=ALU.add).then_inc(s["y_ok"], 1)

            x_low(0, 0)

            def one(t, c):
                link = Chain(dve, s["norm_step2"], (t - 2) * CH, s["tab"])
                c2 = (c - 2) % RING
                if there(t) and there(t + 1):
                    x_low(t + 1, (c + 1) % RING)
                if there(t - 2):
                    residual(t - 2, c2, link)
                if there(t):
                    gelu_low(t, c, 0)
                if there(t - 2):
                    normed(t - 2, c2, link)
                if there(t):
                    gelu_low(t, c, 1)
                if there(t - 2):
                    shifted(t - 2, c2)
            rounds(dve, one)

        @block.gpsimd
        def _(pool):
            nc.gpsimd.memset(mhalf[:, :], -0.5).then_inc(s["half_ok"], 1)
            pool.wait_ge(s["half_ok"], 1)
            pool.wait_ge(s["tab"], 1)
            pool.wait_ge(s["c_in"], 16 * 7)

            def biased(t, c):
                e = expert_of(pool, t)
                x_arrived(pool, t, c)
                await_(pool, s["r_ok"], t - 1)
                nc.gpsimd.tensor_tensor(xb[:, c % 2, :], X[:, c, 0:D], b2s[:, :, :].rearrange("p e d -> p (e d)")[:, bass.ds(e * D, D)],
                                        ALU.add).then_inc(s["xb_ok"], 1)

            def rsqrt(t):
                pool.wait_ge(s["ve_ok"], t + 1)
                nc.gpsimd.tensor_tensor(rs[:, :], ve[:, :], mhalf[:, :], ALU.pow).then_inc(s["rs_ok"], 1)

            def scatter(t, c):
                wait_apart(pool, s["y_ok"], t + 1, s["tab"])
                nc.gpsimd.indirect_dma_start(
                    out=a["y_rows"], out_offset=bass.IndirectOffsetOnAxis(ap=du[:, c % 2, :], axis=0),
                    in_=y[:, c % 2, :], in_offset=None, bounds_check=2 * N - 1, oob_is_err=False).then_inc(y_out[c % 2], 16)

            def scaled(t):
                e = expert_of(pool, t)
                pool.wait_ge(s["nrm_ok"], t + 1)
                await_(pool, s["y_ok"], t)
                nc.gpsimd.tensor_tensor(y1[:, :], nrm[:, :], gam[:, :, :].rearrange("p e d -> p (e d)")[:, bass.ds(e * D, D)],
                                        ALU.mult).then_inc(s["y1_ok"], 1)

            def one(t, c):
                if there(t):
                    biased(t, c)
                if there(t - 2):
                    rsqrt(t - 2)
                if there(t - 3):
                    scatter(t - 3, (c - 3) % RING)
                if there(t - 2):
                    scaled(t - 2)
            rounds(pool, one)
            pool.wait_ge(y_out[0], 16 * ((TILES + 1) // 2))
            pool.wait_ge(y_out[1], 16 * (TILES // 2))


def stage_combine(nc, a):
    PR = 120
    ROWS = N // PR
    NCH = 11
    RC = ROWS // NCH
    with ExitStack() as ctx:
        sb = lambda n, s, d: ctx.enter_context(nc.sbuf_tensor(n, s, d))
        sem = lambda n: ctx.enter_context(nc.semaphore(n))
        h = sb("hc", [PR, ROWS, D], F32)
        y = sb("yc", [PR, ROWS, 2, D], F32)
        s_in = [sem(f"c_in{i}") for i in range(NCH)]
        sum_ok = sem("sum_ok")
        half_ok = sem("half_ok")
        out_done = sem("out_done")
        block = ctx.enter_context(nc.Block())
        hv = a["h2_rows"].rearrange("(p r) d -> p r d", p=PR)
        yv = a["y_rows"].rearrange("(p r c) d -> p r c d", p=PR, c=2)
        ov = a["out"].rearrange("b s d -> (b s) d").rearrange("(p r) d -> p r d", p=PR)

        @block.sync
        def _(sp):
            for i in range(NCH):
                r = slice(i * RC, (i + 1) * RC)
                sp.dma_start(y[:, r], yv[:, r]).then_inc(s_in[i], 16)
                sp.dma_start(h[:, r, :], hv[:, r, :]).then_inc(s_in[i], 16)

        @block.vector
        def _(dve):
            for i in range(NCH):
                r = slice(i * RC, (i + 1) * RC)
                dve.wait_ge(s_in[i], 32)
                nc.vector.tensor_tensor(h[:, r, :], h[:, r, :], y[:, r, 0, :], ALU.add).then_inc(half_ok, 1)
                dve.wait_ge(half_ok, i + 1)
                nc.vector.tensor_tensor(h[:, r, :], h[:, r, :], y[:, r, 1, :], ALU.add).then_inc(sum_ok, 1)

        @block.scalar
        def _(act):
            for i in range(NCH):
                r = slice(i * RC, (i + 1) * RC)
                act.wait_ge(sum_ok, i + 1)
                act.dma_start(ov[:, r, :], h[:, r, :]).then_inc(out_done, 16)
            act.wait_ge(out_done, 16 * NCH)


def build(nc, a):
    with ExitStack() as ctx:
        a["total"] = ctx.enter_context(nc.sbuf_tensor("total", [P, E], F32))
        stage_patches(nc, a["patch_t"], a["tok_w"], a["tok_b"], a["pe_rows"])
        with ExitStack() as w:
            sb = lambda n, s: w.enter_context(nc.sbuf_tensor(n, s, F16))
            wts = (sb("W1H", [P, E * KD, FF]), sb("W1L", [P, E * KD, FF]),
                   sb("W2H", [P, E * KF, D]), sb("W2L", [P, E * KF, D]))
            stage_attention(nc, a, wts)
            stage_experts(nc, a, wts)
        stage_combine(nc, a)


def constants():
    def bf16_bits(v):
        return (np.ascontiguousarray(v, dtype=np.float32).view(np.uint32) >> 16).astype(np.uint16)

    c = {}
    c["ident"] = np.eye(P, dtype=np.float32)
    c["ident_h"] = np.eye(P, dtype=np.float16)
    c["ident_b"] = bf16_bits(np.eye(P))
    q = np.arange(P)
    m = np.where(q[None, :] > q[:, None], np.float32(NEG), np.float32(0))
    c["mask_m"] = bf16_bits(m)
    mt = np.zeros((P, S), np.float32)
    for g in (0, 64):
        for i in range(TAIL):
            mt[g + i, P + i + 1:] = NEG
    c["mask_t"] = bf16_bits(mt)
    inv = (np.float32(10000.0) ** (np.arange(0, DK, 2, dtype=np.float32) / np.float32(DK))).astype(np.float32)
    ang = (np.arange(S, dtype=np.float32)[:, None] / inv[None, :]).astype(np.float32)
    cos, sin = np.cos(ang).astype(np.float32), np.sin(ang).astype(np.float32)
    ct = np.zeros((P, 2, DK // 2, 2), np.float32)
    st = np.zeros_like(ct)
    for half, n in ((0, P), (1, TAIL)):
        cc, ss = cos[half * P:half * P + n], sin[half * P:half * P + n]
        ct[:n, half] = cc[:, :, None]
        st[:n, half, :, 0] = -ss
        st[:n, half, :, 1] = ss
    c["cosT"] = (ct / np.float32(WSCALE)).reshape(P, 2, DK)
    c["sinT"] = (st / np.float32(WSCALE)).reshape(P, 2, DK)
    c["upper"] = bf16_bits(np.triu(np.ones((P, P), np.float32), 1))
    c["ones_b"] = bf16_bits(np.ones((P, P)))
    r = np.zeros((P, 24), np.float32)
    r[:, 0:E] = np.arange(E)
    r[:, 8:16] = np.arange(E) * REG
    r[TAIL:, 17] = 100.0
    for half in range(2):
        for k in range(2):
            r[:, 18 + 2 * half + k] = 2 * (half * P + q) + k
    c["route_c"] = r
    pad = np.zeros((P, XROW), np.float32)
    pad[:, D + 1] = 1.0e6
    c["pad"] = pad
    t = np.zeros((1, TILES * E + E), np.float32)
    t[0, :TILES * E] = np.repeat(np.arange(TILES), E)
    t[0, TILES * E:] = np.arange(E) * REG
    c["tile_c"] = t
    return c


def kernel(**inputs):
    import numpy as _np
    import concourse.bacc as _bacc
    from concourse import mybir as _mybir
    from concourse.bass_utils import run_bass_kernel_spmd as _run

    g = {k: _np.asarray(v) for k, v in inputs.items()}
    x = g["x"].reshape(NB, CH, GRID, PATCH, GRID, PATCH)
    arrays = {
        "patch_t": x.transpose(1, 3, 5, 0, 2, 4).reshape(CH * PATCH * PATCH, NB * NPATCH),
        "txt": g["txt"], "tok_w": g["L0_tok_W"], "tok_b": g["L0_tok_b"], "cls": g["L0_tok_cls_token"],
        "wqkv_t": g["L0_attn_W_qkv"].T, "wo_t": g["L0_attn_W_o"].T, "router": g["L0_ffn_router_w"],
        "w1": g["L0_ffn_w1"], "w2": g["L0_ffn_w2"], "b2": g["L0_ffn_b2"],
        "b1_t": g["L0_ffn_b1"].reshape(E, KF, P).transpose(2, 0, 1).reshape(P, E * KF),
        "gamma": g["L0_ffn_gamma"], "beta": g["L0_ffn_beta"],
    }
    arrays.update(constants())
    arrays = {n: _np.ascontiguousarray(v) for n, v in arrays.items()}
    nc = _bacc.Bacc("TRN2", target_bir_lowering=False, num_devices=1)
    a = {n: nc.dram_tensor("in_" + n, v.shape, _mybir.dt.from_np(v.dtype), kind="ExternalInput").ap() for n, v in arrays.items()}
    a["out"] = nc.dram_tensor("out_0", (NB, S, D), _mybir.dt.float32, kind="ExternalOutput").ap()
    a["pe_rows"] = nc.dram_tensor("pe_rows", (NB * NPATCH, D), _mybir.dt.float32).ap()
    a["h2_rows"] = nc.dram_tensor("h2_rows", (N, D), _mybir.dt.float32).ap()
    a["slots"] = nc.dram_tensor("slots", (E * REG + P, XROW), _mybir.dt.float32).ap()
    a["y_rows"] = nc.dram_tensor("y_rows", (2 * N, D), _mybir.dt.float32).ap()
    build(nc, a)
    r = _run(nc, [{"in_" + n: v for n, v in arrays.items()}], core_ids=[0])
    return r.results[0]["out_0"]
```

```python
from contextlib import ExitStack

import numpy as np
import concourse.bass as bass
from concourse import mybir

F32 = mybir.dt.float32
F16 = mybir.dt.float16
BF16 = mybir.dt.bfloat16
I32 = mybir.dt.int32
U32 = mybir.dt.uint32
ALU = mybir.AluOpType
ACT = mybir.ActivationFunctionType
AX = mybir.AxisListType

P = 128
NB, CH, IMG, PATCH = 16, 3, 96, 16
GRID = IMG // PATCH
NPATCH = GRID * GRID
KP = CH * PATCH * PATCH // P
D = 256
KD = D // P
TXT = 128
S = 1 + NPATCH + TXT
SR = S + 1
TAIL = S - P
HEAD = 1 + NPATCH
NH, DK = 16, 16
PAIRS = NH // 2
E, FF = 8, 1024
KF = FF // P
N = NB * S
TR = 2 * P
REG = N + TR
XROW = D + 2
TILES = (2 * N + E * (TR - 1)) // TR
WSCALE = 64.0
VSCALE = 8.0
NEG = -1.0e30
LN1_EPS = 1e-5
MOE_EPS = 1e-6
MSCALE = 16.0
TAIL_UNITS = [(0, 3, 3), (6, 1, 1)]
ST_UNITS = [(0, 3), (3, 3), (6, 2)]
SLOT = 64


def wait_apart(eng, sem, value, stood):
    if not isinstance(value, int):
        value = eng.to_reg(value)
    eng.wait_ge(stood, 1)
    eng.wait_ge(sem, value)


class Chain:

    def __init__(self, eng, sem, base, stood=None):
        self.eng, self.sem, self.base, self.stood, self.n = eng, sem, base, stood, 0

    def __call__(self, ins, alone=False):
        self.n += 1
        ins.then_inc(self.sem, 1)
        if alone:
            wait_apart(self.eng, self.sem, self.base + self.n, self.stood)
        else:
            self.eng.wait_ge(self.sem, self.base + self.n)


def stage_attention(nc, a, wts):
    W1H, W1L, W2H, W2L = wts
    with ExitStack() as ctx:
        sb = lambda n, s, d: ctx.enter_context(nc.sbuf_tensor(n, s, d))
        ps = lambda n, s, d=F32: ctx.enter_context(nc.psum_tensor(n, s, d))
        sem = lambda n: ctx.enter_context(nc.semaphore(n))

        ident = sb("ident", [P, P], F32)
        ident_h = sb("ident_h", [P, P], F16)
        ident_b = sb("ident_b", [P, P], BF16)
        mask_m = sb("mask_m", [P, P], BF16)
        mask_t = sb("mask_t", [P, S], BF16)
        cosT = sb("cosT", [P, 2, DK], F32)
        sinT = sb("sinT", [P, 2, DK], F32)
        upper = sb("upper", [P, P], BF16)
        ones_b = sb("ones_b", [P, 2], BF16)
        route_c = sb("route_c", [P, 24], F32)
        wq_h = sb("wq_h", [P, KD, 3 * D], F16)
        wq_l = sb("wq_l", [P, KD, 3 * D], F16)
        wo_h = sb("wo_h", [P, KD, D], F16)
        wo_l = sb("wo_l", [P, KD, D], F16)
        rw = sb("rw", [P, KD, E], F32)
        mhalf = sb("mhalf", [P, 2, 1], F32)
        consts = sb("consts", [P, 4], F32)
        H = sb("H", [P, 2, D], F32)
        st1 = sb("st1", [P, 2, 6], F32)
        mv1 = sb("mv1", [P, 2, 2], F32)
        ve1 = sb("ve1", [P, 2, 1], F32)
        rs1 = sb("rs1", [P, 2, 1], F32)
        xh = sb("xh", [P, KD, 2 * P], F16)
        xl = sb("xl", [P, KD, 2 * P], F16)
        rt1 = sb("rt1", [P, 2, 2 * D], F32)
        rt2 = sb("rt2", [P, 2, 2 * D], F32)
        xn = rt2[:, :, 0:D]
        blk = sb("blk", [P, 2, 2, NH, SLOT], F16)
        VH = sb("VH", [P, 2, 2, NH, DK + 1], F16)
        VL = sb("VL", [P, 2, 2, NH, DK + 1], F16)
        QA = sb("QA", [P, 2, PAIRS, SR], F16)
        KA = sb("KA", [P, 2, PAIRS, SR], F16)
        mx_m = sb("mx_m", [P, 2, PAIRS], F32)
        mx_t = sb("mx_t", [P, 8], F32)
        mT_m = sb("mT_m", [2 * PAIRS, P], F16)
        mT_t = sb("mT_t", [8, P], F16)
        PT = sb("PT", [P, 2, PAIRS, S], F32)
        PTt = sb("PTt", [P, 2, PAIRS, TAIL], F32)
        PH = sb("PH", [P, 2, PAIRS, S], F16)
        PL = PT[:, :, :, :].rearrange("p a j t -> p (a j t)").bitcast(F16)\
            .rearrange("p (a j t two) -> p a j t two", a=2, j=PAIRS, two=2)[:, :, :, :, 0]
        PLt = PTt[:, :, :, :].rearrange("p a j t -> p (a j t)").bitcast(F16)\
            .rearrange("p (a j t two) -> p a j t two", a=2, j=PAIRS, two=2)[:, :, :, :, 0]
        PHt = sb("PHt", [P, 2, PAIRS, TAIL], F16)
        rec = sb("rec", [P, 2, NH], F32)
        On = sb("On", [P, 2, D], F32)
        ohl = sb("ohl", [P, 2, KD, 2 * P], F16)
        oh, ol = ohl[:, 0], ohl[:, 1]
        x2T = ohl[:, :, :, :].rearrange("p a k t -> p (a k t)").bitcast(F32).rearrange("p (k t) -> p k t", k=KD)
        HR = sb("HR", [P, 2, D], F32)
        st2 = sb("st2", [P, 2, 6], F32)
        mv2 = sb("mv2", [P, 2, 2], F32)
        ve2 = sb("ve2", [P, 2, 1], F32)
        rs2 = sb("rs2", [P, 2, 1], F32)
        XR = sb("XR", [P, 2, 2, XROW], F32)
        lg = sb("lg", [P, 2, E], F32)
        m8 = sb("m8", [P, 2, 8], F32)
        i8 = sb("i8", [P, 2, 8], U32)
        idf = sb("idf", [P, 2, 2], F32)
        df = sb("df", [P, 2, 1], F32)
        ed = sb("ed", [P, 2, 1], F32)
        e1 = sb("e1", [P, 2, 1], F32)
        onehot = sb("onehot", [P, 2, 2, E], F32)
        cnt = sb("cnt", [P, 2, E], BF16)
        run = sb("run", [P, 2, E], F32)
        runb = sb("runb", [P, 2, E], BF16)
        rkb = sb("rkb", [P, 2, E], F32)
        prod = sb("prod", [P, 2, 2, E], F32)
        slotf = sb("slotf", [P, 2, 2], F32)
        slotu = sb("slotu", [P, 2, 2], U32)
        dest = sb("dest", [P, 2, 2], F32)
        stg = sb("stg", [P, FF], F32)
        small = PT[:, :, :, :].rearrange("p a j t -> p (a j t)")
        wq32 = small[:, 0:3 * D * KD].rearrange("p (k f) -> p k f", k=KD)
        wo32 = small[:, 3 * D * KD:4 * D * KD].rearrange("p (k f) -> p k f", k=KD)

        room = W2L[:, :, :].rearrange("p a d -> p (a d)").bitcast(F32)
        TOK = NB * NPATCH
        tok_tiles = [(t * P, min(P, TOK - t * P)) for t in range(-(-TOK // P))]
        cut = np.cumsum([0, KP * TOK, KP * D, D, len(tok_tiles) * D]).tolist()
        pt = room[:, cut[0]:cut[1]].rearrange("p (k n) -> p k n", k=KP)
        pw = room[:, cut[1]:cut[2]].rearrange("p (k d) -> p k d", k=KP)
        pb = room[:, cut[2]:cut[3]]
        emb = room[:, cut[3]:cut[4]].rearrange("p (t d) -> p t d", d=D)

        A6 = ps("A6", [P, 512])
        A7 = ps("A7", [P, 512])
        AQ = ps("AQ", [P, 2, 512])
        AS = [ps("AS0", [P, 512]), ps("AS1", [P, 512])]
        AT = [ps("AT0", [P, 512]), ps("AT1", [P, 512])]

        acc = [A7[:, 0:D], AQ[:, 0, 0:D], AQ[:, 1, 0:D], AS[0][:, 0:D], AS[1][:, 0:D]]

        names = ("tokw_in tokb_in emb_mm emb_ok pe_out const_in qwo_in h_in hr_in wst cleared ready wcv whi wlo "
                 "ve1_ok rs1_ok xn_ok xT_ps xh_ok xl_ok qk_ps v_ps v_ok rt_ok rope_ok hi_ok lo_ok "
                 "qa_ps qa_ev s_ps s_max mt_ps mt_ok mrow st_ps exp_ok sel_ok ph_ok pl_ok pl_odd_ok vl_ok pv_ps on_ok "
                 "ot_ps oh_ok ol_ok pj_ps h2_ok h2_out gate_step lgc_ok ve2_ok rs2_ok x2_ok x2b_ok x2t_ps x2t_ok "
                 "lg_ps df_ok ed_ok cnt_ok rk_ps slot_ok row_ok scattered norm_step route_step").split()
        s = {n: sem(n) for n in names}
        patch_in = [sem(f"patch_in{k}") for k in range(KP)]
        block = ctx.enter_context(nc.Block())

        def await_(eng, name, value):
            if isinstance(value, int) and value <= 0:
                return
            eng.wait_ge(s[name], value)

        def there(b):
            return not isinstance(b, int) or 0 <= b < NB

        def rounds(eng, one):
            for b in range(3):
                one(b, b % 2)
            with eng.Fori(0, (NB - 4) // 2) as g:
                one(g * 2 + 3, 1)
                one(g * 2 + 4, 0)
            for b in range(NB - 1, NB + 3):
                one(b, b % 2)

        CONSTS = [(ident, "ident"), (ident_h, "ident_h"), (ident_b, "ident_b"), (mask_m, "mask_m"), (mask_t, "mask_t"),
                  (cosT, "cosT"), (sinT, "sinT"), (upper, "upper"), (ones_b, "ones_b"), (route_c, "route_c")]

        @block.sync
        def _(sp):
            for k in range(KP):
                sp.dma_start(pt[:, k, :], a["patch_t"][k * P:(k + 1) * P, :]).then_inc(patch_in[k], 16)
            for t, n in CONSTS:
                dst = t[:].bitcast(mybir.dt.uint16) if t.dtype == BF16 else t[:]
                sp.dma_start(dst, a[n]).then_inc(s["const_in"], 16)
            sp.dma_start(rw[:, :, :], a["router"].rearrange("(k p) e -> p k e", p=P)).then_inc(s["const_in"], 16)
            txt = a["txt"].rearrange("b t d -> (b t) d")

            def load_rows(dst, b, landed):
                sp.dma_start(dst[0:1, 0, :], a["cls"].rearrange("a b d -> (a b) d")).then_inc(landed, 16)
                sp.dma_start(dst[1:HEAD, 0, :], a["pe_rows"][bass.ds(b * NPATCH, NPATCH), :]).then_inc(landed, 16)
                sp.dma_start(dst[HEAD:P, 0, :], txt[bass.ds(b * TXT, P - HEAD), :]).then_inc(landed, 16)
                sp.dma_start(dst[0:TAIL, 1, :], txt[bass.ds(b * TXT + P - HEAD, TAIL), :]).then_inc(landed, 16)

            def load_w1(b):
                sp.dma_start(stg[:, :].rearrange("p (a f) -> p a f", a=1),
                             a["w1"].rearrange("e (k p) f -> p (e k) f", p=P)[:, bass.ds(b, 1), :]).then_inc(s["wst"], 16)

            def load_w2(b):
                sp.dma_start(stg[:, :].rearrange("p (a f) -> p a f", a=4),
                             a["w2"].rearrange("e (k p) f -> p (e k) f", p=P)[:, bass.ds(b * 4, 4), :]).then_inc(s["wst"], 16)

            def move_maxima(b, par):
                sp.wait_ge(s["mt_ok"], 2 * b + 2)
                rows = QA[48:113:64, par]
                sp.dma_start(rows[:, :, 0:P], mT_m[:, :]).then_inc(s["mrow"], 16)
                for c, (a0, n, gap) in zip((0, 6), TAIL_UNITS):
                    for g in range(2):
                        sp.dma_start(rows[:, a0 + g * gap:a0 + g * gap + n, P:S],
                                     mT_t[c:c + 2 * n, 64 * g:64 * g + TAIL]).then_inc(s["mrow"], 16)

            def store_h2(b):
                sp.wait_ge(s["h2_ok"], b + 1)
                sp.dma_start(a["h2_rows"][bass.ds(b * S, P), :], HR[:, 0, :]).then_inc(s["h2_out"], 16)
                sp.dma_start(a["h2_rows"][bass.ds(b * S + P, TAIL), :], HR[0:TAIL, 1, :]).then_inc(s["h2_out"], 16)

            for t, (r0, n) in enumerate(tok_tiles):
                sp.wait_ge(s["emb_ok"], t + 1)
                sp.dma_start(a["pe_rows"][r0:r0 + n, :], emb[0:n, t, :]).then_inc(s["pe_out"], 16)
            sp.wait_ge(s["pe_out"], 16 * len(tok_tiles))
            sp.wait_ge(s["cleared"], 1)
            load_rows(H, 0, s["h_in"])
            load_w1(0)

            def one(b, par):
                if there(b + 1):
                    await_(sp, "xn_ok", b + 1)
                    load_rows(H, b + 1, s["h_in"])
                if there(b) and there(b - 1):
                    await_(sp, "wlo", 2 * b)
                    load_w1(b)
                if there(b - 3):
                    store_h2(b - 3)
                if there(b - 2):
                    normed, stored = b - 2, 32 * (b - 2)
                    if not isinstance(b, int):
                        normed, stored = sp.to_reg(normed), sp.to_reg(stored)
                    await_(sp, "x2_ok", normed)
                    await_(sp, "h2_out", stored)
                    load_rows(HR, b - 2, s["hr_in"])
                if there(b):
                    await_(sp, "wlo", 2 * b + 1)
                    load_w2(b)
                if there(b - 1):
                    move_maxima(b - 1, 1 - par)

            rounds(sp, one)
            sp.wait_ge(s["h2_out"], 32 * NB)

        @block.gpsimd
        def _(pool):
            nc.gpsimd.memset(H[:, 1, :], 0.0)
            nc.gpsimd.memset(HR[:, 1, :], 0.0)
            nc.gpsimd.memset(On[:, 1, :], 0.0)
            nc.gpsimd.memset(VH[:, :, :, :, DK:DK + 1], VSCALE)
            nc.gpsimd.memset(VL[:, :, :, :, DK:DK + 1], 0.0)
            nc.gpsimd.memset(run[:, :, :], 0.0)
            nc.gpsimd.memset(mhalf[:, :, :], -0.5)
            for i, v in enumerate((1.0, -1.0, 2.0 * S, 0.0)):
                nc.gpsimd.memset(consts[:, i:i + 1], v)
            nc.gpsimd.memset(blk[:, :, 0, :, 48:SLOT], 0.0)
            nc.gpsimd.memset(blk[:, :, 1, :, 48:49], MSCALE)
            nc.gpsimd.memset(blk[:, :, 1, :, 49:SLOT], 0.0).then_inc(s["cleared"], 1)
            pool.wait_ge(s["const_in"], 16 * (len(CONSTS) + 1))
            nc.gpsimd.tensor_copy(dest[:, :, :], route_c[:, 18:22].rearrange("p (a b) -> p a b", a=2)).then_inc(s["ready"], 1)
            pool.wait_ge(s["cleared"], 1)

            def rsqrt(ve, rs, done, wanted, b):
                pool.wait_ge(s[wanted], b + 1)
                nc.gpsimd.tensor_tensor(rs[:, :, :], ve[:, :, :], mhalf[:, :, :], ALU.pow).then_inc(s[done], 1)

            def rope(b):
                pool.wait_ge(s["rt_ok"], 3 * b + 3)
                await_(pool, "hi_ok", 4 * b)
                nc.gpsimd.tensor_tensor(rt1[:, :, :], rt1[:, :, :], rt2[:, :, :], ALU.add).then_inc(s["rope_ok"], 1)

            def lows(b):
                pool.wait_ge(s["hi_ok"], 4 * b + 4)
                r = rt1[:, :, :].rearrange("p a (q h d) -> p a q h d", q=2, h=NH)
                for q, slot in ((0, 2), (1, 1)):
                    nc.gpsimd.tensor_tensor(blk[:, :, q, :, slot * DK:(slot + 1) * DK], r[:, :, q],
                                            blk[:, :, q, :, 0:DK], ALU.subtract).then_inc(s["lo_ok"], 1)

            def select(b, units):
                for u in units:
                    a0, n = ST_UNITS[u // 2]
                    wait_apart(pool, s["exp_ok"], 8 * b + u + 1, s["cleared"])
                    v = PT[:, u % 2, a0:a0 + n, 0:P]
                    nc.gpsimd.affine_select(out=v, in_=v, compare_op=ALU.is_ge, fill=0.0, base=0,
                                            pattern=[[0, n], [1, P]], channel_multiplier=-1).then_inc(s["sel_ok"], 1)

            def select_tail(b):
                wait_apart(pool, s["exp_ok"], 8 * b + 8, s["cleared"])
                v = PTt[0:TAIL, :, :, :].rearrange("p a j t -> p (a j) t")
                nc.gpsimd.affine_select(out=v, in_=v, compare_op=ALU.is_ge, fill=0.0, base=0,
                                        pattern=[[0, 2 * PAIRS], [1, TAIL]], channel_multiplier=-1).then_inc(s["sel_ok"], 1)

            def weights_low(b):
                pool.wait_ge(s["ph_ok"], 3 * b + 2)
                nc.gpsimd.tensor_tensor(PL[:, 1], PT[:, 1], PH[:, 1], ALU.subtract).then_inc(s["pl_odd_ok"], 1)
                pool.wait_ge(s["ph_ok"], 3 * b + 3)
                nc.gpsimd.tensor_tensor(PLt[0:TAIL], PTt[0:TAIL], PHt[0:TAIL], ALU.subtract).then_inc(s["pl_odd_ok"], 1)

            def gates(b):
                pool.wait_ge(s["ed_ok"], b + 1)
                await_(pool, "scattered", 64 * b)
                nc.gpsimd.tensor_tensor(e1[:, :, :], ed[:, :, :], consts[:, 0:1].rearrange("p (o a) -> p o a", o=1).to_broadcast([P, 2, 1]),
                                        ALU.add).then_inc(s["gate_step"], 1)
                pool.wait_ge(s["gate_step"], 4 * b + 1)
                nc.gpsimd.tensor_tensor(XR[:, :, 0, D:D + 1], e1[:, :, :],
                                        consts[:, 1:2].rearrange("p (o a) -> p o a", o=1).to_broadcast([P, 2, 1]),
                                        ALU.pow).then_inc(s["gate_step"], 1)
                pool.wait_ge(s["gate_step"], 4 * b + 2)
                nc.gpsimd.tensor_tensor(XR[:, :, 1, D:D + 1], XR[:, :, 0, D:D + 1], ed[:, :, :], ALU.mult).then_inc(s["gate_step"], 1)
                step = consts[:, 2:3].rearrange("p (o a) -> p o a", o=1).to_broadcast([P, 2, 2])
                nc.gpsimd.tensor_tensor(dest[:, :, :], dest[:, :, :], step, ALU.add).then_inc(s["gate_step"], 1)
                pool.wait_ge(s["gate_step"], 4 * b + 4)
                nc.gpsimd.tensor_tensor(XR[:, :, :, D + 1:D + 2].rearrange("p a c o -> p a (c o)"), dest[:, :, :],
                                        consts[:, 3:4].rearrange("p (o a) -> p o a", o=1).to_broadcast([P, 2, 2]), ALU.add).then_inc(s["row_ok"], 1)

            def scatter(b):
                wait_apart(pool, s["row_ok"], b + 1, s["cleared"])
                pool.wait_ge(s["x2b_ok"], b + 1)
                pool.wait_ge(s["slot_ok"], b + 1)
                for half, n in ((0, P), (1, TAIL)):
                    for c in range(2):
                        nc.gpsimd.indirect_dma_start(
                            out=a["slots"], out_offset=bass.IndirectOffsetOnAxis(ap=slotu[0:n, half, c:c + 1], axis=0),
                            in_=XR[0:n, half, c, :], in_offset=None).then_inc(s["scattered"], 16)

            rsqrt(ve1, rs1, "rs1_ok", "ve1_ok", 0)

            def one(b, par):
                if there(b + 1) and there(b):
                    rsqrt(ve1, rs1, "rs1_ok", "ve1_ok", b + 1)
                if there(b - 3):
                    rsqrt(ve2, rs2, "rs2_ok", "ve2_ok", b - 3)
                if there(b - 2):
                    select(b - 2, range(6))
                    select_tail(b - 2)
                if there(b):
                    rope(b)
                if there(b - 2):
                    weights_low(b - 2)
                if there(b):
                    lows(b)
                if there(b - 3):
                    gates(b - 3)
                    scatter(b - 3)

            rounds(pool, one)
            pool.wait_ge(s["scattered"], 64 * NB)

        @block.scalar
        def _(act):
            act.dma_start(pw, a["tok_w"].rearrange("(k p) d -> p k d", p=P)).then_inc(s["tokw_in"], 16)
            act.dma_start(pb, a["tok_b"].rearrange("(a d) -> a d", a=1).to_broadcast([P, D])).then_inc(s["tokb_in"], 16)
            act.dma_start(wq32, a["wqkv_t"].rearrange("(k p) f -> p k f", p=P)).then_inc(s["qwo_in"], 16)
            act.dma_start(wo32, a["wo_t"].rearrange("(k p) f -> p k f", p=P)).then_inc(s["qwo_in"], 16)
            act.wait_ge(s["qwo_in"], 32)
            nc.scalar.activation(wq_h[:, :, :], wq32, ACT.Copy, scale=WSCALE).then_inc(s["wcv"], 1)
            nc.scalar.activation(wo_h[:, :, :], wo32, ACT.Copy, scale=WSCALE).then_inc(s["wcv"], 1)
            act.wait_ge(s["cleared"], 1)
            act.wait_ge(s["wcv"], 4)

            def x_high(b):
                act.wait_ge(s["xT_ps"], b + 1)
                nc.scalar.activation(xh[:, :, :], A6[:, :].rearrange("p (k t) -> p k t", k=KD), ACT.Copy).then_inc(s["xh_ok"], 1)

            def v_copy(b, par):
                act.wait_ge(s["v_ps"], b + 1)
                await_(act, "pv_ps", b - 1)
                nc.scalar.activation(VH[:, par, :, :, 0:DK], A6[:, :].rearrange("p (a h d) -> p a h d", a=2, h=NH),
                                     ACT.Copy, scale=VSCALE / WSCALE).then_inc(s["v_ok"], 1)

            def highs(b):
                act.wait_ge(s["rope_ok"], b + 1)
                await_(act, "qa_ps", 4 * b)
                r = rt1[:, :, :].rearrange("p a (q h d) -> p a q h d", q=2, h=NH)
                for q, slot in ((0, 0), (1, 0), (0, 1), (1, 2)):
                    nc.scalar.activation(blk[:, :, q, :, slot * DK:(slot + 1) * DK], r[:, :, q], ACT.Copy).then_inc(s["hi_ok"], 1)

            def qa_evac(b, par, q):
                for u in range(2):
                    act.wait_ge(s["qa_ps"], 4 * b + 2 * q + u + 1)
                    await_(act, "st_ps", 8 * (b - 1))
                    src = AQ[:, u, :].bitcast(F16)[:, 0:4 * SR].rearrange("p (j t) -> p j t", j=4)[:, :, 0:S]
                    nc.scalar.activation((QA, KA)[q][:, par, 4 * u:4 * u + 4, 0:S], src, ACT.Copy).then_inc(s["qa_ev"], 1)

            def exps(b):
                await_(act, "pv_ps", b)
                u = 0
                for a0, n in ST_UNITS:
                    for odd in range(2):
                        u += 1
                        act.wait_ge(s["st_ps"], 8 * b + u)
                        nc.scalar.activation(PT[:, odd, a0:a0 + n, :],
                                             AT[odd][:, 0:n * S].rearrange("p (j t) -> p j t", j=n),
                                             ACT.Exp, scale=DK ** -0.5).then_inc(s["exp_ok"], 1)
                for odd in range(2):
                    u += 1
                    act.wait_ge(s["st_ps"], 8 * b + u)
                    nc.scalar.activation(PTt[0:TAIL, odd, :, :],
                                         AT[odd][0:TAIL, 0:PAIRS * TAIL].rearrange("p (j t) -> p j t", j=PAIRS),
                                         ACT.Exp, scale=DK ** -0.5).then_inc(s["exp_ok"], 1)

            def weights_high(b):
                for odd in range(2):
                    act.wait_ge(s["sel_ok"], 7 * b + 5 + odd)
                    nc.scalar.activation(PH[:, odd], PT[:, odd], ACT.Copy).then_inc(s["ph_ok"], 1)
                act.wait_ge(s["sel_ok"], 7 * b + 7)
                nc.scalar.activation(PHt[0:TAIL], PTt[0:TAIL], ACT.Copy).then_inc(s["ph_ok"], 1)

            def w_high(b, which):
                act.wait_ge(s["wst"], 32 * b + 16 * which + 16)
                n, high = ((1, W1H), (4, W2H))[which]
                nc.scalar.activation(high[:, bass.ds(b * n, n), :], stg[:, :].rearrange("p (a f) -> p a f", a=n),
                                     ACT.Copy, scale=WSCALE).then_inc(s["whi"], 1)

            def o_high(b):
                act.wait_ge(s["ot_ps"], b + 1)
                nc.scalar.activation(oh, A7[:, :].rearrange("p (k t) -> p k t", k=KD), ACT.Copy).then_inc(s["oh_ok"], 1)

            def x2_turned(b):
                act.wait_ge(s["x2t_ps"], b + 1)
                nc.scalar.activation(x2T, A7[:, :].rearrange("p (k t) -> p k t", k=KD), ACT.Copy).then_inc(s["x2t_ok"], 1)

            def x2_copy(b):
                act.wait_ge(s["x2_ok"], b + 1)
                nc.scalar.activation(XR[:, :, 1, 0:D], XR[:, :, 0, 0:D], ACT.Copy).then_inc(s["x2b_ok"], 1)

            def logits_copy(b):
                act.wait_ge(s["lg_ps"], b + 1)
                nc.scalar.activation(lg[:, :, :], A7[:, 0:2 * E].rearrange("p (a e) -> p a e", a=2), ACT.Copy).then_inc(s["lgc_ok"], 1)

            def gate_exp(b):
                act.wait_ge(s["df_ok"], b + 1)
                nc.scalar.activation(ed[:, :, :], df[:, :, :], ACT.Exp).then_inc(s["ed_ok"], 1)

            def one(b, par):
                if there(b - 1):
                    qa_evac(b - 1, 1 - par, 0)
                if there(b):
                    x_high(b)
                if there(b - 1):
                    qa_evac(b - 1, 1 - par, 1)
                if there(b - 3):
                    o_high(b - 3)
                if there(b - 1):
                    w_high(b - 1, 1)
                if there(b - 2):
                    exps(b - 2)
                if there(b - 3):
                    x2_turned(b - 3)
                    x2_copy(b - 3)
                if there(b - 2):
                    weights_high(b - 2)
                if there(b):
                    highs(b)
                if there(b - 3):
                    logits_copy(b - 3)
                    gate_exp(b - 3)
                if there(b):
                    w_high(b, 0)
                    v_copy(b, par)

            rounds(act, one)

        @block.vector
        def _(dve):
            dve.wait_ge(s["wcv"], 2)
            nc.vector.scalar_tensor_tensor(out=wq_l[:, :, :], in0=wq32, scalar=WSCALE, in1=wq_h[:, :, :],
                                           op0=ALU.mult, op1=ALU.subtract).then_inc(s["wcv"], 1)
            nc.vector.scalar_tensor_tensor(out=wo_l[:, :, :], in0=wo32, scalar=WSCALE, in1=wo_h[:, :, :],
                                           op0=ALU.mult, op1=ALU.subtract).then_inc(s["wcv"], 1)
            dve.wait_ge(s["tokb_in"], 16)
            for t, (r0, n) in enumerate(tok_tiles):
                dve.wait_ge(s["emb_mm"], t + 1)
                nc.vector.tensor_tensor(emb[0:n, t, :], acc[t][0:n, :], pb[0:n, :], ALU.add).then_inc(s["emb_ok"], 1)
            dve.wait_ge(s["const_in"], 16 * (len(CONSTS) + 1))
            dve.wait_ge(s["cleared"], 1)
            dve.wait_ge(s["ready"], 1)

            def stats(link, src, st, mv, ve):
                for half in range(2):
                    ins = nc.vector.bn_stats(st[:, half, :], src[:, half, :])
                link(ins, alone=True)
                for half in range(2):
                    ins = nc.vector.bn_aggr(mv[:, half, :], st[:, half, :])
                link(ins)
                return nc.vector.tensor_scalar(ve[:, :, :], mv[:, :, 1:2], LN1_EPS, None, ALU.add)

            def normed(src, mv, rs, dst):
                for half in range(2):
                    ins = nc.vector.tensor_scalar(dst[:, half], src[:, half, :], mv[:, half, 0:1], rs[:, half, :],
                                                  ALU.subtract, ALU.mult)
                return ins

            def norm1_stats(b):
                link = Chain(dve, s["norm_step"], b * 2, s["cleared"])
                dve.wait_ge(s["h_in"], 64 * b + 64)
                stats(link, H, st1, mv1, ve1).then_inc(s["ve1_ok"], 1)

            def norm1_apply(b):
                await_(dve, "rope_ok", b)
                dve.wait_ge(s["rs1_ok"], b + 1)
                normed(H, mv1, rs1, xn).then_inc(s["xn_ok"], 1)

            def x_low(b):
                dve.wait_ge(s["xh_ok"], b + 1)
                nc.vector.tensor_tensor(xl[:, :, :], A6[:, :].rearrange("p (k t) -> p k t", k=KD), xh[:, :, :],
                                        ALU.subtract).then_inc(s["xl_ok"], 1)

            def rotate(b):
                dve.wait_ge(s["qk_ps"], 2 * b + 2)
                await_(dve, "lo_ok", 2 * b)

                def heads(v):
                    return v.rearrange("p a (h n two) -> p a h n two", h=2 * NH, two=2)

                def table(v, which):
                    v = v[:, :, :].rearrange("p a (o n two) -> p a o n two", o=1, two=2)[:, :, :, :, which]
                    return v.to_broadcast([P, 2, 2 * NH, DK // 2])
                cs = cosT[:, :, :].rearrange("p a (o n) -> p a o n", o=1).to_broadcast([P, 2, 2 * NH, DK])
                nc.vector.tensor_tensor(rt1[:, :, :].rearrange("p a (h n) -> p a h n", n=DK),
                                        AQ[:, :, :].rearrange("p a (h n) -> p a h n", n=DK), cs, ALU.mult).then_inc(s["rt_ok"], 1)
                for even in range(2):
                    nc.vector.tensor_tensor(heads(rt2[:, :, :])[:, :, :, :, even], heads(AQ[:, :, :])[:, :, :, :, 1 - even],
                                            table(sinT, even), ALU.mult).then_inc(s["rt_ok"], 1)

            def maxima(b):
                u = 0
                for r in range(2):
                    for odd in range(2):
                        u += 1
                        dve.wait_ge(s["s_ps"], 8 * b + u)
                        nc.vector.tensor_reduce(mx_m[:, odd, 4 * r:4 * r + 4],
                                                AS[odd][:, :].rearrange("p (j t) -> p j t", j=4), AX.X, ALU.max).then_inc(s["s_max"], 1)
                for c0, (a0, n, gap) in zip((0, 6), TAIL_UNITS):
                    for odd in range(2):
                        u += 1
                        dve.wait_ge(s["s_ps"], 8 * b + u)
                        nc.vector.tensor_reduce(mx_t[:, c0 + odd * n:c0 + odd * n + n],
                                                AS[odd][:, 0:n * S].rearrange("p (j t) -> p j t", j=n), AX.X, ALU.max).then_inc(s["s_max"], 1)

            def weights_low(b):
                dve.wait_ge(s["ph_ok"], 3 * b + 1)
                nc.vector.tensor_tensor(PL[:, 0], PT[:, 0], PH[:, 0], ALU.subtract).then_inc(s["pl_ok"], 1)

            def v_low(b, par):
                dve.wait_ge(s["v_ok"], b + 1)
                nc.vector.scalar_tensor_tensor(out=VL[:, par, :, :, 0:DK], in0=A6[:, :].rearrange("p (a h d) -> p a h d", a=2, h=NH),
                                               scalar=VSCALE / WSCALE, in1=VH[:, par, :, :, 0:DK],
                                               op0=ALU.mult, op1=ALU.subtract).then_inc(s["vl_ok"], 1)

            def maxima_turned(b):
                dve.wait_ge(s["mt_ps"], b + 1)
                nc.vector.tensor_scalar(mT_m[:, :], AS[0][0:2 * PAIRS, 0:P], -1.0 / MSCALE, None, ALU.mult).then_inc(s["mt_ok"], 1)
                nc.vector.tensor_scalar(mT_t[:, :], AS[0][0:8, P:2 * P], -1.0 / MSCALE, None, ALU.mult).then_inc(s["mt_ok"], 1)

            def w_low(b, which):
                dve.wait_ge(s["whi"], 2 * b + which + 1)
                n, high, low = ((1, W1H, W1L), (4, W2H, W2L))[which]
                nc.vector.scalar_tensor_tensor(out=low[:, bass.ds(b * n, n), :], in0=stg[:, :].rearrange("p (a f) -> p a f", a=n),
                                               scalar=WSCALE, in1=high[:, bass.ds(b * n, n), :],
                                               op0=ALU.mult, op1=ALU.subtract).then_inc(s["wlo"], 1)

            RS = 11

            def o_norm(b):
                dve.wait_ge(s["pv_ps"], b + 1)
                await_(dve, "ot_ps", b)
                sums = [AT[half][:, 0:NH * (DK + 1)].rearrange("p (h d) -> p h d", h=NH) for half in range(2)]
                nc.vector.reciprocal(rec[:, 0, :], sums[0][:, :, DK]).then_inc(s["on_ok"], 1)
                nc.vector.reciprocal(rec[0:TAIL, 1, :], sums[1][0:TAIL, :, DK]).then_inc(s["on_ok"], 1)
                dve.wait_ge(s["on_ok"], 4 * b + 2)
                for half, n in ((0, P), (1, TAIL)):
                    nc.vector.tensor_tensor(On[0:n, half, :].rearrange("p (h d) -> p h d", h=NH), sums[half][0:n, :, 0:DK],
                                            rec[0:n, half, :].rearrange("p (h a) -> p h a", a=1).to_broadcast([n, NH, DK]),
                                            ALU.mult).then_inc(s["on_ok"], 1)

            def o_low(b):
                dve.wait_ge(s["oh_ok"], b + 1)
                nc.vector.tensor_tensor(ol, A7[:, :].rearrange("p (k t) -> p k t", k=KD), oh,
                                        ALU.subtract).then_inc(s["ol_ok"], 1)

            def residual(b, link):
                dve.wait_ge(s["pj_ps"], b + 1)
                dve.wait_ge(s["hr_in"], 64 * b + 64)
                nc.vector.scalar_tensor_tensor(out=HR[:, :, :], in0=A7[:, :].rearrange("p (a t) -> p a t", a=2),
                                               scalar=1.0 / WSCALE, in1=HR[:, :, :], op0=ALU.mult, op1=ALU.add).then_inc(s["h2_ok"], 1)
                dve.wait_ge(s["h2_ok"], b + 1)
                stats(link, HR, st2, mv2, ve2).then_inc(s["ve2_ok"], 1)

            def norm2_apply(b):
                await_(dve, "scattered", 64 * b)
                dve.wait_ge(s["rs2_ok"], b + 1)
                normed(HR, mv2, rs2, XR[:, :, 0, 0:D]).then_inc(s["x2_ok"], 1)

            def choose(b, link):
                wait_apart(dve, s["lgc_ok"], b + 1, s["cleared"])
                for half in range(2):
                    ins = nc.vector.max(m8[:, half, :], lg[:, half, :])
                link(ins, alone=True)
                for half in range(2):
                    ins = nc.vector.max_index(i8[:, half, :], m8[:, half, :], lg[:, half, :])
                link(ins)
                nc.vector.tensor_tensor(df[:, :, :], m8[:, :, 1:2], m8[:, :, 0:1], ALU.subtract).then_inc(s["df_ok"], 1)
                link(nc.vector.tensor_tensor(idf[:, :, :], i8[:, :, 0:2],
                                             route_c[:, 16:18].rearrange("p (a o) -> p a o", o=1).to_broadcast([P, 2, 2]), ALU.add))
                for half in range(2):
                    for c in range(2):
                        ins = nc.vector.tensor_scalar(onehot[:, half, c, :], route_c[:, 0:E], idf[:, half, c:c + 1], None, ALU.is_equal)
                link(ins)
                link(nc.vector.tensor_tensor(cnt[:, :, :], onehot[:, :, 0, :], onehot[:, :, 1, :], ALU.add))
                link(nc.vector.tensor_tensor(run[:, 1, :], run[:, 0, :], cnt[:, 0, :], ALU.add))
                nc.vector.tensor_copy(runb[:, :, :], run[:, :, :]).then_inc(s["cnt_ok"], 1)
                dve.wait_ge(s["cnt_ok"], b + 1)
                nc.vector.tensor_tensor(run[:, 0, :], run[:, 1, :], cnt[:, 1, :], ALU.add)

            def place(b, link):
                dve.wait_ge(s["rk_ps"], b + 1)
                link(nc.vector.tensor_tensor(rkb[:, :, :], A7[:, 32:32 + 2 * E].rearrange("p (a e) -> p a e", a=2),
                                             route_c[:, 8:16].rearrange("p (o e) -> p o e", o=1).to_broadcast([P, 2, E]), ALU.add))
                for c in range(2):
                    ins = nc.vector.tensor_tensor(prod[:, :, c, :], onehot[:, :, c, :], rkb[:, :, :], ALU.mult)
                link(ins)
                link(nc.vector.tensor_reduce(slotf[:, :, :], prod[:, :, :, :], AX.X, ALU.add))
                nc.vector.tensor_copy(slotu[:, :, :], slotf[:, :, :]).then_inc(s["slot_ok"], 1)

            norm1_stats(0)
            norm1_apply(0)

            def one(b, par):
                link = Chain(dve, s["route_step"], (b - 3) * RS, s["cleared"])
                if there(b):
                    x_low(b)
                if there(b - 3):
                    o_low(b - 3)
                if there(b - 1):
                    w_low(b - 1, 1)
                if there(b + 1) and there(b):
                    norm1_stats(b + 1)
                if there(b - 3):
                    residual(b - 3, link)
                    norm2_apply(b - 3)
                if there(b):
                    rotate(b)
                if there(b - 1):
                    maxima(b - 1)
                if there(b - 2):
                    weights_low(b - 2)
                if there(b + 1) and there(b):
                    norm1_apply(b + 1)
                if there(b - 3):
                    choose(b - 3, link)
                if there(b):
                    w_low(b, 0)
                if there(b - 1):
                    maxima_turned(b - 1)
                if there(b):
                    v_low(b, par)
                if there(b - 3):
                    place(b - 3, link)
                    assert link.n == RS, link.n
                if there(b - 2):
                    o_norm(b - 2)

            rounds(dve, one)
            nc.vector.tensor_copy(a["total"][:, :], run[:, 0, :])

        @block.tensor
        def _(pe):
            mm = nc.tensor.matmul
            pe.wait_ge(s["tokw_in"], 16)
            for k in range(KP):
                pe.wait_ge(patch_in[k], 16)
                for t, (r0, n) in enumerate(tok_tiles):
                    ins = mm(acc[t][0:n, :], pt[:, k, r0:r0 + n], pw[:, k, :], start=(k == 0), stop=(k == KP - 1))
                    if k == KP - 1:
                        ins.then_inc(s["emb_mm"], 1)
            pe.wait_ge(s["const_in"], 16 * (len(CONSTS) + 1))
            pe.wait_ge(s["wcv"], 4)
            pe.wait_ge(s["cleared"], 1)

            def three(out, xh_, xl_, wh_, wl_, start, stop):
                mm(out, xh_, wh_, start=start, stop=False)
                mm(out, xh_, wl_, start=False, stop=False)
                return mm(out, xl_, wh_, start=False, stop=stop)

            def turn(dst, src, done):
                for k in range(KD):
                    for half in range(2):
                        ins = nc.tensor.transpose(dst[:, k * 2 * P + half * P:k * 2 * P + half * P + P],
                                                  src[:, half, k * P:(k + 1) * P], ident[:, :])
                ins.then_inc(s[done], 1)

            def x_turn(b):
                pe.wait_ge(s["xn_ok"], b + 1)
                await_(pe, "vl_ok", b)
                turn(A6, xn, "xT_ps")

            def project_qk(b, half):
                if half == 0:
                    pe.wait_ge(s["xl_ok"], b + 1)
                    await_(pe, "qa_ev", 4 * b)
                for k in range(KD):
                    t = slice(half * P, half * P + P)
                    ins = three(AQ[:, half, :], xh[:, k, t], xl[:, k, t], wq_h[:, k, 0:2 * D], wq_l[:, k, 0:2 * D],
                                k == 0, k == KD - 1)
                ins.then_inc(s["qk_ps"], 1)

            def project_v(b):
                for half in range(2):
                    for k in range(KD):
                        t = slice(half * P, half * P + P)
                        ins = three(A6[:, half * D:(half + 1) * D], xh[:, k, t], xl[:, k, t],
                                    wq_h[:, k, 2 * D:3 * D], wq_l[:, k, 2 * D:3 * D], k == 0, k == KD - 1)
                ins.then_inc(s["v_ps"], 1)

            def qa_turn(b, q):
                if q == 0:
                    pe.wait_ge(s["lo_ok"], 2 * b + 2)
                else:
                    pe.wait_ge(s["qa_ev"], 4 * b + 2)
                for u in (2 * q, 2 * q + 1):
                    j0 = 4 * (u % 2)
                    out = AQ[:, u % 2, :].bitcast(F16)
                    for j in range(4):
                        for half, n in ((0, P), (1, TAIL)):
                            src = blk[0:n, half, q, 2 * (j0 + j):2 * (j0 + j) + 2, :].rearrange("p h d -> p (h d)")
                            ins = nc.tensor.transpose(out[:, j * SR + half * P:j * SR + half * P + n], src, ident_h[0:n, 0:n])
                    ins.then_inc(s["qa_ps"], 1)

            def wait_bank(b, u):
                await_(pe, "s_max", 8 * b + (u - 2))

            def scores(b, par):
                pe.wait_ge(s["qa_ev"], 4 * b + 4)
                await_(pe, "mt_ok", 2 * b)
                u = 0
                for r in range(2):
                    for odd in range(2):
                        u += 1
                        wait_bank(b, u)
                        mm(AS[odd][:, :].rearrange("p (j t) -> p j t", j=4), ident_b[:, :],
                           mask_m[:, :].rearrange("p (j t) -> p j t", j=1).to_broadcast([P, 4, P]), start=True, stop=False,
                           skip_group_check=True)
                        rows = slice(64 * odd, 64 * odd + 64)
                        for j in range(4):
                            ins = mm(AS[odd][:, j * P:(j + 1) * P], QA[rows, par, 4 * r + j, 0:P], KA[rows, par, 4 * r + j, 0:P],
                                     start=False, stop=(j == 3), skip_group_check=True)
                        ins.then_inc(s["s_ps"], 1)
                for a0, n, gap in TAIL_UNITS:
                    for odd in range(2):
                        u += 1
                        wait_bank(b, u)
                        mm(AS[odd][:, 0:n * S].rearrange("p (j t) -> p j t", j=n), ident_b[:, :],
                           mask_t[:, :].rearrange("p (j t) -> p j t", j=1).to_broadcast([P, n, S]),
                           start=True, stop=False, skip_group_check=True)
                        rows = slice(64 * odd, 64 * odd + 64)
                        for g in range(2):
                            for j in range(n):
                                jj = a0 + g * gap + j
                                ins = mm(AS[odd][64 * g:64 * g + TAIL, j * S:(j + 1) * S], QA[rows, par, jj, P:S],
                                         KA[rows, par, jj, 0:S], start=False, stop=True, skip_group_check=True)
                        ins.then_inc(s["s_ps"], 1)

            def maxima_turn(b):
                pe.wait_ge(s["s_max"], 8 * b + 8)
                nc.tensor.transpose(AS[0][0:2 * PAIRS, 0:P], mx_m[:, :, :].rearrange("p a j -> p (a j)"), ident[:, :])
                nc.tensor.transpose(AS[0][0:8, P:2 * P], mx_t[:, :], ident[:, :]).then_inc(s["mt_ps"], 1)

            def scores_turned(b, par, units):
                for u in units:
                    odd = u % 2
                    rows = slice(64 * odd, 64 * odd + 64)
                    if u >= 2:
                        wait_apart(pe, s["exp_ok"], 8 * b + u - 1, s["cleared"])
                    elif u == 0:
                        await_(pe, "on_ok", 4 * b)
                        wait_apart(pe, s["mrow"], 80 * b + 80, s["cleared"])
                    if u < 6:
                        a0, n = ST_UNITS[u // 2]
                        for j in range(n):
                            ins = mm(AT[odd][:, j * S:(j + 1) * S], KA[rows, par, a0 + j, 0:P], QA[rows, par, a0 + j, 0:S],
                                     start=True, stop=True, skip_group_check=True)
                    else:
                        for j in range(PAIRS):
                            ins = mm(AT[odd][0:TAIL, j * TAIL:(j + 1) * TAIL], KA[rows, par, j, P:S], QA[rows, par, j, P:S],
                                     start=True, stop=True, skip_group_check=True)
                    ins.then_inc(s["st_ps"], 1)

            def values(b, par):
                w = DK + 1
                pe.wait_ge(s["vl_ok"], b + 1)
                for odd in range(2):
                    pe.wait_ge(*((s["pl_ok"], b + 1), (s["pl_odd_ok"], 2 * b + 1))[odd])
                    for h in range(odd, NH, 2):
                        wh, wl = PH[:, odd, h // 2, 0:P], PL[:, odd, h // 2, 0:P]
                        out = AT[0][:, h * w:(h + 1) * w]
                        mm(out, wh, VH[:, par, 0, h, :], start=True, stop=False, skip_group_check=True)
                        mm(out, wh, VL[:, par, 0, h, :], start=False, stop=False, skip_group_check=True)
                        mm(out, wl, VH[:, par, 0, h, :], start=False, stop=True, skip_group_check=True)

            def values_tail(b, par):
                w = DK + 1
                pe.wait_ge(s["pl_odd_ok"], 2 * b + 2)
                for h in range(NH):
                    odd, j = h % 2, h // 2
                    out = AT[1][0:TAIL, h * w:(h + 1) * w]
                    for n, wh, wl, half in ((P, PH[:, odd, j, P:S], PL[:, odd, j, P:S], 0),
                                            (TAIL, PHt[0:TAIL, odd, j, :], PLt[0:TAIL, odd, j, :], 1)):
                        mm(out, wh, VH[0:n, par, half, h, :], start=(half == 0), stop=False, skip_group_check=True)
                        mm(out, wh, VL[0:n, par, half, h, :], start=False, stop=False, skip_group_check=True)
                        ins = mm(out, wl, VH[0:n, par, half, h, :], start=False, stop=(half == 1), skip_group_check=True)
                ins.then_inc(s["pv_ps"], 1)

            def o_turn(b):
                pe.wait_ge(s["on_ok"], 4 * b + 4)
                await_(pe, "slot_ok", b)
                turn(A7, On, "ot_ps")

            def project(b):
                pe.wait_ge(s["ol_ok"], b + 1)
                for half in range(2):
                    for k in range(KD):
                        t = slice(half * P, half * P + P)
                        ins = three(A7[:, half * D:(half + 1) * D], oh[:, k, t], ol[:, k, t], wo_h[:, k, :], wo_l[:, k, :],
                                    k == 0, k == KD - 1)
                ins.then_inc(s["pj_ps"], 1)

            def x2_turn(b):
                pe.wait_ge(s["x2_ok"], b + 1)
                turn(A7, XR[:, :, 0, 0:D], "x2t_ps")

            def logits(b):
                pe.wait_ge(s["x2t_ok"], b + 1)
                for half in range(2):
                    for k in range(KD):
                        ins = mm(A7[:, half * E:(half + 1) * E], x2T[:, k, half * P:(half + 1) * P], rw[:, k, :],
                                 start=(k == 0), stop=(k == KD - 1))
                ins.then_inc(s["lg_ps"], 1)

            def ranks(b):
                pe.wait_ge(s["cnt_ok"], b + 1)
                for half in range(2):
                    out = A7[:, 32 + half * E:32 + (half + 1) * E]
                    mm(out, upper[:, :], cnt[:, half, :], start=True, stop=False)
                    ins = mm(out, ones_b[:, 0:1].to_broadcast([P, P]), runb[:, half, :], start=False, stop=True)
                ins.then_inc(s["rk_ps"], 1)

            def one(b, par):
                if there(b - 1):
                    qa_turn(b - 1, 0)
                if there(b):
                    x_turn(b)
                if there(b - 1):
                    qa_turn(b - 1, 1)
                if there(b - 3):
                    o_turn(b - 3)
                if there(b):
                    project_qk(b, 0)
                if there(b - 2):
                    scores_turned(b - 2, par, (0, 1))
                if there(b - 3):
                    project(b - 3)
                if there(b - 2):
                    scores_turned(b - 2, par, (2, 3))
                if there(b):
                    project_qk(b, 1)
                if there(b):
                    project_v(b)
                if there(b - 2):
                    scores_turned(b - 2, par, (4, 5))
                if there(b - 2):
                    scores_turned(b - 2, par, (6, 7))
                if there(b - 3):
                    x2_turn(b - 3)
                if there(b - 1):
                    scores(b - 1, 1 - par)
                if there(b - 3):
                    logits(b - 3)
                if there(b - 1):
                    maxima_turn(b - 1)
                if there(b - 2):
                    values(b - 2, par)
                    values_tail(b - 2, par)
                if there(b - 3):
                    ranks(b - 3)

            rounds(pe, one)


RING = 4
FB = 2


def stage_experts(nc, a, wts):
    W1H, W1L, W2H, W2L = wts
    with ExitStack() as ctx:
        sb = lambda n, s, d: ctx.enter_context(nc.sbuf_tensor(n, s, d))
        sem = lambda n: ctx.enter_context(nc.semaphore(n))
        ident = sb("ident2", [P, P], F32)
        ones = sb("ones2", [P, P], F32)
        gam = sb("gam", [P, E, D], F32)
        bet = sb("bet", [P, E, D], F32)
        b2s = sb("b2s", [P, E, D], F32)
        b1s = sb("b1s", [P, E * KF], F32)
        pad = sb("pad", [P, XROW], F32)
        tc_ = sb("tc_", [1, TILES * E + E], F32)
        ctot = sb("ctot", [P, E], F32)
        ni = sb("ni", [1, 2, E], I32)
        ntf = sb("ntf", [1, E], F32)
        cum = sb("cum", [1, 4, 2 * E], F32)
        gap = sb("gap", [1, E], F32)
        ge = sb("ge", [1, TILES, E], F32)
        gp = sb("gp", [1, TILES, E], F32)
        tf = sb("tf", [1, 3, TILES], F32)
        zf = sb("zf", [1, E], F32)
        table = sb("table", [1, 2 * TILES], I32)
        ends = sb("ends", [1, E], I32)
        X = sb("X", [P, RING, 2, XROW], F32)
        gd = sb("gd", [P, RING, 2, 2], F32)
        xh = sb("xh2", [P, 2, KD, TR], F16)
        xl = sb("xl2", [P, 2, KD, TR], F16)
        hf = sb("hf", [P, KF, TR], F32)
        hh = sb("hh", [P, 2, KF, TR], F16)
        hl = sb("hl", [P, 2, KF, TR], F16)
        xb = sb("xb", [P, 2, 2, D], F32)
        r = sb("r", [P, 2, D], F32)
        st = sb("st", [P, 2, 6], F32)
        mv = sb("mv", [P, 2, 2], F32)
        rs = sb("rs", [P, 2, 1], F32)
        rg = sb("rg", [P, 2, 1], F32)
        ve = sb("ve", [P, 2, 1], F32)
        mhalf = sb("mhalf2", [P, 2, 1], F32)
        nrm = sb("nrm", [P, 2, D], F32)
        y = sb("y", [P, 2, 2, D], F32)
        du = sb("du", [P, 2, 2, 1], U32)
        XT = [ctx.enter_context(nc.psum_tensor(f"XT{i}", [P, KD, TR], F32)) for i in range(2)]
        HP = [ctx.enter_context(nc.psum_tensor(f"HP{i}", [P, FB, TR], F32)) for i in range(KF // FB)]
        OP = [ctx.enter_context(nc.psum_tensor(f"OP{i}", [P, 2, D], F32)) for i in range(2)]
        names = ("ve_ok rs_ok half_ok c_in params_in ends_ok tab tot_ps pad_ok pads xt_ps xh_ok xl_ok gd_ok h_ps h_ok hh_ok hl_ok o_ps xb_ok r_ok "
                 "setup_step norm_step2 nrm_ok scaled_ok y_ok y_out0 y_out1").split()
        s = {n: sem(n) for n in names}
        x_in = [sem(f"x_in_{i}") for i in range(RING)]
        y_out = [s["y_out0"], s["y_out1"]]
        block = ctx.enter_context(nc.Block())

        def rounds(eng, one):
            for t in range(RING):
                one(t, t)
            fours = (TILES - 1) // RING
            with eng.Fori(1, fours) as g:
                for c in range(RING):
                    one(g * RING + c, c)
            for t in range(fours * RING, TILES + 3):
                one(t, t % RING)

        def there(t):
            return not isinstance(t, int) or 0 <= t < TILES

        def await_(eng, sem_, value):
            if isinstance(value, int) and value <= 0:
                return
            eng.wait_ge(sem_, value)

        def expert_of(eng, t):
            return eng.value_load(table[0:1, bass.ds(t, 1)], min_val=0, max_val=E - 1)

        def x_arrived(eng, t, c):
            eng.wait_ge(x_in[c], 16 * (t // RING + 1) if isinstance(t, int) else (t + (RING - c)) * (16 // RING))

        def two_halves(rows):
            return rows.rearrange("(h p) c -> p h c", p=P)

        pads = pad[:, :].rearrange("p (h c) -> p h c", h=1).to_broadcast([P, 2, XROW])

        def store_pads(eng, experts):
            for e in experts:
                z = eng.value_load(ends[0:1, e:e + 1], min_val=0, max_val=E * REG - TR)
                eng.dma_start(two_halves(a["slots"][bass.ds(z, TR), :]), pads).then_inc(s["pads"], 16)

        @block.sync
        def _(sp):
            for dst, n in ((tc_, "tile_c"), (ident, "ident"), (b1s, "b1_t"), (pad, "pad")):
                sp.dma_start(dst[:, :], a[n]).then_inc(s["c_in"], 16)
            sp.wait_ge(s["c_in"], 16 * 4)
            sp.dma_start(two_halves(a["slots"][E * REG:E * REG + TR, :]), pads).then_inc(s["pads"], 16)
            sp.wait_ge(s["ends_ok"], 1)
            store_pads(sp, range(E // 2))
            sp.wait_ge(s["tab"], 1)
            sp.wait_ge(s["pads"], 16 * (E + 1))

            def load(t, c):
                row = sp.value_load(table[0:1, bass.ds(t + TILES, 1)], min_val=0, max_val=E * REG)
                free = t - (RING - 1)
                if not isinstance(t, int):
                    free = sp.to_reg(free)
                await_(sp, s["xt_ps"], free)
                await_(sp, s["gd_ok"], free)
                await_(sp, s["xb_ok"], free)
                sp.dma_start(X[:, c], two_halves(a["slots"][bass.ds(row, TR), :])).then_inc(x_in[c], 16)

            def one(t, c):
                if there(t):
                    load(t, c)
            rounds(sp, one)

        @block.tensor
        def _(pe):
            mm = nc.tensor.matmul
            pe.wait_ge(s["pad_ok"], 1)
            mm(XT[0][:, 0, 0:E], ones[:, :], a["total"][:, :], start=True, stop=True).then_inc(s["tot_ps"], 1)
            pe.wait_ge(s["c_in"], 16 * 4)
            pe.wait_ge(s["tab"], 1)

            def turn(t, c):
                x_arrived(pe, t, c)
                await_(pe, s["xl_ok"], t - 1)
                for k in range(KD):
                    for half in range(2):
                        ins = nc.tensor.transpose(XT[c % 2][:, k, half * P:(half + 1) * P], X[:, c, half, k * P:(k + 1) * P], ident[:, :])
                ins.then_inc(s["xt_ps"], 1)

            def up(t, c, e):
                par = c % 2
                pe.wait_ge(s["xl_ok"], t + 1)
                for bank in range(KF // FB):
                    await_(pe, s["h_ok"], (t - 1) * (KF // FB) + bank + 1)
                    for f in range(FB):
                        for k in range(KD):
                            off = k * FF + (bank * FB + f) * P
                            wh = W1H[:, :, :].rearrange("p a f -> p (a f)")[:, bass.ds(e * (KD * FF) + off, P)]
                            wl = W1L[:, :, :].rearrange("p a f -> p (a f)")[:, bass.ds(e * (KD * FF) + off, P)]
                            out = HP[bank][:, f, :]
                            mm(out, wh, xh[:, par, k, :], start=(k == 0), stop=False)
                            mm(out, wh, xl[:, par, k, :], start=False, stop=False)
                            ins = mm(out, wl, xh[:, par, k, :], start=False, stop=(k == KD - 1))
                    ins.then_inc(s["h_ps"], 1)

            def down(t, c, e):
                par = c % 2
                await_(pe, s["r_ok"], t - 1)
                for half in range(2):
                    rows = slice(half * P, (half + 1) * P)
                    for f in range(KF):
                        if half == 0 and f % FB == 0:
                            pe.wait_ge(s["hl_ok"], (KF // FB) * t + f // FB + 1)
                        wh = W2H[:, :, :].rearrange("p a f -> p (a f)")[:, bass.ds(e * (KF * D) + f * D, D)]
                        wl = W2L[:, :, :].rearrange("p a f -> p (a f)")[:, bass.ds(e * (KF * D) + f * D, D)]
                        mm(OP[par][:, half, :], hh[:, par, f, rows], wh, start=(f == 0), stop=False)
                        mm(OP[par][:, half, :], hh[:, par, f, rows], wl, start=False, stop=False)
                        ins = mm(OP[par][:, half, :], hl[:, par, f, rows], wh, start=False, stop=(f == KF - 1))
                ins.then_inc(s["o_ps"], 1)

            turn(0, 0)
            expert = {}

            def one(t, c):
                before = (c - 1) % RING
                if there(t - 1) and (before not in expert or c == 0):
                    expert[before] = expert_of(pe, t - 1)
                if there(t):
                    expert[c] = expert_of(pe, t)
                if there(t) and there(t + 1):
                    turn(t + 1, (c + 1) % RING)
                if there(t):
                    up(t, c, expert[c])
                if there(t - 1):
                    down(t - 1, before, expert[before])
            rounds(pe, one)

        @block.scalar
        def _(act):
            act.wait_ge(s["c_in"], 16 * 4)
            act.wait_ge(s["ends_ok"], 1)
            store_pads(act, range(E // 2, E))
            for dst, n in ((b2s, "b2"), (gam, "gamma"), (bet, "beta")):
                act.dma_start(dst[:, :, :].rearrange("p e d -> p (e d)"),
                              a[n].rearrange("(o e) d -> o (e d)", o=1).to_broadcast([P, E * D])).then_inc(s["params_in"], 16)
            act.wait_ge(s["tab"], 1)

            def x_high(t, c):
                act.wait_ge(s["xt_ps"], t + 1)
                await_(act, s["h_ps"], (KF // FB) * (t - 1))
                nc.scalar.activation(xh[:, c % 2], XT[c % 2][:, :, :], ACT.Copy).then_inc(s["xh_ok"], 1)

            def gelu(t, c, bank, e):
                n = (KF // FB) * t + bank + 1
                act.wait_ge(s["h_ps"], n)
                await_(act, s["hl_ok"], n - KF // FB)
                for f in range(FB):
                    ins = nc.scalar.activation(hf[:, bank * FB + f, :], HP[bank][:, f, :], ACT.Gelu,
                                               bias=b1s[:, bass.ds(e * KF + (bank * FB + f), 1)], scale=1.0 / WSCALE)
                ins.then_inc(s["h_ok"], 1)

            def gelu_high(t, c, bank):
                if bank == 0:
                    await_(act, s["o_ps"], t - 1)
                act.wait_ge(s["h_ok"], (KF // FB) * t + bank + 1)
                f = slice(FB * bank, FB * bank + FB)
                nc.scalar.activation(hh[:, c % 2, f, :], hf[:, f, :], ACT.Copy).then_inc(s["hh_ok"], 1)

            x_high(0, 0)

            def one(t, c):
                if there(t) and there(t + 1):
                    x_high(t + 1, (c + 1) % RING)
                if there(t):
                    e = expert_of(act, t)
                    for bank in range(KF // FB):
                        gelu(t, c, bank, e)
                        gelu_high(t, c, bank)
            rounds(act, one)

        @block.vector
        def _(dve):
            link = Chain(dve, s["setup_step"], 0)
            nc.vector.memset(ones[:, :], 1.0).then_inc(s["pad_ok"], 1)
            dve.wait_ge(s["c_in"], 16 * 4)
            dve.wait_ge(s["tot_ps"], 1)
            link(nc.vector.tensor_copy(ctot[:, :], XT[0][:, 0, 0:E]))
            link(nc.vector.tensor_tensor(zf[:, :], ctot[0:1, :], tc_[:, TILES * E:], ALU.add))
            nc.vector.tensor_copy(ends[:, :], zf[:, :]).then_inc(s["ends_ok"], 1)
            link(nc.vector.tensor_scalar(ntf[:, :], ctot[0:1, :], float(TR - 1), None, ALU.add))
            link(nc.vector.tensor_copy(ni[:, 0, :], ntf[:, :]))
            link(nc.vector.tensor_single_scalar(ni[:, 1, :], ni[:, 0, :], TR.bit_length() - 1, ALU.arith_shift_right))
            link(nc.vector.tensor_copy(ntf[:, :], ni[:, 1, :]))
            link(nc.vector.memset(cum[:, :, 0:E], 0.0))
            link(nc.vector.tensor_copy(cum[:, 0, E:2 * E], ntf[:, :]))
            for i, d in enumerate((1, 2, 4)):
                link(nc.vector.tensor_tensor(cum[:, i + 1, E:2 * E], cum[:, i, E:2 * E], cum[:, i, E - d:2 * E - d], ALU.add))
            link(nc.vector.tensor_scalar(gap[:, :], ntf[:, :], -float(TR), float(REG), ALU.mult, ALU.add))
            tn = tc_[:, 0:TILES * E].rearrange("o (t e) -> o t e", e=E)
            link(nc.vector.tensor_tensor(ge[:, :, :], tn, cum[:, 3, E:2 * E].rearrange("o (a e) -> o a e", a=1).to_broadcast([1, TILES, E]),
                                         ALU.is_ge))
            link(nc.vector.tensor_tensor(gp[:, :, :], ge[:, :, :],
                                         gap[:, :].rearrange("o (a e) -> o a e", a=1).to_broadcast([1, TILES, E]), ALU.mult))
            link(nc.vector.tensor_reduce(tf[:, 0, :], ge[:, :, :], AX.X, ALU.add))
            link(nc.vector.tensor_reduce(tf[:, 1, :], gp[:, :, :], AX.X, ALU.add))
            link(nc.vector.scalar_tensor_tensor(out=tf[:, 1, :], in0=tn[:, :, 0], scalar=float(TR), in1=tf[:, 1, :],
                                                op0=ALU.mult, op1=ALU.add))
            link(nc.vector.tensor_scalar(tf[:, 2, :], tf[:, 0, :], float(E) - 0.5, None, ALU.is_lt))
            for j in range(2):
                ins = nc.vector.tensor_tensor(tf[:, j, :], tf[:, j, :], tf[:, 2, :], ALU.mult)
            link(ins)
            link(nc.vector.tensor_scalar(tf[:, 2, :], tf[:, 2, :], -float(E * REG), float(E * REG), ALU.mult, ALU.add))
            link(nc.vector.tensor_tensor(tf[:, 1, :], tf[:, 1, :], tf[:, 2, :], ALU.add))
            nc.vector.tensor_copy(table[:, :], tf[:, 0:2, :].rearrange("o a t -> o (a t)")).then_inc(s["tab"], 1)
            dve.wait_ge(s["tab"], 1)

            def x_low(t, c):
                dve.wait_ge(s["xh_ok"], t + 1)
                nc.vector.tensor_tensor(xl[:, c % 2], XT[c % 2][:, :, :], xh[:, c % 2],
                                        ALU.subtract).then_inc(s["xl_ok"], 1)
                x_arrived(dve, t, c)
                await_(dve, s["y_ok"], t - (RING - 1))
                nc.vector.tensor_copy(gd[:, c], X[:, c, :, D:D + 2]).then_inc(s["gd_ok"], 1)

            def gelu_low(t, c, banks):
                for bank in banks:
                    f = slice(FB * bank, FB * bank + FB)
                    dve.wait_ge(s["hh_ok"], (KF // FB) * t + bank + 1)
                    nc.vector.tensor_tensor(hl[:, c % 2, f, :], hf[:, f, :], hh[:, c % 2, f, :], ALU.subtract).then_inc(s["hl_ok"], 1)

            CH = 3

            def residual(t, c, link):
                dve.wait_ge(s["o_ps"], t + 1)
                dve.wait_ge(s["xb_ok"], t + 1)
                nc.vector.scalar_tensor_tensor(out=r[:, :, :], in0=OP[c % 2][:, :, :], scalar=1.0 / WSCALE, in1=xb[:, c % 2],
                                               op0=ALU.mult, op1=ALU.add).then_inc(s["r_ok"], 1)
                dve.wait_ge(s["r_ok"], t + 1)
                for half in range(2):
                    ins = nc.vector.bn_stats(st[:, half, :], r[:, half, :])
                link(ins, alone=True)
                for half in range(2):
                    ins = nc.vector.bn_aggr(mv[:, half, :], st[:, half, :])
                link(ins)
                nc.vector.tensor_scalar(ve[:, :, :], mv[:, :, 1:2], MOE_EPS, None, ALU.add).then_inc(s["ve_ok"], 1)

            def normed(t, c, link):
                dve.wait_ge(s["rs_ok"], t + 1)
                link(nc.vector.tensor_tensor(rg[:, :, :], rs[:, :, :], gd[:, c, :, 0:1], ALU.mult))
                await_(dve, s["y_ok"], t)
                for half in range(2):
                    ins = nc.vector.tensor_scalar(nrm[:, half, :], r[:, half, :], mv[:, half, 0:1], rg[:, half, :],
                                                  ALU.subtract, ALU.mult)
                ins.then_inc(s["nrm_ok"], 1)
                await_(dve, y_out[c % 2], 32 * (t // 2) if isinstance(t, int) else (t - c % 2) * 16)
                nc.vector.tensor_copy(du[:, c % 2], gd[:, c, :, 1:2])

            def shifted(t, c):
                e = expert_of(dve, t)
                dve.wait_ge(s["scaled_ok"], t + 1)
                for half in range(2):
                    ins = nc.vector.scalar_tensor_tensor(out=y[:, c % 2, half, :],
                                                         in0=bet[:, :, :].rearrange("p e d -> p (e d)")[:, bass.ds(e * D, D)],
                                                         scalar=gd[:, c, half, 0:1], in1=nrm[:, half, :], op0=ALU.mult, op1=ALU.add)
                ins.then_inc(s["y_ok"], 1)

            dve.wait_ge(s["params_in"], 16 * 3)
            x_low(0, 0)

            def one(t, c):
                link = Chain(dve, s["norm_step2"], (t - 2) * CH, s["tab"])
                c2 = (c - 2) % RING
                if there(t) and there(t + 1):
                    x_low(t + 1, (c + 1) % RING)
                if there(t - 2):
                    residual(t - 2, c2, link)
                if there(t):
                    gelu_low(t, c, (0, 1))
                if there(t - 2):
                    normed(t - 2, c2, link)
                if there(t):
                    gelu_low(t, c, (2, 3))
                if there(t - 2):
                    shifted(t - 2, c2)
            rounds(dve, one)

        @block.gpsimd
        def _(pool):
            nc.gpsimd.memset(mhalf[:, :, :], -0.5).then_inc(s["half_ok"], 1)
            pool.wait_ge(s["half_ok"], 1)
            pool.wait_ge(s["tab"], 1)
            pool.wait_ge(s["params_in"], 16 * 3)

            def of_expert(table_, e):
                row = table_[:, :, :].rearrange("p e d -> p (e d)")[:, bass.ds(e * D, D)]
                return row.rearrange("p (h d) -> p h d", h=1).to_broadcast([P, 2, D])

            def biased(t, c):
                e = expert_of(pool, t)
                x_arrived(pool, t, c)
                await_(pool, s["r_ok"], t - 1)
                nc.gpsimd.tensor_tensor(xb[:, c % 2], X[:, c, :, 0:D], of_expert(b2s, e), ALU.add).then_inc(s["xb_ok"], 1)

            def rsqrt(t):
                pool.wait_ge(s["ve_ok"], t + 1)
                nc.gpsimd.tensor_tensor(rs[:, :, :], ve[:, :, :], mhalf[:, :, :], ALU.pow).then_inc(s["rs_ok"], 1)

            def scatter(t, c):
                wait_apart(pool, s["y_ok"], t + 1, s["tab"])
                for half in range(2):
                    nc.gpsimd.indirect_dma_start(
                        out=a["y_rows"], out_offset=bass.IndirectOffsetOnAxis(ap=du[:, c % 2, half, :], axis=0),
                        in_=y[:, c % 2, half, :], in_offset=None, bounds_check=2 * N - 1, oob_is_err=False).then_inc(y_out[c % 2], 16)

            def scaled(t):
                e = expert_of(pool, t)
                pool.wait_ge(s["nrm_ok"], t + 1)
                nc.gpsimd.tensor_tensor(nrm[:, :, :], nrm[:, :, :], of_expert(gam, e), ALU.mult).then_inc(s["scaled_ok"], 1)

            def one(t, c):
                if there(t):
                    biased(t, c)
                if there(t - 2):
                    rsqrt(t - 2)
                if there(t - 3):
                    scatter(t - 3, (c - 3) % RING)
                if there(t - 2):
                    scaled(t - 2)
            rounds(pool, one)
            pool.wait_ge(y_out[0], 32 * ((TILES + 1) // 2))
            pool.wait_ge(y_out[1], 32 * (TILES // 2))


def stage_combine(nc, a):
    PR = 120
    ROWS = N // PR
    NCH = 11
    RC = ROWS // NCH
    with ExitStack() as ctx:
        sb = lambda n, s, d: ctx.enter_context(nc.sbuf_tensor(n, s, d))
        sem = lambda n: ctx.enter_context(nc.semaphore(n))
        h = sb("hc", [PR, ROWS, D], F32)
        y = sb("yc", [PR, ROWS, 2, D], F32)
        s_in = [sem(f"c_in{i}") for i in range(NCH)]
        sum_ok = sem("sum_ok")
        half_ok = sem("half_ok")
        out_done = sem("out_done")
        block = ctx.enter_context(nc.Block())
        hv = a["h2_rows"].rearrange("(p r) d -> p r d", p=PR)
        yv = a["y_rows"].rearrange("(p r c) d -> p r c d", p=PR, c=2)
        ov = a["out"].rearrange("b s d -> (b s) d").rearrange("(p r) d -> p r d", p=PR)

        @block.sync
        def _(sp):
            for i in range(NCH):
                r = slice(i * RC, (i + 1) * RC)
                sp.dma_start(y[:, r], yv[:, r]).then_inc(s_in[i], 16)
                sp.dma_start(h[:, r, :], hv[:, r, :]).then_inc(s_in[i], 16)

        @block.vector
        def _(dve):
            for i in range(NCH):
                r = slice(i * RC, (i + 1) * RC)
                dve.wait_ge(s_in[i], 32)
                nc.vector.tensor_tensor(h[:, r, :], h[:, r, :], y[:, r, 0, :], ALU.add).then_inc(half_ok, 1)
                dve.wait_ge(half_ok, i + 1)
                nc.vector.tensor_tensor(h[:, r, :], h[:, r, :], y[:, r, 1, :], ALU.add).then_inc(sum_ok, 1)

        @block.scalar
        def _(act):
            for i in range(NCH):
                r = slice(i * RC, (i + 1) * RC)
                act.wait_ge(sum_ok, i + 1)
                act.dma_start(ov[:, r, :], h[:, r, :]).then_inc(out_done, 16)
            act.wait_ge(out_done, 16 * NCH)


def build(nc, a):
    with ExitStack() as ctx:
        a["total"] = ctx.enter_context(nc.sbuf_tensor("total", [P, E], F32))
        with ExitStack() as w:
            sb = lambda n, s: w.enter_context(nc.sbuf_tensor(n, s, F16))
            wts = (sb("W1H", [P, E * KD, FF]), sb("W1L", [P, E * KD, FF]),
                   sb("W2H", [P, E * KF, D]), sb("W2L", [P, E * KF, D]))
            stage_attention(nc, a, wts)
            stage_experts(nc, a, wts)
        stage_combine(nc, a)


def constants():
    def bf16_bits(v):
        return (np.ascontiguousarray(v, dtype=np.float32).view(np.uint32) >> 16).astype(np.uint16)

    c = {}
    c["ident"] = np.eye(P, dtype=np.float32)
    c["ident_h"] = np.eye(P, dtype=np.float16)
    c["ident_b"] = bf16_bits(np.eye(P))
    q = np.arange(P)
    m = np.where(q[None, :] > q[:, None], np.float32(NEG), np.float32(0))
    c["mask_m"] = bf16_bits(m)
    mt = np.zeros((P, S), np.float32)
    for g in (0, 64):
        for i in range(TAIL):
            mt[g + i, P + i + 1:] = NEG
    c["mask_t"] = bf16_bits(mt)
    inv = (np.float32(10000.0) ** (np.arange(0, DK, 2, dtype=np.float32) / np.float32(DK))).astype(np.float32)
    ang = (np.arange(S, dtype=np.float32)[:, None] / inv[None, :]).astype(np.float32)
    cos, sin = np.cos(ang).astype(np.float32), np.sin(ang).astype(np.float32)
    ct = np.zeros((P, 2, DK // 2, 2), np.float32)
    st = np.zeros_like(ct)
    for half, n in ((0, P), (1, TAIL)):
        cc, ss = cos[half * P:half * P + n], sin[half * P:half * P + n]
        ct[:n, half] = cc[:, :, None]
        st[:n, half, :, 0] = -ss
        st[:n, half, :, 1] = ss
    c["cosT"] = (ct / np.float32(WSCALE)).reshape(P, 2, DK)
    c["sinT"] = (st / np.float32(WSCALE)).reshape(P, 2, DK)
    c["upper"] = bf16_bits(np.triu(np.ones((P, P), np.float32), 1))
    c["ones_b"] = bf16_bits(np.ones((P, 2)))
    r = np.zeros((P, 24), np.float32)
    r[:, 0:E] = np.arange(E)
    r[:, 8:16] = np.arange(E) * REG
    r[TAIL:, 17] = 100.0
    for half in range(2):
        for k in range(2):
            r[:, 18 + 2 * half + k] = 2 * (half * P + q) + k - 2 * S
    c["route_c"] = r
    pad = np.zeros((P, XROW), np.float32)
    pad[:, D + 1] = 1.0e6
    c["pad"] = pad
    t = np.zeros((1, TILES * E + E), np.float32)
    t[0, :TILES * E] = np.repeat(np.arange(TILES), E)
    t[0, TILES * E:] = np.arange(E) * REG
    c["tile_c"] = t
    return c


def kernel(**inputs):
    import numpy as _np
    import concourse.bacc as _bacc
    from concourse import mybir as _mybir
    from concourse.bass_utils import run_bass_kernel_spmd as _run

    g = {k: _np.asarray(v) for k, v in inputs.items()}
    x = g["x"].reshape(NB, CH, GRID, PATCH, GRID, PATCH)
    arrays = {
        "patch_t": x.transpose(1, 3, 5, 0, 2, 4).reshape(CH * PATCH * PATCH, NB * NPATCH),
        "txt": g["txt"], "tok_w": g["L0_tok_W"], "tok_b": g["L0_tok_b"], "cls": g["L0_tok_cls_token"],
        "wqkv_t": g["L0_attn_W_qkv"].T, "wo_t": g["L0_attn_W_o"].T, "router": g["L0_ffn_router_w"],
        "w1": g["L0_ffn_w1"], "w2": g["L0_ffn_w2"], "b2": g["L0_ffn_b2"],
        "b1_t": g["L0_ffn_b1"].reshape(E, KF, P).transpose(2, 0, 1).reshape(P, E * KF),
        "gamma": g["L0_ffn_gamma"], "beta": g["L0_ffn_beta"],
    }
    arrays.update(constants())
    arrays = {n: _np.ascontiguousarray(v) for n, v in arrays.items()}
    nc = _bacc.Bacc("TRN2", target_bir_lowering=False, num_devices=1)
    a = {n: nc.dram_tensor("in_" + n, v.shape, _mybir.dt.from_np(v.dtype), kind="ExternalInput").ap() for n, v in arrays.items()}
    a["out"] = nc.dram_tensor("out_0", (NB, S, D), _mybir.dt.float32, kind="ExternalOutput").ap()
    a["pe_rows"] = nc.dram_tensor("pe_rows", (NB * NPATCH, D), _mybir.dt.float32).ap()
    a["h2_rows"] = nc.dram_tensor("h2_rows", (N, D), _mybir.dt.float32).ap()
    a["slots"] = nc.dram_tensor("slots", (E * REG + TR, XROW), _mybir.dt.float32).ap()
    a["y_rows"] = nc.dram_tensor("y_rows", (2 * N, D), _mybir.dt.float32).ap()
    build(nc, a)
    r = _run(nc, [{"in_" + n: v for n, v in arrays.items()}], core_ids=[0])
    return r.results[0]["out_0"]
```
